# Optimizing a Trainium2 kernel written in Bass

```python
import numpy as np
import jax
import jax.numpy as jnp

def _softmax(x, axis=-1):
    return jax.nn.softmax(x, axis=axis)

def _gelu(x):
    return jax.nn.gelu(x, approximate=True)

def _silu(x):
    return jax.nn.silu(x)

def _sigmoid(x):
    return jax.nn.sigmoid(x)

def _layernorm(x, axis=-1, eps=1e-05):
    m = jnp.mean(x, axis=axis, keepdims=True)
    v = jnp.var(x, axis=axis, keepdims=True)
    return (x - m) / jnp.sqrt(v + eps)

def _scatter_add(tgt, idx, src, axis=0):
    return tgt.at[idx].add(src)

def _segment_sum(src, seg, n):
    return jax.ops.segment_sum(src, seg, n)
kernel_name = 'mk_decoder_postln_d1_seqx_r4_e58c83'

def setup_inputs(seed: int=0):
    np.random.seed(seed)
    _w = jnp.asarray

    def _rec_inputs():
        import jax
        import jax.numpy as jnp
        _rk = jax.random.key(seed)
        x = -0.000125 + 0.9999 * jax.random.normal(jax.random.fold_in(_rk, 1), (4, 512, 512), jnp.float32)
        _lenS = 512 - jax.random.randint(jax.random.fold_in(_rk, 7), (4,), 0, max(1, 512 // 4) + 1, jnp.int32)
        _lenS2 = 1601 - jax.random.randint(jax.random.fold_in(_rk, 8), (4,), 0, max(1, 1601 // 4) + 1, jnp.int32)
        _ctx_2048P = jax.random.normal(jax.random.fold_in(_rk, 11), (4, 16, 512), jnp.float32)
        _ctx_2048c = jax.random.dirichlet(jax.random.fold_in(_rk, 511), 0.3 * jnp.ones((16,), jnp.float32), (4, 1601))
        _ctx_2048t = jnp.einsum('bsk,bkd->bsd', _ctx_2048c, _ctx_2048P)
        _ctx_2048t = _ctx_2048t * jax.lax.rsqrt(jnp.mean(jnp.square(_ctx_2048t)) + 1e-12) * 0.953939
        ctx_2048 = -0.000514642 + 1.00011 * (_ctx_2048t + 0.3 * jax.random.normal(jax.random.fold_in(_rk, 611), (4, 1601, 512), jnp.float32))
        _validS = jnp.arange(512)[None, :] < _lenS[:, None]
        _validS2 = jnp.arange(1601)[None, :] < _lenS2[:, None]
        _causal = jnp.tril(jnp.ones((512, 512), dtype=bool))
        mask_BxS2_bk0 = jnp.logical_not(jnp.broadcast_to(_validS2[:, :], (4, 1601)))
        return (x, ctx_2048, mask_BxS2_bk0)
    x, ctx_2048, mask_BxS2_bk0 = _rec_inputs()

    def _L0_attn_setup():
        import jax, jax.numpy as jnp
        import numpy as np
        import math
        N_HEADS = 16

        def _rope_cache(seq_len, head_dim, dtype):
            half = head_dim // 2
            inv_freq = 1.0 / 10000.0 ** (jnp.arange(half, dtype=jnp.float32) / half)
            t = jnp.arange(seq_len, dtype=jnp.float32)
            freqs = jnp.einsum('t,f->tf', t, inv_freq)
            cos = jnp.repeat(jnp.cos(freqs), 2, axis=-1).astype(dtype)
            sin = jnp.repeat(jnp.sin(freqs), 2, axis=-1).astype(dtype)
            return (cos, sin)

        def _rotate_half(x):
            x1 = x[..., ::2]
            x2 = x[..., 1::2]
            return jnp.stack((-x2, x1), axis=-1).reshape(x.shape)
        key = jax.random.key(seed)
        ks = jax.random.split(key, 5)
        B, T, D = (2, 512, 512)
        s = 1.0 / math.sqrt(D)
        return {'x': jax.random.normal(ks[0], (B, T, D), dtype=jnp.float32), 'Wq': jax.random.normal(ks[1], (D, D), dtype=jnp.float32) * s, 'Wk': jax.random.normal(ks[2], (D, D), dtype=jnp.float32) * s, 'Wv': jax.random.normal(ks[3], (D, D), dtype=jnp.float32) * s, 'Wo': jax.random.normal(ks[4], (D, D), dtype=jnp.float32) * s}
    _L0_attn_all = _L0_attn_setup()
    _L0_attn_in = {k: v for k, v in _L0_attn_all.items() if k in ('Wq', 'Wk', 'Wv', 'Wo')}
    del _L0_attn_all

    def _L0_xattn_setup():
        import jax, jax.numpy as jnp
        import numpy as np
        key = jax.random.key(seed)
        k1, k2, k3 = jax.random.split(key, 3)
        B, S, D, M = (8, 512, 512, 128)
        hidden_states = jax.random.normal(k1, (B, S, D), dtype=jnp.float32)
        memory_tokens = jax.random.normal(k2, (B, M, D), dtype=jnp.float32)
        memory_mask = jax.random.randint(k3, (B, M), 0, 2).astype(jnp.bool_)
        return {'hidden_states': hidden_states, 'memory_tokens': memory_tokens, 'memory_mask': memory_mask}
    _L0_xattn_all = _L0_xattn_setup()
    _L0_xattn_in = {k: v for k, v in _L0_xattn_all.items() if k in ()}
    del _L0_xattn_all

    def _L0_ffn_setup():
        import jax, jax.numpy as jnp
        import numpy as np
        from jax import lax
        TOP_K = 4
        ROUTED_SCALING = 1.0
        RENORMALIZE = True

        def _swiglu_ffn(x, wg, wu, wd):
            return jax.nn.silu(x @ wg.T) * (x @ wu.T) @ wd.T
        key = jax.random.key(seed)
        ks = jax.random.split(key, 9)
        H, I, E = (512, 256, 16)
        s = 0.02
        return {'hidden_states': jax.random.normal(ks[0], (2, 256, H), jnp.float32), 'gate_w': jax.random.normal(ks[1], (E, H), jnp.float32) * s, 'expert_bias': jax.random.normal(ks[2], (E,), jnp.float32) * s, 'w_gate': jax.random.normal(ks[3], (E, I, H), jnp.float32) * s, 'w_up': jax.random.normal(ks[4], (E, I, H), jnp.float32) * s, 'w_down': jax.random.normal(ks[5], (E, H, I), jnp.float32) * s, 'sw_gate': jax.random.normal(ks[6], (I, H), jnp.float32) * s, 'sw_up': jax.random.normal(ks[7], (I, H), jnp.float32) * s, 'sw_down': jax.random.normal(ks[8], (H, I), jnp.float32) * s}
    _L0_ffn_all = _L0_ffn_setup()
    _L0_ffn_in = {k: v for k, v in _L0_ffn_all.items() if k in ('gate_w', 'expert_bias', 'w_gate', 'w_up', 'w_down', 'sw_gate', 'sw_up', 'sw_down')}
    del _L0_ffn_all
    return {'x': x, 'ctx_2048': ctx_2048, 'mask_BxS2_bk0': mask_BxS2_bk0, 'L0_attn_Wq': _L0_attn_in['Wq'], 'L0_attn_Wk': _L0_attn_in['Wk'], 'L0_attn_Wv': _L0_attn_in['Wv'], 'L0_attn_Wo': _L0_attn_in['Wo'], 'L0_ffn_gate_w': _L0_ffn_in['gate_w'], 'L0_ffn_expert_bias': _L0_ffn_in['expert_bias'], 'L0_ffn_w_gate': _L0_ffn_in['w_gate'], 'L0_ffn_w_up': _L0_ffn_in['w_up'], 'L0_ffn_w_down': _L0_ffn_in['w_down'], 'L0_ffn_sw_gate': _L0_ffn_in['sw_gate'], 'L0_ffn_sw_up': _L0_ffn_in['sw_up'], 'L0_ffn_sw_down': _L0_ffn_in['sw_down']}

def reference(x, ctx_2048, mask_BxS2_bk0, L0_attn_Wq, L0_attn_Wk, L0_attn_Wv, L0_attn_Wo, L0_ffn_gate_w, L0_ffn_expert_bias, L0_ffn_w_gate, L0_ffn_w_up, L0_ffn_w_down, L0_ffn_sw_gate, L0_ffn_sw_up, L0_ffn_sw_down):
    import jax
    import jax.numpy as jnp

    def _L0_attn_ref(x, Wq, Wk, Wv, Wo):
        import jax, jax.numpy as jnp
        import numpy as np
        import math
        N_HEADS = 16

        def _rope_cache(seq_len, head_dim, dtype):
            half = head_dim // 2
            inv_freq = 1.0 / 10000.0 ** (jnp.arange(half, dtype=jnp.float32) / half)
            t = jnp.arange(seq_len, dtype=jnp.float32)
            freqs = jnp.einsum('t,f->tf', t, inv_freq)
            cos = jnp.repeat(jnp.cos(freqs), 2, axis=-1).astype(dtype)
            sin = jnp.repeat(jnp.sin(freqs), 2, axis=-1).astype(dtype)
            return (cos, sin)

        def _rotate_half(x):
            x1 = x[..., ::2]
            x2 = x[..., 1::2]
            return jnp.stack((-x2, x1), axis=-1).reshape(x.shape)
        B, T, D = x.shape
        H = N_HEADS
        hd = D // H

        def proj(W):
            return (x @ W.T).reshape(B, T, H, hd).transpose(0, 2, 1, 3)
        q, k, v = (proj(Wq), proj(Wk), proj(Wv))
        cos, sin = _rope_cache(T, hd, x.dtype)
        q = q * cos + _rotate_half(q) * sin
        k = k * cos + _rotate_half(k) * sin
        att = jnp.einsum('bhqd,bhkd->bhqk', q, k) / math.sqrt(hd)
        mask = jnp.triu(jnp.full((T, T), -jnp.inf, dtype=att.dtype), k=1)
        att = jax.nn.softmax(att + mask, axis=-1)
        out = jnp.einsum('bhqk,bhkd->bhqd', att, v)
        out = out.transpose(0, 2, 1, 3).reshape(B, T, D)
        return out @ Wo.T

    def _L0_xattn_ref(hidden_states, memory_tokens, memory_mask):
        import jax, jax.numpy as jnp
        import numpy as np
        B, S, D = hidden_states.shape
        scale = 1.0 / jnp.sqrt(jnp.asarray(D, hidden_states.dtype))
        scores = jnp.einsum('bsd,bmd->bsm', hidden_states, memory_tokens) * scale
        neg_inf = jnp.asarray(-1e+30, scores.dtype)
        scores = jnp.where(memory_mask[:, None, :], scores, neg_inf)
        attn = jax.nn.softmax(scores, axis=-1)
        readout = jnp.einsum('bsm,bmd->bsd', attn, memory_tokens)
        valid_b = jnp.any(memory_mask, axis=-1)
        out = jnp.where(valid_b[:, None, None], readout, jnp.zeros_like(readout))
        return out

    def _L0_ffn_ref(hidden_states, gate_w, expert_bias, w_gate, w_up, w_down, sw_gate, sw_up, sw_down):
        import jax, jax.numpy as jnp
        import numpy as np
        from jax import lax
        TOP_K = 4
        ROUTED_SCALING = 1.0
        RENORMALIZE = True

        def _swiglu_ffn(x, wg, wu, wd):
            return jax.nn.silu(x @ wg.T) * (x @ wu.T) @ wd.T
        orig_shape = hidden_states.shape
        H = orig_shape[-1]
        x = hidden_states.reshape(-1, H)
        T = x.shape[0]
        logits = x.astype(jnp.float32) @ gate_w.T
        scores = jax.nn.sigmoid(logits)
        _, topk_idx = lax.top_k(scores + expert_bias[None, :], TOP_K)
        topk_w = jnp.take_along_axis(scores, topk_idx, axis=-1)
        if RENORMALIZE:
            topk_w = topk_w / jnp.sum(topk_w, axis=-1, keepdims=True)
        topk_w = topk_w * ROUTED_SCALING
        E = gate_w.shape[0]
        combine = jnp.zeros((T, E), dtype=x.dtype).at[jnp.arange(T)[:, None], topk_idx].set(topk_w.astype(x.dtype))

        def step(acc, ws):
            wg, wu, wd, cw = ws
            return (acc + cw[:, None] * _swiglu_ffn(x, wg, wu, wd), None)
        routed, _ = lax.scan(step, jnp.zeros_like(x), (w_gate, w_up, w_down, combine.T))
        shared = _swiglu_ffn(x, sw_gate, sw_up, sw_down)
        return (routed + shared).reshape(orig_shape)
    x = _layernorm(x + _L0_attn_ref(x, L0_attn_Wq, L0_attn_Wk, L0_attn_Wv, L0_attn_Wo), axis=-1)
    x = _layernorm(x + _L0_xattn_ref(x, ctx_2048, mask_BxS2_bk0), axis=-1)
    x = _layernorm(x + _L0_ffn_ref(x, L0_ffn_gate_w, L0_ffn_expert_bias, L0_ffn_w_gate, L0_ffn_w_up, L0_ffn_w_down, L0_ffn_sw_gate, L0_ffn_sw_up, L0_ffn_sw_down), axis=-1)
    return x

_drawn_inputs = setup_inputs


def setup_inputs(seed=0):
    import zlib

    import numpy as np

    out = dict(_drawn_inputs(seed))
    spreads = {}
    factors = {'L0_ffn_gate_w': 3.793,
     'L0_ffn_expert_bias': 8.0,
     'L0_ffn_w_gate': 3.316,
     'L0_ffn_w_up': 3.239,
     'L0_ffn_w_down': 3.248}
    for name, (base, spread) in spreads.items():
        noise = np.random.default_rng([zlib.crc32(name.encode()), seed]).standard_normal(out[name].shape)
        drawn = base * np.exp(spread * noise) if base else spread * noise
        out[name] = jnp.asarray(drawn.astype(out[name].dtype))
    for name, factor in factors.items():
        out[name] = (out[name] * factor).astype(out[name].dtype)
    return out
```

```python
from contextlib import ExitStack

import numpy as np

import concourse.bass as bass
from concourse import mybir

F32 = mybir.dt.float32
F32R = mybir.dt.float32r
BF16 = mybir.dt.bfloat16
U8 = mybir.dt.uint8
U32 = mybir.dt.uint32
ALU = mybir.AluOpType
ACT = mybir.ActivationFunctionType
AX = mybir.AxisListType.X

P = 128
B, T, D = 4, 512, 512
NH, HD = 16, 32
M = 1601
E, I, TOPK = 16, 256, 4
EPS = 1e-5
MASKED = -1e30

TT = T // P
NT = B * TT
DC = D // P
IC = I // P
HG = NH * HD // P
GH = NH // HG
QK = 2 * GH * HD
GW = QK + GH * HD
MQ = 402
MP = 4 * MQ
MC = -(-M // P)
ML = MP - (MC - 1) * P
MR = M - (MC - 1) * P
WE = 2 * DC * I + IC * D
PASSES = ((0, 0), (0, 1), (1, 0))


def self_attention(nc, sem, rows, xT, x, wqkvT, woT, rope):
    with ExitStack() as ctx:
        def sb(name, shape, dt=F32):
            return ctx.enter_context(nc.sbuf_tensor(name, shape, dt))

        x_raw = sb("x_raw", [P, DC, T])
        x_sp = sb("x_sp", [P, 2, DC, T], F32R)
        wqkv = sb("wqkv", [P, 2, DC, HG * GW], F32R)
        wo = sb("wo", [P, 2, HG, D], F32R)
        cos_t = sb("cos_t", [P, TT, GW - QK])
        sin_t = sb("sin_t", [P, TT, GW - QK])
        qk_cos = sb("qk_cos", [P, 2, TT, GH * HD])
        qk_sin = sb("qk_sin", [P, 2, TT, GH * HD])
        qk_sp = sb("qk_sp", [P, 2, TT, GH, 3, HD], F32R)
        v = sb("v", [P, 2, TT, GH * HD])
        q_st = sb("q_st", [P, GH, T], F32R)
        k_st = sb("k_st", [P, GH, T], F32R)
        p_t = sb("p_t", [P, GH, TT * (TT + 1) // 2 * P])
        row_max = sb("row_max", [P, TT, GH])
        neg_max = sb("neg_max", [P, TT, GH, 32], F32R)
        o_f = sb("o_f", [P, T])
        o_sp = sb("o_sp", [P, 2, HG, T], F32R)
        ident_f = sb("ident_f", [P, P])
        ident_r = sb("ident_r", [P, P], F32R)
        ident_b = sb("ident_b", [P, P], BF16)
        mask_qk = sb("mask_qk", [P, P], BF16)
        mask_kq = sb("mask_kq", [P, P], BF16)
        ones = sb("ones", [P, HD])

        proj_ps = ctx.enter_context(nc.psum_tensor("proj_ps", [P, 4, 512], F32))
        score_ps = ctx.enter_context(nc.psum_tensor("score_ps", [P, 2, 512], F32))
        o_ps = ctx.enter_context(nc.psum_tensor("o_ps", [P, 512], F32))
        den_ps = ctx.enter_context(nc.psum_tensor("den_ps", [P, 512], F32))

        tables_in, x_in, rows_in = sem("tables_in"), sem("x_in"), sem("rows_in")
        w_in = sem("w_in")
        const_pool, const_ready = sem("const_pool"), sem("const_ready")
        w_hi, w_lo = sem("w_hi"), sem("w_lo")
        x_hi, x_lo = sem("x_hi"), sem("x_lo")
        projected, roped = sem("projected"), sem("roped")
        v_copied, qk_hi, qk_lo = sem("v_copied"), sem("qk_hi"), sem("qk_lo")
        turned, q_stacked, k_stacked = sem("turned"), sem("q_stacked"), sem("k_stacked")
        scored, maxed, max_hi, max_lo = sem("scored"), sem("maxed"), sem("max_hi"), sem("max_lo")
        max_turned = sem("max_turned")
        max_stacked_a, max_stacked_v = sem("max_stacked_a"), sem("max_stacked_v")
        scored_t, exped, summed = sem("scored_t"), sem("exped"), sem("summed")
        den_inv, o_scaled, o_hi, o_lo = sem("den_inv"), sem("o_scaled"), sem("o_hi"), sem("o_lo")
        out_proj, res_added = sem("out_proj"), sem("res_added")

        NG = B * HG
        assert HG == TT
        p_at = [sum(TT - j for j in range(kc)) * P for kc in range(TT)]
        W_LOADS = DC + 1
        w_view = x_raw[:, :, :].rearrange("p c t -> p (c t)")

        def groups(body, finish):
            def run(eng):
                for hg in range(HG):
                    body(0, hg, hg == 0, False)
                with eng.Fori(1, B - 1) as b:
                    for hg in range(HG):
                        body(b, hg, False, False)
                for hg in range(HG):
                    body(B - 1, hg, False, hg == HG - 1)
                finish()
            return run

        with nc.Block() as block:

            @block.sync
            def _(sp):
                sp.dma_start(cos_t[:, :, :], rope[0]).then_inc(tables_in, 16)
                sp.dma_start(sin_t[:, :, :], rope[1]).then_inc(tables_in, 16)
                for n in range(W_LOADS):
                    if n >= 1:
                        sp.wait_ge(w_lo, n)
                    if n < DC:
                        sp.dma_start(w_view[:, 0:HG * GW], wqkvT[:, n, :]).then_inc(w_in, 16)
                    else:
                        sp.dma_start(w_view[:, 0:HG * D], woT).then_inc(w_in, 16)
                sp.wait_ge(w_lo, W_LOADS)
                sp.dma_start(x_raw[:, :, :], xT[0]).then_inc(x_in, 16)
                sp.dma_start(rows[:, :, :], x).then_inc(rows_in, 16)
                with sp.Fori(1, B) as b:
                    sp.wait_ge(x_lo, b)
                    sp.dma_start(x_raw[:, :, :], xT[b]).then_inc(x_in, 16)

            @block.gpsimd
            def _(pool):
                nc.gpsimd.memset(ident_f[:, :], 1.0).then_inc(const_pool, 1)
                nc.gpsimd.memset(ident_b[:, :], 1.0).then_inc(const_pool, 1)
                nc.gpsimd.memset(mask_qk[:, :], 0.0).then_inc(const_pool, 1)
                nc.gpsimd.memset(mask_kq[:, :], 0.0).then_inc(const_pool, 1)
                nc.gpsimd.memset(ones[:, :], 1.0).then_inc(const_pool, 1)
                pool.wait_ge(const_pool, 5)
                for m in (ident_f, ident_b):
                    nc.gpsimd.affine_select(out=m[:, :], in_=m[:, :], compare_op=ALU.is_equal, fill=0.0,
                                            base=0, pattern=[[-1, P]], channel_multiplier=1).then_inc(const_pool, 1)
                nc.gpsimd.affine_select(out=mask_qk[:, :], in_=mask_qk[:, :], compare_op=ALU.is_ge, fill=MASKED,
                                        base=0, pattern=[[-1, P]], channel_multiplier=1).then_inc(const_pool, 1)
                nc.gpsimd.affine_select(out=mask_kq[:, :], in_=mask_kq[:, :], compare_op=ALU.is_ge, fill=MASKED,
                                        base=0, pattern=[[1, P]], channel_multiplier=-1).then_inc(const_pool, 1)

                def lo_x(b):
                    pool.wait_ge(x_hi, b + 1)
                    nc.gpsimd.tensor_tensor(x_sp[:, 1, :, :], x_raw[:, :, :], x_sp[:, 0, :, :].bitcast(F32),
                                            ALU.subtract).then_inc(x_lo, 1)

                def lo_qk(g):
                    for s in range(2):
                        pool.wait_ge(qk_hi, g * 2 + s + 1)
                        block = qk_sp[:, s, :, :, :, :].rearrange("p t h n d -> p (t h) n d")
                        nc.gpsimd.tensor_tensor(block[:, :, 2 - s, :],
                                                qk_cos[:, s, :, :].rearrange("p t (h d) -> p (t h) d", d=HD),
                                                block[:, :, 0, :].bitcast(F32), ALU.subtract).then_inc(qk_lo, 1)

                def lo_out(g, hg):
                    pool.wait_ge(o_hi, g + 1)
                    nc.gpsimd.tensor_tensor(o_sp[:, 1, hg, :], o_f[:, :], o_sp[:, 0, hg, :].bitcast(F32),
                                            ALU.subtract).then_inc(o_lo, 1)

                def group(b, hg, first, last):
                    g = b * HG + hg
                    if not first:
                        lo_out(g - 1, (hg - 1) % HG)
                    if not last:
                        lo_qk(g + 1)
                    if hg == HG - 2 and not (isinstance(b, int) and b == B - 1):
                        lo_x(b + 1)

                lo_x(0)
                lo_qk(0)
                groups(group, lambda: lo_out(NG - 1, HG - 1))(pool)

            @block.scalar
            def _(act):
                for n in range(W_LOADS):
                    act.wait_ge(w_in, 16 * (n + 1))
                    if n < DC:
                        nc.scalar.activation(wqkv[:, 0, n, :], w_view[:, 0:HG * GW], ACT.Copy).then_inc(w_hi, 1)
                    else:
                        nc.scalar.activation(wo[:, 0, :, :].rearrange("p g n -> p (g n)"), w_view[:, 0:HG * D],
                                             ACT.Copy).then_inc(w_hi, 1)

                def split_x(b):
                    act.wait_ge(x_in, b * 16 + 16)
                    act.wait_ge(projected, b * (HG * TT))
                    nc.scalar.activation(x_sp[:, 0, :, :], x_raw[:, :, :], ACT.Copy).then_inc(x_hi, 1)

                def keep_v(g, par):
                    act.wait_ge(projected, g * TT + TT)
                    if not isinstance(g, int) or g >= 2:
                        act.wait_ge(summed, g - 1)
                    nc.scalar.activation(v[:, par, :, :], proj_ps[:, :, QK:GW], ACT.Copy).then_inc(v_copied, 1)

                def hi_qk(g):
                    act.wait_ge(roped, g * 5 + 5)
                    act.wait_ge(turned, g * 2 * GH)
                    for s in range(2):
                        blocks = slice(0, 2) if s == 0 else slice(0, 3, 2)
                        nc.scalar.activation(qk_sp[:, s, :, :, blocks, :].rearrange("p t h two d -> p (t h) two d"),
                                             qk_cos[:, s, :, :].rearrange("p t (h d) -> p (t h) d", d=HD)
                                             .unsqueeze(2).broadcast_to([P, TT * GH, 2, HD]),
                                             ACT.Copy).then_inc(qk_hi, 1)

                def hi_out(g, hg):
                    act.wait_ge(o_scaled, g + 1)
                    if hg == 0:
                        act.wait_ge(out_proj, g)
                    nc.scalar.activation(o_sp[:, 0, hg, :], o_f[:, :], ACT.Copy).then_inc(o_hi, 1)

                def group(b, hg, first, last):
                    g = b * HG + hg
                    act.wait_ge(scored_t, g * GH * TT)
                    for h in range(GH):
                        act.wait_ge(turned, g * 2 * GH + 2 * h + 1)
                        nc.scalar.activation(q_st[0:3 * HD, h, :], proj_ps[0:3 * HD, 2 * h % 4, :],
                                             ACT.Copy).then_inc(q_stacked, 1)
                    if not first:
                        hi_out(g - 1, (hg - 1) % HG)
                    act.wait_ge(max_turned, g + 1)
                    for h in range(0, GH, 2):
                        nc.scalar.activation(q_st[3 * HD:P, h, :], den_ps[32 * h:32 * h + 32, :],
                                             ACT.Copy).then_inc(max_stacked_a, 1)
                    act.wait_ge(summed, g)
                    for kc in range(TT):
                        w = T - kc * P
                        for h in range(GH):
                            n = kc * GH + h
                            act.wait_ge(scored_t, g * GH * TT + n + 1)
                            nc.scalar.activation(p_t[:, h, p_at[kc]:p_at[kc] + w],
                                                 score_ps[:, n % 2, kc * P:T], ACT.Exp,
                                                 scale=float(HD) ** -0.5).then_inc(exped, 1)
                        if kc == 0 and not last:
                            keep_v(g + 1, (hg + 1) % 2)
                        if kc == 2 and not last:
                            hi_qk(g + 1)
                    if hg == HG - 2 and not (isinstance(b, int) and b == B - 1):
                        split_x(b + 1)

                split_x(0)
                keep_v(0, 0)
                hi_qk(0)
                groups(group, lambda: hi_out(NG - 1, HG - 1))(act)

            @block.vector
            def _(dve):
                dve.wait_ge(const_pool, 9)
                nc.vector.tensor_copy(ident_r[:, :], ident_f[:, :]).then_inc(const_ready, 1)
                nc.vector.memset(neg_max[:, :, :, :].bitcast(F32), 0.0).then_inc(const_ready, 1)
                nc.vector.memset(k_st[3 * HD:P, :, :].bitcast(F32), 1.0).then_inc(const_ready, 1)
                for n in range(W_LOADS):
                    dve.wait_ge(w_hi, n + 1)
                    if n < DC:
                        nc.vector.tensor_tensor(wqkv[:, 1, n, :], w_view[:, 0:HG * GW],
                                                wqkv[:, 0, n, :].bitcast(F32), ALU.subtract).then_inc(w_lo, 1)
                    else:
                        nc.vector.tensor_tensor(wo[:, 1, :, :].rearrange("p g n -> p (g n)"), w_view[:, 0:HG * D],
                                                wo[:, 0, :, :].rearrange("p g n -> p (g n)").bitcast(F32),
                                                ALU.subtract).then_inc(w_lo, 1)

                def rotate(g):
                    dve.wait_ge(projected, g * TT + TT)
                    dve.wait_ge(v_copied, g + 1)
                    dve.wait_ge(qk_lo, g * 2)
                    for s in range(2):
                        part = slice(s * QK // 2, (s + 1) * QK // 2)
                        nc.vector.tensor_tensor(qk_cos[:, s, :, :], proj_ps[:, :, part], cos_t[:, :, :],
                                                ALU.mult).then_inc(roped, 1)
                        swapped = proj_ps[:, :, part].rearrange("p t (n two) -> p t n two", two=2)[:, :, :, ::-1]
                        nc.vector.tensor_tensor(qk_sin[:, s, :, :].rearrange("p t (n two) -> p t n two", two=2),
                                                swapped, sin_t[:, :, :].rearrange("p t (n two) -> p t n two", two=2),
                                                ALU.mult).then_inc(roped, 1)
                    dve.wait_ge(roped, g * 5 + 4)
                    nc.vector.tensor_tensor(qk_cos[:, :, :, :], qk_cos[:, :, :, :], qk_sin[:, :, :, :],
                                            ALU.add).then_inc(roped, 1)

                def finish_out(g):
                    dve.wait_ge(summed, g + 1)
                    dve.wait_ge(o_lo, g)
                    nc.vector.reciprocal(o_f[:, :], den_ps[:, :]).then_inc(den_inv, 1)
                    dve.wait_ge(den_inv, g + 1)
                    nc.vector.tensor_tensor(o_f[:, :], o_ps[:, :], o_f[:, :], ALU.mult).then_inc(o_scaled, 1)

                def add_residual(b):
                    for tt in range(TT):
                        dve.wait_ge(out_proj, b * TT + tt + 1)
                        row = rows[:, b * TT + tt, :]
                        nc.vector.tensor_tensor(row, score_ps[:, tt % 2, :], row, ALU.add).then_inc(res_added, 1)

                def group(b, hg, first, last):
                    g = b * HG + hg
                    dve.wait_ge(scored_t, g * GH * TT)
                    for h in range(GH):
                        dve.wait_ge(turned, g * 2 * GH + 2 * h + 2)
                        nc.vector.tensor_copy(k_st[0:3 * HD, h, :], proj_ps[0:3 * HD, (2 * h + 1) % 4, :]
                                              ).then_inc(k_stacked, 1)
                    if not first:
                        finish_out(g - 1)
                        if hg == 0:
                            add_residual(b - 1)
                    for qt in range(TT):
                        for h in range(GH):
                            n = qt * GH + h
                            dve.wait_ge(scored, g * GH * TT + n + 1)
                            if n == 0:
                                dve.wait_ge(max_lo, g)
                            nc.vector.tensor_reduce(row_max[:, qt, h:h + 1], score_ps[:, n % 2, 0:(qt + 1) * P],
                                                    AX, ALU.max).then_inc(maxed, 1)
                    dve.wait_ge(maxed, g * GH * TT + GH * TT)
                    dve.wait_ge(max_turned, g)
                    nc.vector.tensor_scalar(neg_max[:, :, :, 0], row_max[:, :, :], -1.0, None,
                                            ALU.mult).then_inc(max_hi, 1)
                    dve.wait_ge(max_hi, g + 1)
                    nc.vector.scalar_tensor_tensor(neg_max[:, :, :, 1], row_max[:, :, :], -1.0,
                                                   neg_max[:, :, :, 0].bitcast(F32), ALU.mult, ALU.subtract
                                                   ).then_inc(max_lo, 1)
                    dve.wait_ge(max_turned, g + 1)
                    for h in range(1, GH, 2):
                        nc.vector.tensor_copy(q_st[3 * HD:P, h, :], den_ps[32 * h:32 * h + 32, :]
                                              ).then_inc(max_stacked_v, 1)
                    if not last:
                        rotate(g + 1)

                def finish():
                    finish_out(NG - 1)
                    add_residual(B - 1)

                dve.wait_ge(tables_in, 32)
                rotate(0)
                dve.wait_ge(rows_in, 16)
                groups(group, finish)(dve)

            @block.tensor
            def _(pe):
                products = [(tt, c, n) for tt in range(TT) for c in range(DC) for n in range(3)]

                def project(g, hg, start, stop):
                    for tt, c, n in products[start:stop]:
                        xs, ws = PASSES[n]
                        mm = nc.tensor.matmul(proj_ps[:, tt, 0:GW], x_sp[:, xs, c, tt * P:(tt + 1) * P],
                                              wqkv[:, ws, c, hg * GW:(hg + 1) * GW],
                                              start=(c == 0 and n == 0), stop=(c == DC - 1 and n == 2))
                        if c == DC - 1 and n == 2:
                            mm.then_inc(projected, 1)

                def project_out(b):
                    pe.wait_ge(o_lo, b * HG + HG)
                    pe.wait_ge(exped, (b + 1) * (HG * GH * TT))
                    for tt in range(TT):
                        if tt >= 2:
                            pe.wait_ge(res_added, b * TT + tt - 1)
                        for c in range(HG):
                            for n, (os, ws) in enumerate(PASSES):
                                mm = nc.tensor.matmul(score_ps[:, tt % 2, :], o_sp[:, os, c, tt * P:(tt + 1) * P],
                                                      wo[:, ws, c, :], start=(c == 0 and n == 0),
                                                      stop=(c == HG - 1 and n == 2))
                        mm.then_inc(out_proj, 1)

                def scores(g, qt, half):
                    w = (qt + 1) * P
                    for h in range(2 * half, 2 * half + 2):
                        n = qt * GH + h
                        if qt == 0:
                            pe.wait_ge(q_stacked, g * GH + h + 1)
                            pe.wait_ge(k_stacked, g * GH + h + 1)
                        if n >= 2:
                            pe.wait_ge(maxed, g * GH * TT + n - 1)
                        else:
                            pe.wait_ge(exped, g * GH * TT)
                        wide = max(w, 2 * P)
                        nc.tensor.matmul(score_ps[:, n % 2, 0:wide], q_st[0:3 * HD, h, qt * P:w],
                                         k_st[0:3 * HD, h, 0:wide], start=True, stop=False)
                        nc.tensor.matmul(score_ps[:, n % 2, w - P:w], ident_b[:, :], mask_qk[:, :],
                                         start=False, stop=True).then_inc(scored, 1)

                def scores_t(g, kc, half):
                    q0 = min(kc * P, T - 2 * P)
                    for h in range(2 * half, 2 * half + 2):
                        n = kc * GH + h
                        if kc == 0 and h % 2 == 0:
                            pe.wait_ge(max_stacked_a, g * (GH // 2) + h // 2 + 1)
                        if kc == 0 and h % 2 == 1:
                            pe.wait_ge(max_stacked_v, g * (GH // 2) + h // 2 + 1)
                        if n >= 2:
                            pe.wait_ge(exped, g * GH * TT + n - 1)
                        nc.tensor.matmul(score_ps[:, n % 2, q0:T], k_st[:, h, kc * P:(kc + 1) * P],
                                         q_st[:, h, q0:T], start=True, stop=False)
                        nc.tensor.matmul(score_ps[:, n % 2, kc * P:(kc + 1) * P], ident_b[:, :],
                                         mask_kq[:, :], start=False, stop=True).then_inc(scored_t, 1)

                def values(g, hg, kc):
                    pe.wait_ge(exped, g * GH * TT + (kc + 1) * GH)
                    for h in range(GH):
                        nc.tensor.matmul(o_ps[h * HD:(h + 1) * HD, kc * P:T], v[:, hg % 2, kc, h * HD:(h + 1) * HD],
                                         p_t[:, h, p_at[kc]:p_at[kc] + T - kc * P],
                                         start=(kc == 0), stop=(kc == TT - 1))

                def weight_sums(g, kc):
                    for h in range(GH):
                        mm = nc.tensor.matmul(den_ps[h * HD:(h + 1) * HD, kc * P:T], ones[:, :],
                                              p_t[:, h, p_at[kc]:p_at[kc] + T - kc * P],
                                              start=(kc == 0), stop=(kc == TT - 1))
                    return mm

                def group(b, hg, first, last):
                    g = b * HG + hg
                    pe.wait_ge(qk_lo, g * 2 + 2)
                    pe.wait_ge(v_copied, g + 1)
                    for n in range(2 * GH):
                        h, s = n // 2, n % 2
                        if n >= 4:
                            pe.wait_ge(k_stacked if s else q_stacked, g * GH + h - 1)
                        for tt in range(TT):
                            mm = nc.tensor.transpose(proj_ps[0:3 * HD, n % 4, tt * P:(tt + 1) * P].bitcast(F32R),
                                                     qk_sp[:, s, tt, h, :, :].rearrange("p n d -> p (n d)"),
                                                     ident_r[:, :])
                        mm.then_inc(turned, 1)
                    if hg == 0 and not first:
                        project_out(b - 1)
                        pe.wait_ge(res_added, b * TT)
                    if hg == HG - 1 and not last:
                        pe.wait_ge(x_lo, b + 2)
                    STEP = 5
                    for n in range(2 * TT):
                        scores(g, n // 2, n % 2)
                        if n == 1 and not last:
                            pe.wait_ge(q_stacked, g * GH + GH)
                            pe.wait_ge(k_stacked, g * GH + GH)
                        if n >= 1 and not last:
                            project(g + 1, (hg + 1) % HG, (n - 1) * STEP, n * STEP)
                    pe.wait_ge(max_lo, g + 1)
                    pe.wait_ge(o_scaled, g)
                    for qt in range(TT):
                        mm = nc.tensor.transpose(den_ps[:, qt * P:(qt + 1) * P].bitcast(F32R),
                                                 neg_max[:, qt, :, :].rearrange("p h n -> p (h n)"), ident_r[:, :])
                    mm.then_inc(max_turned, 1)
                    at = (2 * TT - 1) * STEP
                    if not last:
                        project(g + 1, (hg + 1) % HG, at, at + 7)
                    pe.wait_ge(maxed, g * GH * TT + GH * TT)
                    scores_t(g, 0, 0)
                    if not last:
                        project(g + 1, (hg + 1) % HG, at + 7, len(products))
                    scores_t(g, 0, 1)
                    for kc in range(1, TT):
                        scores_t(g, kc, 0)
                        values(g, hg, kc - 1)
                        scores_t(g, kc, 1)
                        weight_sums(g, kc - 1)
                    values(g, hg, TT - 1)
                    weight_sums(g, TT - 1).then_inc(summed, 1)

                pe.wait_ge(const_ready, 3)
                pe.wait_ge(w_lo, W_LOADS)
                pe.wait_ge(x_lo, 1)
                project(0, 0, 0, len(products))
                groups(group, lambda: project_out(B - 1))(pe)


def layer_norm_scales(nc, sem, ctx, rows, name):
    stats = ctx.enter_context(nc.sbuf_tensor(name + "_stats", [P, NT, 6], F32))
    mean_var = ctx.enter_context(nc.sbuf_tensor(name + "_mean_var", [P, NT, 2], F32))
    eps = ctx.enter_context(nc.sbuf_tensor(name + "_eps", [P, 1], F32))
    rstd = ctx.enter_context(nc.sbuf_tensor(name + "_rstd", [P, NT], F32))
    half_v = ctx.enter_context(nc.sbuf_tensor(name + "_half_v", [P, NT], F32))
    gathered, aggregated = sem(name + "_gathered"), sem(name + "_aggregated")
    eps_set, rooted, inverted = sem(name + "_eps_set"), sem(name + "_rooted"), sem(name + "_inverted")
    with nc.Block() as block:

        @block.vector
        def _(dve):
            nc.vector.memset(eps[:, :], EPS).then_inc(eps_set, 1)
            for t in range(NT):
                nc.vector.bn_stats(stats[:, t, :], rows[:, t, :]).then_inc(gathered, 1)
            for t in range(NT):
                dve.wait_ge(gathered, t + 1)
                nc.vector.bn_aggr(mean_var[:, t, :], stats[:, t, :]).then_inc(aggregated, 1)
            dve.wait_ge(rooted, 1)
            nc.vector.reciprocal(rstd[:, :], rstd[:, :]).then_inc(inverted, 1)
            nc.vector.tensor_scalar(half_v[:, :], mean_var[:, :, 1], EPS, -0.5, ALU.add, ALU.mult).then_inc(inverted, 1)
            dve.wait_ge(inverted, 2)
            nc.vector.tensor_tensor(half_v[:, :], half_v[:, :], rstd[:, :], ALU.mult).then_inc(inverted, 1)
            dve.wait_ge(inverted, 3)
            nc.vector.tensor_tensor(half_v[:, :], half_v[:, :], rstd[:, :], ALU.mult).then_inc(inverted, 1)
            dve.wait_ge(inverted, 4)
            nc.vector.scalar_tensor_tensor(rstd[:, :], half_v[:, :], 1.5, rstd[:, :], ALU.add, ALU.mult
                                           ).then_inc(inverted, 1)

        @block.scalar
        def _(act):
            act.wait_ge(eps_set, 1)
            act.wait_ge(aggregated, NT)
            nc.scalar.activation(rstd[:, :], mean_var[:, :, 1], ACT.Sqrt, bias=eps[:, 0:1]).then_inc(rooted, 1)
    return mean_var, rstd


def cross_attention(nc, sem, rows, ctxT, ctx_rows, mask):
    with ExitStack() as ctx:
        def sb(name, shape, dt=F32):
            return ctx.enter_context(nc.sbuf_tensor(name, shape, dt))

        mean_var, rstd = layer_norm_scales(nc, sem, ctx, rows, "norm1")
        raw = sb("raw", [P, 2, (MC + 3) // 4 * D])
        ct = sb("ct", [P, 2, DC, MP], F32R)
        cr = sb("cr", [P, 2, MC, D], F32R)
        x1 = sb("x1", [P, TT, D])
        x1_t = sb("x1_t", [P, 2, DC, T], F32R)
        mask_u8 = sb("mask_u8", [1, MP], U8)
        mask_bias = sb("mask_bias", [1, MP], BF16)
        any_kept = sb("any_kept", [1, 1])
        weigh = sb("weigh", [P, MP])
        mask_f = weigh[0:1, :]
        weigh_t = sb("weigh_t", [P, 2, MC, P], F32R)
        stat = sb("stat", [P, 2, 4])
        kept = sb("kept", [P, 1])
        ident = sb("c_ident", [P, P])
        ones_b = sb("c_ones_b", [1, P], BF16)
        ones_f = sb("c_ones_f", [1, P])

        score_ps = ctx.enter_context(nc.psum_tensor("c_score_ps", [P, 4, 512], F32))
        turn_ps = ctx.enter_context(nc.psum_tensor("c_turn_ps", [P, 2, 512], F32))
        out_ps = ctx.enter_context(nc.psum_tensor("c_out_ps", [P, 2, 512], F32))

        raw_in = [sem("c_raw_in0"), sem("c_raw_in1")]
        mask_in = sem("c_mask_in")
        consts, zeroed = sem("c_consts"), sem("c_zeroed")
        raw_hi, raw_lo = sem("c_raw_hi"), sem("c_raw_lo")
        mask_done, kept_ps, kept_done = sem("c_mask_done"), sem("c_kept_ps"), sem("c_kept_done")
        normed, x1_turned, x1_hi, x1_lo = sem("c_normed"), sem("c_x1_turned"), sem("c_x1_hi"), sem("c_x1_lo")
        scored, maxed, exped = sem("c_scored"), sem("c_maxed"), sem("c_exped")
        inverted, w_turned, w_hi, w_lo = sem("c_inverted"), sem("c_w_turned"), sem("c_w_hi"), sem("c_w_lo")
        read_out, written = sem("c_read_out"), sem("c_written")

        SCALE = float(D) ** -0.5
        GR = (MC + 3) // 4
        row_groups = [(c, min(c + GR, MC)) for c in range(0, MC, GR)]
        LOADS = DC + len(row_groups)
        TG = [(c, min(c + 4, MC)) for c in range(0, MC, 4)]
        NG = len(TG)

        def chunk(n):
            if n < DC:
                return [(ctxT, n, raw[:, n % 2, 0:M], ct[:, 0, n, 0:M], ct[:, 1, n, 0:M])]
            c0, c1 = row_groups[n - DC]
            full = c1 if c1 * P <= M else c1 - 1
            parts = []
            if full > c0:
                parts.append(((c0, full), None, raw[:, n % 2, 0:(full - c0) * D],
                              cr[:, 0, c0:full, :].rearrange("p c d -> p (c d)"),
                              cr[:, 1, c0:full, :].rearrange("p c d -> p (c d)")))
            if full < c1:
                parts.append(((full, c1), None, raw[0:MR, n % 2, (full - c0) * D:(c1 - c0) * D],
                              cr[0:MR, 0, full, :], cr[0:MR, 1, full, :]))
            return parts

        parts_before = [0]
        for n in range(LOADS):
            parts_before.append(parts_before[-1] + len(chunk(n)))
        PARTS = parts_before[-1]

        def loaded(b, n):
            mine = [len(chunk(i)) for i in range(n % 2, LOADS, 2)]
            return b * (16 * sum(mine)) + 16 * sum(mine[:n // 2 + 1])

        with nc.Block() as block:

            @block.sync
            def _(sp):
                sp.wait_ge(consts, 5)
                with sp.Fori(0, B) as b:
                    for n in range(LOADS):
                        sp.wait_ge(raw_lo, b * PARTS + (parts_before[n - 1] if n >= 1 else 0))
                        for src, c, dst, _, _ in chunk(n):
                            if c is not None:
                                sp.dma_start(dst, ctxT[b, :, c, :]).then_inc(raw_in[n % 2], 16)
                                if n == 0:
                                    sp.dma_start(mask_u8[:, 0:M], mask[b]).then_inc(mask_in, 16)
                            elif src[1] * P <= M:
                                sp.dma_start(dst.rearrange("p (c d) -> p c d", d=D),
                                             ctx_rows[b, src[0] * P:src[1] * P, :].rearrange("(c p) d -> p c d", p=P)
                                             ).then_inc(raw_in[n % 2], 16)
                            else:
                                sp.dma_start(dst, ctx_rows[b, src[0] * P:M, :]).then_inc(raw_in[n % 2], 16)

            @block.gpsimd
            def _(pool):
                nc.gpsimd.memset(ident[:, :], 1.0).then_inc(consts, 1)
                nc.gpsimd.memset(ones_b[:, :], 1.0).then_inc(consts, 1)
                nc.gpsimd.memset(ones_f[:, :], 1.0).then_inc(consts, 1)
                nc.gpsimd.memset(mask_u8[:, :], 0).then_inc(consts, 1)
                pool.wait_ge(consts, 4)
                nc.gpsimd.affine_select(out=ident[:, :], in_=ident[:, :], compare_op=ALU.is_equal, fill=0.0,
                                        base=0, pattern=[[-1, P]], channel_multiplier=1).then_inc(consts, 1)

            @block.scalar
            def _(act):
                act.wait_ge(zeroed, 4)
                with act.Fori(0, B) as b:
                    act.wait_ge(read_out, b * TT)
                    for n in range(LOADS):
                        act.wait_ge(raw_in[n % 2], loaded(b, n))
                        for _, _, src, hi, _ in chunk(n):
                            nc.scalar.activation(hi, src, ACT.Copy).then_inc(raw_hi, 1)
                    for c in range(DC):
                        act.wait_ge(x1_turned, b * DC + c + 1)
                        nc.scalar.activation(x1_t[:, 0, c, :], turn_ps[:, c % 2, :], ACT.Copy).then_inc(x1_hi, 1)
                    for qt in range(TT):
                        n = b * TT + qt
                        act.wait_ge(maxed, n * 2 + 2)
                        act.wait_ge(w_turned, n * NG)
                        nc.scalar.activation(weigh[:, :].rearrange("p (f m) -> p f m", f=4), score_ps[:, :, 0:MQ],
                                             ACT.Exp, bias=stat[:, qt % 2, 1:2], scale=SCALE,
                                             accum_out=stat[:, qt % 2, 2:3]).then_inc(exped, 1)
                        act.wait_ge(read_out, n)
                        for i, (c0, c1) in enumerate(TG):
                            act.wait_ge(w_turned, n * NG + i + 1)
                            k = P if c1 < MC else ML
                            nc.scalar.activation(weigh_t[0:k, 0, c0:c1, :].rearrange("p c q -> p (c q)"),
                                                 turn_ps[0:k, i % 2, 0:(c1 - c0) * P], ACT.Copy).then_inc(w_hi, 1)

            @block.vector
            def _(dve):
                for part in range(2):
                    nc.vector.memset(ct[:, part, :, M:MP].bitcast(F32), 0.0).then_inc(zeroed, 1)
                    nc.vector.memset(cr[:, part, MC - 1, :].bitcast(F32), 0.0).then_inc(zeroed, 1)
                dve.wait_ge(zeroed, 4)
                with dve.Fori(0, B) as b:
                    dve.wait_ge(mask_in, b * 16 + 16)
                    dve.wait_ge(consts, 5)
                    dve.wait_ge(scored, b * TT)
                    dve.wait_ge(w_turned, b * (TT * NG))
                    nc.vector.tensor_copy(mask_f[:, :], mask_u8[:, :]).then_inc(mask_done, 1)
                    dve.wait_ge(mask_done, b * 3 + 1)
                    nc.vector.tensor_scalar(mask_bias[:, :], mask_f[:, :], 1.0, -MASKED, ALU.subtract,
                                            ALU.mult).then_inc(mask_done, 1)
                    nc.vector.tensor_reduce(any_kept[:, :], mask_f[:, :], AX, ALU.max).then_inc(mask_done, 1)
                    for t in range(TT):
                        row = rows[:, b * TT + t, :]
                        nc.vector.tensor_scalar(x1[:, t, :], row, mean_var[:, bass.ds(b * TT + t, 1), 0],
                                                rstd[:, bass.ds(b * TT + t, 1)], ALU.subtract, ALU.mult
                                                ).then_inc(normed, 1)
                    at = 0
                    for n in range(LOADS):
                        for _, _, src, hi, lo in chunk(n):
                            dve.wait_ge(raw_hi, b * PARTS + at + 1)
                            nc.vector.tensor_tensor(lo, src, hi.bitcast(F32), ALU.subtract).then_inc(raw_lo, 1)
                            at += 1
                    for c in range(DC):
                        dve.wait_ge(x1_hi, b * DC + c + 1)
                        nc.vector.tensor_tensor(x1_t[:, 1, c, :], turn_ps[:, c % 2, :], x1_t[:, 0, c, :].bitcast(F32),
                                                ALU.subtract).then_inc(x1_lo, 1)
                    dve.wait_ge(kept_ps, b + 1)
                    nc.vector.tensor_copy(kept[:, :], out_ps[:, 1, 0:1]).then_inc(kept_done, 1)

                    def maximum(qt):
                        n = b * TT + qt
                        dve.wait_ge(scored, n + 1)
                        nc.vector.tensor_reduce(stat[:, qt % 2, 0:1], score_ps[:, :, 0:MQ],
                                                mybir.AxisListType.XY, ALU.max).then_inc(maxed, 1)
                        dve.wait_ge(maxed, n * 2 + 1)
                        nc.vector.tensor_scalar(stat[:, qt % 2, 1:2], stat[:, qt % 2, 0:1], 0.1 * MASKED, -SCALE,
                                                ALU.max, ALU.mult).then_inc(maxed, 1)

                    maximum(0)
                    for qt in range(TT):
                        n = b * TT + qt
                        dve.wait_ge(exped, n + 1)
                        nc.vector.tensor_scalar(stat[:, qt % 2, 3:4], stat[:, qt % 2, 2:3], 1e-30, None,
                                                ALU.max).then_inc(inverted, 1)
                        dve.wait_ge(inverted, n * 3 + 1)
                        nc.vector.reciprocal(stat[:, qt % 2, 3:4], stat[:, qt % 2, 3:4]).then_inc(inverted, 1)
                        for i, (c0, c1) in enumerate(TG):
                            dve.wait_ge(w_hi, n * NG + i + 1)
                            k = P if c1 < MC else ML
                            nc.vector.tensor_tensor(weigh_t[0:k, 1, c0:c1, :].rearrange("p c q -> p (c q)"),
                                                    turn_ps[0:k, i % 2, 0:(c1 - c0) * P],
                                                    weigh_t[0:k, 0, c0:c1, :].rearrange("p c q -> p (c q)").bitcast(F32),
                                                    ALU.subtract).then_inc(w_lo, 1)
                        dve.wait_ge(inverted, n * 3 + 2)
                        dve.wait_ge(kept_done, b + 1)
                        nc.vector.tensor_tensor(stat[:, qt % 2, 3:4], stat[:, qt % 2, 3:4], kept[:, :],
                                                ALU.mult).then_inc(inverted, 1)
                        if qt < TT - 1:
                            maximum(qt + 1)
                        dve.wait_ge(inverted, n * 3 + 3)
                        dve.wait_ge(read_out, n + 1)
                        nc.vector.scalar_tensor_tensor(rows[:, b * TT + qt, :], out_ps[:, qt % 2, :],
                                                       stat[:, qt % 2, 3:4], x1[:, qt, :], ALU.mult, ALU.add
                                                       ).then_inc(written, 1)

            @block.tensor
            def _(pe):
                pe.wait_ge(consts, 5)
                with pe.Fori(0, B) as b:
                    pe.wait_ge(normed, b * TT + TT)
                    pe.wait_ge(w_lo, b * (TT * NG))
                    for c in range(DC):
                        if c >= 2:
                            pe.wait_ge(x1_lo, b * DC + c - 1)
                        for t in range(TT):
                            mm = nc.tensor.transpose(turn_ps[:, c % 2, t * P:(t + 1) * P],
                                                     x1[:, t, c * P:(c + 1) * P], ident[:, :])
                        mm.then_inc(x1_turned, 1)
                    pe.wait_ge(mask_done, b * 3 + 3)
                    pe.wait_ge(written, b * TT)
                    nc.tensor.matmul(out_ps[:, 1, 0:1], ones_f[:, :], any_kept[:, :], start=True,
                                     stop=True).then_inc(kept_ps, 1)

                    def scores(qt):
                        n = b * TT + qt
                        pe.wait_ge(exped, n)
                        for f in range(4):
                            nc.tensor.matmul(score_ps[:, f, 0:MQ], ones_b[:, :], mask_bias[:, f * MQ:(f + 1) * MQ],
                                             start=True, stop=False)
                        for c in range(DC):
                            if qt == 0:
                                pe.wait_ge(raw_lo, b * PARTS + c + 1)
                            for xs, cs in PASSES:
                                for f in range(4):
                                    mm = nc.tensor.matmul(score_ps[:, f, 0:MQ], x1_t[:, xs, c, qt * P:(qt + 1) * P],
                                                          ct[:, cs, c, f * MQ:(f + 1) * MQ], start=False,
                                                          stop=(c == DC - 1 and (xs, cs) == PASSES[-1]))
                        mm.then_inc(scored, 1)

                    pe.wait_ge(x1_lo, b * DC + DC)
                    scores(0)
                    for qt in range(TT):
                        n = b * TT + qt
                        if qt < TT - 1:
                            scores(qt + 1)
                        pe.wait_ge(exped, n + 1)
                        for i, (c0, c1) in enumerate(TG):
                            if i >= 2:
                                pe.wait_ge(w_lo, n * NG + i - 1)
                            for c in range(c0, c1):
                                k = P if c < MC - 1 else ML
                                mm = nc.tensor.transpose(turn_ps[0:k, i % 2, (c - c0) * P:(c - c0 + 1) * P],
                                                         weigh[:, c * P:c * P + k], ident[:, :])
                            mm.then_inc(w_turned, 1)
                        pe.wait_ge(kept_done, b + 1)
                        if qt >= 2:
                            pe.wait_ge(written, n - 1)
                        for c in range(MC):
                            k = P if c < MC - 1 else ML
                            pe.wait_ge(w_lo, n * NG + c // 4 + 1)
                            if qt == 0:
                                pe.wait_ge(raw_lo, b * PARTS + PARTS)
                            for m, (ws, cs) in enumerate(PASSES):
                                mm = nc.tensor.matmul(out_ps[:, qt % 2, :], weigh_t[0:k, ws, c, :],
                                                      cr[0:k, cs, c, :], start=(c == 0 and m == 0),
                                                      stop=(c == MC - 1 and m == 2))
                        mm.then_inc(read_out, 1)


def experts(nc, sem, rows, w_experts, gate_wT, expert_bias):
    with ExitStack() as ctx:
        def sb(name, shape, dt=F32):
            return ctx.enter_context(nc.sbuf_tensor(name, shape, dt))

        x2_t = sb("x2_t", [P, 2, DC, NT * P], F32R)
        weight = sb("weight", [P, (E + 1) * NT])
        SHARED = E

        route(nc, sem, rows, x2_t, weight, gate_wT, expert_bias)

        w_raw = sb("w_raw", [P, WE])
        w_sp = sb("w_sp", [P, 2, 2, WE], F32R)
        gated = sb("gated", [P, IC, T])
        h_f = sb("h_f", [P, IC, T])
        h_sp = sb("h_sp", [P, 2, 2, IC, T], F32R)
        gate_ps = ctx.enter_context(nc.psum_tensor("gate_ps", [P, IC, T], F32))
        up_ps = ctx.enter_context(nc.psum_tensor("up_ps", [P, IC, T], F32))
        down_ps = ctx.enter_context(nc.psum_tensor("down_ps", [P, TT, D], F32))

        w_in, w_hi, w_lo = sem("m_w_in"), sem("m_w_hi"), sem("m_w_lo")
        gate_done, up_done, down_done = sem("m_gate_done"), sem("m_up_done"), sem("m_down_done")
        silu_done, h_done, h_hi, h_lo = sem("m_silu_done"), sem("m_h_done"), sem("m_h_hi"), sem("m_h_lo")
        combined = sem("m_combined")

        SPLITS = 3
        PART = WE // SPLITS

        def gate_w(par, part, c, i):
            at = c * I + i * P
            return w_sp[:, par, part, at:at + P]

        def up_w(par, part, c, i):
            at = DC * I + c * I + i * P
            return w_sp[:, par, part, at:at + P]

        def down_w(par, part, i):
            at = 2 * DC * I + i * D
            return w_sp[:, par, part, at:at + D]

        def pipeline(eng, front, back):
            front(0, 0, 0)
            with eng.Fori(0, E // 2) as pair:
                for par in range(2):
                    e = pair * 2 + par
                    for blk in range(B):
                        if blk < B - 1:
                            front(e, par, blk + 1)
                        else:
                            front(e + 1, 1 - par, 0)
                        back(e, par, blk)
            for blk in range(B):
                if blk < B - 1:
                    front(SHARED, 0, blk + 1)
                back(SHARED, 0, blk)

        with nc.Block() as block:

            @block.sync
            def _(sp):
                sp.dma_start(w_raw[:, :], w_experts[0]).then_inc(w_in, 16)
                with sp.Fori(1, E + 1) as e:
                    sp.wait_ge(w_lo, e * SPLITS)
                    sp.dma_start(w_raw[:, :], w_experts[e]).then_inc(w_in, 16)

            @block.scalar
            def _(act):
                def split(e, par, n):
                    act.wait_ge(w_in, e * 16 + 16)
                    nc.scalar.activation(w_sp[:, par, 0, n * PART:(n + 1) * PART], w_raw[:, n * PART:(n + 1) * PART],
                                         ACT.Copy).then_inc(w_hi, 1)

                def front(e, par, blk):
                    u = e * B + blk
                    act.wait_ge(gate_done, u + 1)
                    act.wait_ge(h_done, u)
                    nc.scalar.activation(gated[:, :, :], gate_ps[:, :, :], ACT.Silu).then_inc(silu_done, 1)
                    act.wait_ge(h_done, u + 1)
                    if not isinstance(u, int) or u >= 2:
                        act.wait_ge(down_done, (u - 1) * TT)
                    nc.scalar.activation(h_sp[:, blk % 2, 0, :, :], h_f[:, :, :], ACT.Copy).then_inc(h_hi, 1)

                def back(e, par, blk):
                    if blk < SPLITS and not (isinstance(e, int) and e == SHARED):
                        act.wait_ge(down_done, e * (B * TT))
                        split(e + 1, 1 - par, blk)

                for n in range(SPLITS):
                    split(0, 0, n)
                pipeline(act, front, back)

            @block.vector
            def _(dve):
                def split(e, par, n):
                    part = slice(n * PART, (n + 1) * PART)
                    dve.wait_ge(w_hi, e * SPLITS + n + 1)
                    nc.vector.tensor_tensor(w_sp[:, par, 1, part], w_raw[:, part], w_sp[:, par, 0, part].bitcast(F32),
                                            ALU.subtract).then_inc(w_lo, 1)

                def front(e, par, blk):
                    u = e * B + blk
                    dve.wait_ge(silu_done, u + 1)
                    dve.wait_ge(up_done, u + 1)
                    dve.wait_ge(h_lo, u)
                    nc.vector.tensor_tensor(h_f[:, :, :], up_ps[:, :, :], gated[:, :, :], ALU.mult).then_inc(h_done, 1)
                    dve.wait_ge(h_hi, u + 1)
                    nc.vector.tensor_tensor(h_sp[:, blk % 2, 1, :, :], h_f[:, :, :],
                                            h_sp[:, blk % 2, 0, :, :].bitcast(F32), ALU.subtract).then_inc(h_lo, 1)

                def back(e, par, blk):
                    u = e * B + blk
                    if blk < SPLITS and not (isinstance(e, int) and e == SHARED):
                        split(e + 1, 1 - par, blk)
                    dve.wait_ge(combined, u * TT)
                    for tt in range(TT):
                        t = blk * TT + tt
                        dve.wait_ge(down_done, u * TT + tt + 1)
                        nc.vector.scalar_tensor_tensor(rows[:, t, :], down_ps[:, tt, :],
                                                       weight[:, bass.ds(e * NT + t, 1)], rows[:, t, :],
                                                       ALU.mult, ALU.add).then_inc(combined, 1)

                for n in range(SPLITS):
                    split(0, 0, n)
                pipeline(dve, front, back)

            @block.tensor
            def _(pe):
                def front(e, par, blk):
                    u = e * B + blk
                    if blk == 0:
                        pe.wait_ge(w_lo, e * SPLITS + SPLITS)
                    for ps, w, free, done in ((gate_ps, gate_w, silu_done, gate_done), (up_ps, up_w, h_done, up_done)):
                        pe.wait_ge(free, u)
                        for i in range(IC):
                            for c in range(DC):
                                for n, (ws, xs) in enumerate(PASSES):
                                    mm = nc.tensor.matmul(ps[:, i, :], w(par, ws, c, i),
                                                          x2_t[:, xs, c, blk * T:(blk + 1) * T],
                                                          start=(c == 0 and n == 0), stop=(c == DC - 1 and n == 2))
                        mm.then_inc(done, 1)

                def back(e, par, blk):
                    u = e * B + blk
                    pe.wait_ge(h_lo, u + 1)
                    pe.wait_ge(combined, u * TT)
                    for tt in range(TT):
                        for i in range(IC):
                            for n, (hs, ws) in enumerate(PASSES):
                                mm = nc.tensor.matmul(down_ps[:, tt, :], h_sp[:, blk % 2, hs, i, tt * P:(tt + 1) * P],
                                                      down_w(par, ws, i), start=(i == 0 and n == 0),
                                                      stop=(i == IC - 1 and n == 2))
                        mm.then_inc(down_done, 1)

                pipeline(pe, front, back)


def route(nc, sem, rows, x2_t, weight, gate_wT, expert_bias):
    with ExitStack() as ctx:
        def sb(name, shape, dt=F32):
            return ctx.enter_context(nc.sbuf_tensor(name, shape, dt))

        mean_var, rstd = layer_norm_scales(nc, sem, ctx, rows, "norm2")
        x2 = sb("x2", [P, TT, D])
        gw = sb("gw", [P, DC, P])
        gw_sp = sb("gw_sp", [P, 2, DC, P], F32R)
        bias = sb("bias", [P, E])
        logits_t = sb("logits_t", [P, T])
        score = sb("score", [P, NT, E])
        ranked = sb("ranked", [P, NT, E])
        top = sb("top", [P, NT, 8])
        top_at = sb("top_at", [P, NT, 8], U32)
        top_f = sb("top_f", [P, NT, TOPK])
        expert_id = sb("expert_id", [P, E])
        hit = sb("hit", [P, NT, E, TOPK])
        chosen = sb("chosen", [P, NT, E])
        total = sb("total", [P, NT])
        ident = sb("r_ident", [P, P])
        turn_ps = ctx.enter_context(nc.psum_tensor("r_turn_ps", [P, 4, 512], F32))
        logit_ps = ctx.enter_context(nc.psum_tensor("r_logit_ps", [P, 512], F32))
        score_ps = ctx.enter_context(nc.psum_tensor("r_score_ps", [P, 512], F32))

        gate_in, consts = sem("r_gate_in"), sem("r_consts")
        gw_hi, gw_lo = sem("r_gw_hi"), sem("r_gw_lo")
        normed, kept = sem("r_normed"), sem("r_kept")
        turned, x2_hi, x2_lo = sem("r_turned"), sem("r_x2_hi"), sem("r_x2_lo")
        logits, logits_out, scores_turned = sem("r_logits"), sem("r_logits_out"), sem("r_scores_turned")
        scored, step = sem("r_scored"), sem("r_step")

        with nc.Block() as block:

            @block.sync
            def _(sp):
                sp.wait_ge(consts, 4)
                sp.dma_start(gw[:, :, 0:E], gate_wT).then_inc(gate_in, 16)
                sp.dma_start(bias[:, :], expert_bias).then_inc(gate_in, 16)

            @block.gpsimd
            def _(pool):
                nc.gpsimd.memset(ident[:, :], 1.0).then_inc(consts, 1)
                nc.gpsimd.memset(gw[:, :, :], 0.0).then_inc(consts, 1)
                nc.gpsimd.iota(expert_id[:, :], pattern=[[1, E]], base=0, channel_multiplier=0,
                               allow_small_or_imprecise_dtypes=True).then_inc(consts, 1)
                pool.wait_ge(consts, 3)
                nc.gpsimd.affine_select(out=ident[:, :], in_=ident[:, :], compare_op=ALU.is_equal, fill=0.0,
                                        base=0, pattern=[[-1, P]], channel_multiplier=1).then_inc(consts, 1)

            @block.scalar
            def _(act):
                act.wait_ge(gate_in, 32)
                nc.scalar.activation(gw_sp[:, 0, :, :], gw[:, :, :], ACT.Copy).then_inc(gw_hi, 1)
                with act.Fori(0, B) as b:
                    for c in range(DC):
                        act.wait_ge(turned, b * DC + c + 1)
                        nc.scalar.activation(x2_t[:, 0, c, bass.ds(b * T, T)], turn_ps[:, c, :], ACT.Copy
                                             ).then_inc(x2_hi, 1)
                    act.wait_ge(logits, b + 1)
                    act.wait_ge(scores_turned, b)
                    nc.scalar.activation(logits_t[:, :], logit_ps[:, :], ACT.Copy).then_inc(logits_out, 1)
                    act.wait_ge(scores_turned, b + 1)
                    nc.scalar.activation(score[:, bass.ds(b * TT, TT), :],
                                         score_ps[:, :].rearrange("p (t e) -> p t e", e=P)[:, :, 0:E],
                                         ACT.Sigmoid).then_inc(scored, 1)

            @block.vector
            def _(dve):
                nc.vector.memset(weight[:, E * NT:(E + 1) * NT], 1.0)
                dve.wait_ge(gw_hi, 1)
                nc.vector.tensor_tensor(gw_sp[:, 1, :, :], gw[:, :, :], gw_sp[:, 0, :, :].bitcast(F32),
                                        ALU.subtract).then_inc(gw_lo, 1)
                with dve.Fori(0, B) as b:
                    dve.wait_ge(turned, b * DC)
                    dve.wait_ge(kept, b * TT)
                    for t in range(TT):
                        nc.vector.tensor_scalar(x2[:, t, :], rows[:, b * TT + t, :],
                                                mean_var[:, bass.ds(b * TT + t, 1), 0],
                                                rstd[:, bass.ds(b * TT + t, 1)], ALU.subtract, ALU.mult
                                                ).then_inc(normed, 1)
                    for t in range(TT):
                        dve.wait_ge(normed, b * TT + t + 1)
                        nc.vector.tensor_scalar(rows[:, b * TT + t, :], x2[:, t, :], 1.0, None, ALU.mult
                                                ).then_inc(kept, 1)
                    for c in range(DC):
                        dve.wait_ge(x2_hi, b * DC + c + 1)
                        nc.vector.tensor_tensor(x2_t[:, 1, c, bass.ds(b * T, T)], turn_ps[:, c, :],
                                                x2_t[:, 0, c, bass.ds(b * T, T)].bitcast(F32), ALU.subtract
                                                ).then_inc(x2_lo, 1)
                dve.wait_ge(scored, B)
                dve.wait_ge(gate_in, 32)
                nc.vector.tensor_tensor(ranked[:, :, :], score[:, :, :],
                                        bias[:, :].unsqueeze(1).broadcast_to([P, NT, E]), ALU.add).then_inc(step, 1)
                dve.wait_ge(step, 1)
                for t in range(NT):
                    nc.vector.max(top[:, t, :], ranked[:, t, :]).then_inc(step, 1)
                for t in range(NT):
                    dve.wait_ge(step, 2 + t)
                    nc.vector.max_index(top_at[:, t, :], top[:, t, :], ranked[:, t, :]).then_inc(step, 1)
                n = 1 + 2 * NT
                dve.wait_ge(step, n)
                nc.vector.tensor_copy(top_f[:, :, :], top_at[:, :, 0:TOPK]).then_inc(step, 1)
                dve.wait_ge(step, n + 1)
                dve.wait_ge(consts, 4)
                for j in range(TOPK):
                    nc.vector.tensor_tensor(hit[:, :, :, j], expert_id[:, :].unsqueeze(1).broadcast_to([P, NT, E]),
                                            top_f[:, :, j:j + 1].broadcast_to([P, NT, E]), ALU.is_equal
                                            ).then_inc(step, 1)
                n += 1 + TOPK
                dve.wait_ge(step, n)
                nc.vector.tensor_reduce(chosen[:, :, :], hit[:, :, :, :], AX, ALU.add).then_inc(step, 1)
                dve.wait_ge(step, n + 1)
                nc.vector.tensor_tensor(chosen[:, :, :], chosen[:, :, :], score[:, :, :], ALU.mult).then_inc(step, 1)
                dve.wait_ge(step, n + 2)
                nc.vector.tensor_reduce(total[:, :], chosen[:, :, :], AX, ALU.add).then_inc(step, 1)
                dve.wait_ge(step, n + 3)
                nc.vector.reciprocal(total[:, :], total[:, :]).then_inc(step, 1)
                dve.wait_ge(step, n + 4)
                nc.vector.tensor_tensor(weight[:, 0:E * NT].rearrange("p (e t) -> p t e", t=NT), chosen[:, :, :],
                                        total[:, :].unsqueeze(2).broadcast_to([P, NT, E]), ALU.mult
                                        ).then_inc(step, 1)

            @block.tensor
            def _(pe):
                pe.wait_ge(consts, 4)
                pe.wait_ge(gw_lo, 1)
                with pe.Fori(0, B) as b:
                    pe.wait_ge(normed, b * TT + TT)
                    pe.wait_ge(x2_lo, b * DC)
                    for c in range(DC):
                        for t in range(TT):
                            mm = nc.tensor.transpose(turn_ps[:, c, t * P:(t + 1) * P],
                                                     x2[:, t, c * P:(c + 1) * P], ident[:, :])
                        mm.then_inc(turned, 1)
                    pe.wait_ge(logits_out, b)
                    for c in range(DC):
                        pe.wait_ge(x2_lo, b * DC + c + 1)
                        for n, (ws, xs) in enumerate(PASSES):
                            mm = nc.tensor.matmul(logit_ps[:, :], gw_sp[:, ws, c, :], x2_t[:, xs, c, bass.ds(b * T, T)],
                                                  start=(c == 0 and n == 0), stop=(c == DC - 1 and n == 2))
                    mm.then_inc(logits, 1)
                    pe.wait_ge(logits_out, b + 1)
                    pe.wait_ge(scored, b)
                    for t in range(TT):
                        mm = nc.tensor.transpose(score_ps[:, t * P:(t + 1) * P], logits_t[:, t * P:(t + 1) * P],
                                                 ident[:, :])
                    mm.then_inc(scores_turned, 1)


def final_norm(nc, sem, rows, out):
    with ExitStack() as ctx:
        mean_var, rstd = layer_norm_scales(nc, sem, ctx, rows, "norm3")
        normed, stored = sem("f_normed"), sem("f_stored")
        with nc.Block() as block:

            @block.vector
            def _(dve):
                for t in range(NT):
                    nc.vector.tensor_scalar(rows[:, t, :], rows[:, t, :], mean_var[:, t, 0:1], rstd[:, t:t + 1],
                                            ALU.subtract, ALU.mult).then_inc(normed, 1)

            @block.sync
            def _(sp):
                for b in range(B):
                    sp.wait_ge(normed, (b + 1) * TT)
                    sp.dma_start(out[b].rearrange("(t p) d -> p t d", p=P), rows[:, b * TT:(b + 1) * TT, :]
                                 ).then_inc(stored, 16)
                sp.wait_ge(stored, B * 16)


def decoder_block(nc, xT, x, ctxT, ctx_rows, mask, wqkvT, woT, rope, w_experts, gate_wT, expert_bias, out):
    with ExitStack() as ctx:
        def sem(name):
            return ctx.enter_context(nc.semaphore(name))

        rows = ctx.enter_context(nc.sbuf_tensor("rows", [P, NT, D], F32))
        self_attention(nc, sem, rows, xT, x, wqkvT, woT, rope)
        cross_attention(nc, sem, rows, ctxT, ctx_rows, mask)
        experts(nc, sem, rows, w_experts, gate_wT, expert_bias)
        final_norm(nc, sem, rows, out)


def by_chunk(w):
    n, k = w.shape
    return w.reshape(n, k // P, P).transpose(2, 1, 0)


def kernel(x, ctx_2048, mask_BxS2_bk0, L0_attn_Wq, L0_attn_Wk, L0_attn_Wv, L0_attn_Wo, L0_ffn_gate_w,
           L0_ffn_expert_bias, L0_ffn_w_gate, L0_ffn_w_up, L0_ffn_w_down, L0_ffn_sw_gate, L0_ffn_sw_up,
           L0_ffn_sw_down):
    import concourse.bacc as bacc
    from concourse.bass_utils import run_bass_kernel_spmd

    x, context = np.asarray(x), np.asarray(ctx_2048)
    tokens = x.reshape(NT * P, D)
    qkv = [by_chunk(np.asarray(w)).reshape(P, DC, HG, GH * HD) for w in (L0_attn_Wq, L0_attn_Wk, L0_attn_Wv)]

    def packed(gate, up, down):
        return np.concatenate([by_chunk(np.asarray(w)).reshape(P, -1) for w in (gate, up, down)], axis=1)

    w_all = [packed(L0_ffn_w_gate[e], L0_ffn_w_up[e], L0_ffn_w_down[e]) for e in range(E)]
    w_all.append(packed(L0_ffn_sw_gate, L0_ffn_sw_up, L0_ffn_sw_down))
    inv_freq = (1.0 / 10000.0 ** (np.arange(HD // 2, dtype=np.float32) / (HD // 2))).astype(np.float32)
    angles = np.arange(T, dtype=np.float32)[:, None] * inv_freq
    cos, sin = (np.tile(np.repeat(f(angles), 2, axis=-1), (1, GH)).astype(np.float32) for f in (np.cos, np.sin))
    sin[:, 0::2] *= -1

    ins = {
        "xT": tokens.T.reshape(DC, P, B, T).transpose(2, 1, 0, 3),
        "x_rows": tokens.reshape(NT, P, D).transpose(1, 0, 2),
        "ctxT": context.reshape(B, M, DC, P).transpose(0, 3, 2, 1),
        "ctx_rows": context,
        "mask": np.asarray(mask_BxS2_bk0).reshape(B, 1, M),
        "wqkvT": np.stack(qkv, axis=3).reshape(P, DC, HG * GW),
        "woT": by_chunk(np.asarray(L0_attn_Wo)).reshape(P, HG * D),
        "rope": np.stack([cos, sin]).reshape(2, TT, P, GH * HD).transpose(0, 2, 1, 3),
        "w_experts": np.stack(w_all),
        "gate_wT": by_chunk(np.asarray(L0_ffn_gate_w)),
        "expert_bias": np.broadcast_to(np.asarray(L0_ffn_expert_bias), (P, E)),
    }
    nc = bacc.Bacc("TRN2", target_bir_lowering=False, num_devices=1)
    ins = {name: np.ascontiguousarray(a) for name, a in ins.items()}
    args = {name: nc.dram_tensor(name, a.shape, mybir.dt.from_np(a.dtype), kind="ExternalInput").ap()
            for name, a in ins.items()}
    out = nc.dram_tensor("out", (B, T, D), F32, kind="ExternalOutput").ap()
    decoder_block(nc, args["xT"], args["x_rows"], args["ctxT"], args["ctx_rows"], args["mask"], args["wqkvT"],
                  args["woT"], args["rope"], args["w_experts"], args["gate_wT"], args["expert_bias"], out)
    return run_bass_kernel_spmd(nc, [ins], core_ids=[0]).results[0]["out"]
```

```python
from contextlib import ExitStack

import numpy as np

import concourse.bass as bass
from concourse import mybir

F32 = mybir.dt.float32
F32R = mybir.dt.float32r
BF16 = mybir.dt.bfloat16
U8 = mybir.dt.uint8
U32 = mybir.dt.uint32
ALU = mybir.AluOpType
ACT = mybir.ActivationFunctionType
AX = mybir.AxisListType.X

P = 128
B, T, D = 4, 512, 512
NH, HD = 16, 32
M = 1601
E, I, TOPK = 16, 256, 4
EPS = 1e-5
MASKED = -1e30

TT = T // P
NT = B * TT
DC = D // P
IC = I // P
HG = NH * HD // P
GH = NH // HG
QK = 2 * GH * HD
GW = QK + GH * HD
MQ = 402
MP = 4 * MQ
MC = -(-M // P)
ML = MP - (MC - 1) * P
MR = M - (MC - 1) * P
WE = 2 * DC * I + IC * D
PASSES = ((0, 0), (0, 1), (1, 0))


def self_attention(nc, sem, rows, xT, x, wqkvT, woT, rope):
    with ExitStack() as ctx:
        def sb(name, shape, dt=F32):
            return ctx.enter_context(nc.sbuf_tensor(name, shape, dt))

        x_raw = sb("x_raw", [P, DC, T])
        x_sp = sb("x_sp", [P, 2, DC, T], F32R)
        wqkv = sb("wqkv", [P, 2, DC, HG * GW], F32R)
        wo = sb("wo", [P, 2, HG, D], F32R)
        cos_t = sb("cos_t", [P, TT, GW - QK])
        sin_t = sb("sin_t", [P, TT, GW - QK])
        qk_cos = sb("qk_cos", [P, 2, TT, GH * HD])
        qk_sin = sb("qk_sin", [P, 2, TT, GH * HD])
        qk_sp = sb("qk_sp", [P, 2, TT, GH, 3, HD], F32R)
        v = sb("v", [P, 2, TT, GH * HD])
        q_st = sb("q_st", [P, GH, T], F32R)
        k_st = sb("k_st", [P, GH, T], F32R)
        p_t = sb("p_t", [P, GH, TT * (TT + 1) // 2 * P])
        row_max = sb("row_max", [P, TT, GH])
        neg_max = sb("neg_max", [P, TT, GH, 32], F32R)
        o_f = sb("o_f", [P, T])
        o_sp = sb("o_sp", [P, 2, HG, T], F32R)
        ident_f = sb("ident_f", [P, P])
        ident_r = sb("ident_r", [P, P], F32R)
        ident_b = sb("ident_b", [P, P], BF16)
        mask_qk = sb("mask_qk", [P, P], BF16)
        mask_kq = sb("mask_kq", [P, P], BF16)
        ones = sb("ones", [P, HD])

        proj_ps = ctx.enter_context(nc.psum_tensor("proj_ps", [P, 4, 512], F32))
        score_ps = ctx.enter_context(nc.psum_tensor("score_ps", [P, 2, 512], F32))
        o_ps = ctx.enter_context(nc.psum_tensor("o_ps", [P, 512], F32))
        den_ps = ctx.enter_context(nc.psum_tensor("den_ps", [P, 512], F32))

        tables_in, x_in, rows_in = sem("tables_in"), sem("x_in"), sem("rows_in")
        w_in = [sem(f"w_in{slot}") for slot in range(3)]
        const_pool, const_ready = sem("const_pool"), sem("const_ready")
        w_hi, w_lo = sem("w_hi"), sem("w_lo")
        x_hi, x_lo = sem("x_hi"), sem("x_lo")
        projected, roped = sem("projected"), sem("roped")
        v_copied = sem("v_copied")
        q_hi, q_lo, k_hi, k_lo = sem("q_hi"), sem("q_lo"), sem("k_hi"), sem("k_lo")
        turned, q_stacked, k_stacked = sem("turned"), sem("q_stacked"), sem("k_stacked")
        scored, maxed, max_hi, max_lo = sem("scored"), sem("maxed"), sem("max_hi"), sem("max_lo")
        max_turned = sem("max_turned")
        max_stacked_a, max_stacked_v = sem("max_stacked_a"), sem("max_stacked_v")
        scored_t, exped, summed = sem("scored_t"), sem("exped"), sem("summed")
        den_inv, o_scaled, o_hi, o_lo = sem("den_inv"), sem("o_scaled"), sem("o_hi"), sem("o_lo")
        out_proj, res_added = sem("out_proj"), sem("res_added")

        NG = B * HG
        assert HG == TT
        p_at = [sum(TT - j for j in range(kc)) * P for kc in range(TT)]
        W_LOADS = DC + 1
        w_raw = p_t[:, :, :].rearrange("p h n -> p (h n)")

        def weight_load(n):
            slot = n % 3
            if n < DC:
                return slot, w_raw[:, slot * HG * GW:(slot + 1) * HG * GW], wqkv[:, 0, n, :], wqkv[:, 1, n, :]
            assert (slot, n) == (1, DC) and HG * GW + HG * D <= 3 * HG * GW
            return slot, w_raw[:, HG * GW:HG * GW + HG * D], *(wo[:, part, :, :].rearrange("p g n -> p (g n)")
                                                               for part in range(2))

        def split_places(s):
            stack = qk_sp[:, s, :, :, :, :].rearrange("p t h n d -> p (t h) n d")
            src = qk_cos[:, s, :, :].rearrange("p t (h d) -> p (t h) d", d=HD)
            return src, (stack[:, :, 0:2, :], stack[:, :, 0:3:2, :])[s], stack[:, :, 0, :], stack[:, :, 2 - s, :]

        def twice(src):
            return src.unsqueeze(2).broadcast_to([P, TT * GH, 2, HD])

        def groups(body, finish):
            def run(eng):
                for hg in range(HG):
                    body(0, hg, hg == 0, False)
                with eng.Fori(1, B - 1) as b:
                    for hg in range(HG):
                        body(b, hg, False, False)
                for hg in range(HG):
                    body(B - 1, hg, False, hg == HG - 1)
                finish()
            return run

        with nc.Block() as block:

            @block.sync
            def _(sp):
                sp.dma_start(x_raw[:, :, :], xT[0]).then_inc(x_in, 16)
                for n in range(W_LOADS):
                    if n == DC:
                        sp.wait_ge(w_lo, 3)
                    elif n >= 3:
                        sp.wait_ge(w_lo, n - 2)
                    slot, place, _, _ = weight_load(n)
                    sp.dma_start(place, wqkvT[:, n, :] if n < DC else woT).then_inc(w_in[slot], 16)
                    if n == 2:
                        sp.dma_start(cos_t[:, :, :], rope[0]).then_inc(tables_in, 16)
                        sp.dma_start(sin_t[:, :, :], rope[1]).then_inc(tables_in, 16)
                sp.dma_start(rows[:, :, :], x).then_inc(rows_in, 16)
                with sp.Fori(1, B) as b:
                    sp.wait_ge(x_lo, b)
                    sp.dma_start(x_raw[:, :, :], xT[b]).then_inc(x_in, 16)

            @block.gpsimd
            def _(pool):
                nc.gpsimd.memset(ident_f[:, :], 1.0).then_inc(const_pool, 1)
                nc.gpsimd.memset(ident_b[:, :], 1.0).then_inc(const_pool, 1)
                nc.gpsimd.memset(mask_qk[:, :], 0.0).then_inc(const_pool, 1)
                nc.gpsimd.memset(mask_kq[:, :], 0.0).then_inc(const_pool, 1)
                nc.gpsimd.memset(ones[:, :], 1.0).then_inc(const_pool, 1)
                pool.wait_ge(const_pool, 5)
                for m in (ident_f, ident_b):
                    nc.gpsimd.affine_select(out=m[:, :], in_=m[:, :], compare_op=ALU.is_equal, fill=0.0,
                                            base=0, pattern=[[-1, P]], channel_multiplier=1).then_inc(const_pool, 1)
                nc.gpsimd.affine_select(out=mask_qk[:, :], in_=mask_qk[:, :], compare_op=ALU.is_ge, fill=MASKED,
                                        base=0, pattern=[[-1, P]], channel_multiplier=1).then_inc(const_pool, 1)
                nc.gpsimd.affine_select(out=mask_kq[:, :], in_=mask_kq[:, :], compare_op=ALU.is_ge, fill=MASKED,
                                        base=0, pattern=[[1, P]], channel_multiplier=-1).then_inc(const_pool, 1)

                def lo_x(b):
                    pool.wait_ge(x_hi, b + 1)
                    nc.gpsimd.tensor_tensor(x_sp[:, 1, :, :], x_raw[:, :, :], x_sp[:, 0, :, :].bitcast(F32),
                                            ALU.subtract).then_inc(x_lo, 1)

                def lo_q(g):
                    pool.wait_ge(q_hi, g + 1)
                    src, _, hi, lo = split_places(0)
                    nc.gpsimd.tensor_tensor(lo, src, hi.bitcast(F32), ALU.subtract).then_inc(q_lo, 1)

                def lo_out(g, hg):
                    pool.wait_ge(o_hi, g + 1)
                    nc.gpsimd.tensor_tensor(o_sp[:, 1, hg, :], o_f[:, :], o_sp[:, 0, hg, :].bitcast(F32),
                                            ALU.subtract).then_inc(o_lo, 1)

                def group(b, hg, first, last):
                    g = b * HG + hg
                    if not first:
                        lo_out(g - 1, (hg - 1) % HG)
                    if not last:
                        lo_q(g + 1)
                    if hg == HG - 2 and not (isinstance(b, int) and b == B - 1):
                        lo_x(b + 1)

                lo_x(0)
                lo_q(0)
                groups(group, lambda: lo_out(NG - 1, HG - 1))(pool)

            @block.scalar
            def _(act):
                def split_x(b):
                    act.wait_ge(x_in, b * 16 + 16)
                    act.wait_ge(projected, b * (HG * TT))
                    nc.scalar.activation(x_sp[:, 0, :, :], x_raw[:, :, :], ACT.Copy).then_inc(x_hi, 1)

                def keep_v(g, par):
                    act.wait_ge(projected, g * TT + TT)
                    if not isinstance(g, int) or g >= 2:
                        act.wait_ge(summed, g - 1)
                    nc.scalar.activation(v[:, par, :, :], proj_ps[:, :, QK:GW], ACT.Copy).then_inc(v_copied, 1)

                def hi_q(g):
                    act.wait_ge(roped, g * 6 + 3)
                    act.wait_ge(turned, g * 2 * GH)
                    src, two_hi, _, _ = split_places(0)
                    nc.scalar.activation(two_hi, twice(src), ACT.Copy).then_inc(q_hi, 1)

                def hi_out(g, hg):
                    act.wait_ge(o_scaled, g + 1)
                    if hg == 0:
                        act.wait_ge(out_proj, g)
                    nc.scalar.activation(o_sp[:, 0, hg, :], o_f[:, :], ACT.Copy).then_inc(o_hi, 1)

                def group(b, hg, first, last):
                    g = b * HG + hg
                    act.wait_ge(scored_t, g * GH * TT)
                    for h in range(GH):
                        act.wait_ge(turned, g * 2 * GH + 2 * h + 1)
                        nc.scalar.activation(q_st[0:3 * HD, h, :], proj_ps[0:3 * HD, 2 * h % 4, :],
                                             ACT.Copy).then_inc(q_stacked, 1)
                    if not first:
                        hi_out(g - 1, (hg - 1) % HG)
                    act.wait_ge(max_turned, g + 1)
                    for h in range(0, GH, 2):
                        nc.scalar.activation(q_st[3 * HD:P, h, :], den_ps[32 * h:32 * h + 32, :],
                                             ACT.Copy).then_inc(max_stacked_a, 1)
                    act.wait_ge(summed, g)
                    for kc in range(TT):
                        w = T - kc * P
                        for h in range(GH):
                            n = kc * GH + h
                            act.wait_ge(scored_t, g * GH * TT + n + 1)
                            nc.scalar.activation(p_t[:, h, p_at[kc]:p_at[kc] + w],
                                                 score_ps[:, n % 2, kc * P:T], ACT.Exp,
                                                 scale=float(HD) ** -0.5).then_inc(exped, 1)
                            if n == 1 and not last:
                                keep_v(g + 1, (hg + 1) % 2)
                            if n == 2 * GH + 1 and not last:
                                hi_q(g + 1)
                    if hg == HG - 2 and not (isinstance(b, int) and b == B - 1):
                        split_x(b + 1)

                split_x(0)
                for n in range(W_LOADS):
                    slot, place, hi, _ = weight_load(n)
                    act.wait_ge(w_in[slot], 16 * (n // 3 + 1))
                    nc.scalar.activation(hi, place, ACT.Copy).then_inc(w_hi, 1)
                keep_v(0, 0)
                hi_q(0)
                act.wait_ge(w_lo, W_LOADS)
                groups(group, lambda: hi_out(NG - 1, HG - 1))(act)

            @block.vector
            def _(dve):
                dve.wait_ge(const_pool, 9)
                nc.vector.tensor_copy(ident_r[:, :], ident_f[:, :]).then_inc(const_ready, 1)
                nc.vector.memset(neg_max[:, :, :, :].bitcast(F32), 0.0).then_inc(const_ready, 1)
                nc.vector.memset(k_st[3 * HD:P, :, :].bitcast(F32), 1.0).then_inc(const_ready, 1)
                for n in range(W_LOADS):
                    dve.wait_ge(w_hi, n + 1)
                    _, place, hi, lo = weight_load(n)
                    nc.vector.tensor_tensor(lo, place, hi.bitcast(F32), ALU.subtract).then_inc(w_lo, 1)

                def rotate(g):
                    dve.wait_ge(projected, g * TT + TT)
                    dve.wait_ge(v_copied, g + 1)
                    dve.wait_ge(q_lo, g)
                    for s in range(2):
                        part = slice(s * QK // 2, (s + 1) * QK // 2)
                        nc.vector.tensor_tensor(qk_cos[:, s, :, :], proj_ps[:, :, part], cos_t[:, :, :],
                                                ALU.mult).then_inc(roped, 1)
                        swapped = proj_ps[:, :, part].rearrange("p t (n two) -> p t n two", two=2)[:, :, :, ::-1]
                        nc.vector.tensor_tensor(qk_sin[:, s, :, :].rearrange("p t (n two) -> p t n two", two=2),
                                                swapped, sin_t[:, :, :].rearrange("p t (n two) -> p t n two", two=2),
                                                ALU.mult).then_inc(roped, 1)
                        dve.wait_ge(roped, g * 6 + 3 * s + 2)
                        nc.vector.tensor_tensor(qk_cos[:, s, :, :], qk_cos[:, s, :, :], qk_sin[:, s, :, :],
                                                ALU.add).then_inc(roped, 1)
                    dve.wait_ge(roped, g * 6 + 6)
                    dve.wait_ge(turned, g * 2 * GH)
                    src, two_hi, hi, lo = split_places(1)
                    nc.vector.tensor_copy(two_hi, twice(src)).then_inc(k_hi, 1)
                    dve.wait_ge(k_hi, g + 1)
                    nc.vector.tensor_tensor(lo, src, hi.bitcast(F32), ALU.subtract).then_inc(k_lo, 1)

                sums_t = qk_sin[:, 0, :, :].rearrange("p t (n j) -> p (t n) j", j=HD)
                inv_t = qk_sin[:, 1, 0, 0:T // HD]

                def invert_sums(g, part):
                    if part == 0:
                        dve.wait_ge(summed, g + 1)
                        nc.vector.transpose(sums_t, den_ps[:, :].rearrange("p (n j) -> p n j", j=HD)
                                            ).then_inc(den_inv, 1)
                    elif part == 1:
                        dve.wait_ge(den_inv, g * 3 + 1)
                        nc.vector.reciprocal(inv_t, sums_t[:, :, 0]).then_inc(den_inv, 1)
                    elif part == 2:
                        dve.wait_ge(o_lo, g)
                        dve.wait_ge(den_inv, g * 3 + 2)
                        nc.vector.transpose(o_f[:, :].rearrange("p (n j) -> p n j", j=HD),
                                            inv_t.unsqueeze(2).broadcast_to([P, T // HD, HD])).then_inc(den_inv, 1)

                def finish_out(g):
                    dve.wait_ge(den_inv, g * 3 + 3)
                    nc.vector.tensor_tensor(o_f[:, :], o_ps[:, :], o_f[:, :], ALU.mult).then_inc(o_scaled, 1)

                def add_residual(b):
                    for tt in range(TT):
                        dve.wait_ge(out_proj, b * TT + tt + 1)
                        row = rows[:, b * TT + tt, :]
                        nc.vector.tensor_tensor(row, (o_ps, den_ps)[tt % 2][:, :], row, ALU.add
                                                ).then_inc(res_added, 1)

                def group(b, hg, first, last):
                    g = b * HG + hg
                    dve.wait_ge(scored_t, g * GH * TT)
                    for h in range(GH):
                        dve.wait_ge(turned, g * 2 * GH + 2 * h + 2)
                        nc.vector.tensor_copy(k_st[0:3 * HD, h, :], proj_ps[0:3 * HD, (2 * h + 1) % 4, :]
                                              ).then_inc(k_stacked, 1)
                    for qt in range(TT):
                        for h in range(GH):
                            n = qt * GH + h
                            dve.wait_ge(scored, g * GH * TT + n + 1)
                            if n == 0:
                                dve.wait_ge(max_lo, g)
                            nc.vector.tensor_reduce(row_max[:, qt, h:h + 1], score_ps[:, n % 2, 0:(qt + 1) * P],
                                                    AX, ALU.max).then_inc(maxed, 1)
                            if n % 2 == 1 and n < 2 * GH and not first:
                                if n // 2 < 3:
                                    invert_sums(g - 1, n // 2)
                                elif n // 2 == 3:
                                    finish_out(g - 1)
                    dve.wait_ge(maxed, g * GH * TT + GH * TT)
                    dve.wait_ge(max_turned, g)
                    nc.vector.tensor_scalar(neg_max[:, :, :, 0], row_max[:, :, :], -1.0, None,
                                            ALU.mult).then_inc(max_hi, 1)
                    dve.wait_ge(max_hi, g + 1)
                    nc.vector.scalar_tensor_tensor(neg_max[:, :, :, 1], row_max[:, :, :], -1.0,
                                                   neg_max[:, :, :, 0].bitcast(F32), ALU.mult, ALU.subtract
                                                   ).then_inc(max_lo, 1)
                    if hg == 0 and not first:
                        add_residual(b - 1)
                    dve.wait_ge(max_turned, g + 1)
                    for h in range(1, GH, 2):
                        nc.vector.tensor_copy(q_st[3 * HD:P, h, :], den_ps[32 * h:32 * h + 32, :]
                                              ).then_inc(max_stacked_v, 1)
                    if not last:
                        rotate(g + 1)

                def finish():
                    for part in range(3):
                        invert_sums(NG - 1, part)
                    finish_out(NG - 1)
                    add_residual(B - 1)

                dve.wait_ge(tables_in, 32)
                rotate(0)
                dve.wait_ge(rows_in, 16)
                groups(group, finish)(dve)

            @block.tensor
            def _(pe):
                products = [(tt, c, n) for tt in range(TT) for c in range(DC) for n in range(3)]

                def project(g, hg, start, stop):
                    for tt, c, n in products[start:stop]:
                        xs, ws = PASSES[n]
                        mm = nc.tensor.matmul(proj_ps[:, tt, 0:GW], x_sp[:, xs, c, tt * P:(tt + 1) * P],
                                              wqkv[:, ws, c, hg * GW:(hg + 1) * GW],
                                              start=(c == 0 and n == 0), stop=(c == DC - 1 and n == 2))
                        if c == DC - 1 and n == 2:
                            mm.then_inc(projected, 1)

                def project_out(b):
                    pe.wait_ge(o_lo, b * HG + HG)
                    for tt in range(TT):
                        if tt >= 2:
                            pe.wait_ge(res_added, b * TT + tt - 1)
                        for c in range(HG):
                            for n, (os, ws) in enumerate(PASSES):
                                mm = nc.tensor.matmul((o_ps, den_ps)[tt % 2][:, :], o_sp[:, os, c, tt * P:(tt + 1) * P],
                                                      wo[:, ws, c, :], start=(c == 0 and n == 0),
                                                      stop=(c == HG - 1 and n == 2))
                        mm.then_inc(out_proj, 1)

                def scores(g, qt, half):
                    w = (qt + 1) * P
                    for h in range(2 * half, 2 * half + 2):
                        n = qt * GH + h
                        if qt == 0:
                            pe.wait_ge(q_stacked, g * GH + h + 1)
                            pe.wait_ge(k_stacked, g * GH + h + 1)
                        if n >= 2:
                            pe.wait_ge(maxed, g * GH * TT + n - 1)
                        else:
                            pe.wait_ge(exped, g * GH * TT)
                        wide = max(w, 2 * P)
                        nc.tensor.matmul(score_ps[:, n % 2, 0:wide], q_st[0:3 * HD, h, qt * P:w],
                                         k_st[0:3 * HD, h, 0:wide], start=True, stop=False)
                        nc.tensor.matmul(score_ps[:, n % 2, w - P:w], ident_b[:, :], mask_qk[:, :],
                                         start=False, stop=True).then_inc(scored, 1)

                def scores_t(g, kc, half):
                    q0 = min(kc * P, T - 2 * P)
                    for h in range(2 * half, 2 * half + 2):
                        n = kc * GH + h
                        if kc == 0 and h % 2 == 0:
                            pe.wait_ge(max_stacked_a, g * (GH // 2) + h // 2 + 1)
                        if kc == 0 and h % 2 == 1:
                            pe.wait_ge(max_stacked_v, g * (GH // 2) + h // 2 + 1)
                        if n >= 2:
                            pe.wait_ge(exped, g * GH * TT + n - 1)
                        nc.tensor.matmul(score_ps[:, n % 2, q0:T], k_st[:, h, kc * P:(kc + 1) * P],
                                         q_st[:, h, q0:T], start=True, stop=False)
                        nc.tensor.matmul(score_ps[:, n % 2, kc * P:(kc + 1) * P], ident_b[:, :],
                                         mask_kq[:, :], start=False, stop=True).then_inc(scored_t, 1)

                def values(g, hg, kc):
                    pe.wait_ge(exped, g * GH * TT + (kc + 1) * GH)
                    for h in range(GH):
                        nc.tensor.matmul(o_ps[h * HD:(h + 1) * HD, kc * P:T], v[:, hg % 2, kc, h * HD:(h + 1) * HD],
                                         p_t[:, h, p_at[kc]:p_at[kc] + T - kc * P],
                                         start=(kc == 0), stop=(kc == TT - 1))

                def weight_sums(g, kc):
                    for h in range(GH):
                        mm = nc.tensor.matmul(den_ps[h * HD:(h + 1) * HD, kc * P:T], ones[:, :],
                                              p_t[:, h, p_at[kc]:p_at[kc] + T - kc * P],
                                              start=(kc == 0), stop=(kc == TT - 1))
                    return mm

                def group(b, hg, first, last):
                    g = b * HG + hg
                    pe.wait_ge(q_lo, g + 1)
                    pe.wait_ge(roped, g * 6 + 5)
                    pe.wait_ge(v_copied, g + 1)
                    for n in range(2 * GH):
                        h, s = n // 2, n % 2
                        if n == 1:
                            pe.wait_ge(k_lo, g + 1)
                        if n >= 4:
                            pe.wait_ge(k_stacked if s else q_stacked, g * GH + h - 1)
                        for tt in range(TT):
                            mm = nc.tensor.transpose(proj_ps[0:3 * HD, n % 4, tt * P:(tt + 1) * P].bitcast(F32R),
                                                     qk_sp[:, s, tt, h, :, :].rearrange("p n d -> p (n d)"),
                                                     ident_r[:, :])
                        mm.then_inc(turned, 1)
                    if hg == HG - 1 and not last:
                        pe.wait_ge(x_lo, b + 2)
                    STEP = 5
                    for n in range(2 * TT):
                        scores(g, n // 2, n % 2)
                        if n == 1 and not last:
                            pe.wait_ge(q_stacked, g * GH + GH)
                            pe.wait_ge(k_stacked, g * GH + GH)
                        if n >= 1 and not last:
                            project(g + 1, (hg + 1) % HG, (n - 1) * STEP, n * STEP)
                    if hg == 0 and not first:
                        project_out(b - 1)
                    at = (2 * TT - 1) * STEP
                    pe.wait_ge(max_lo, g + 1)
                    if hg == 0 and not first:
                        pe.wait_ge(res_added, b * TT)
                    pe.wait_ge(o_scaled, g)
                    for qt in range(TT):
                        mm = nc.tensor.transpose(den_ps[:, qt * P:(qt + 1) * P].bitcast(F32R),
                                                 neg_max[:, qt, :, :].rearrange("p h n -> p (h n)"), ident_r[:, :])
                    mm.then_inc(max_turned, 1)
                    if not last:
                        project(g + 1, (hg + 1) % HG, at, at + 7)
                    pe.wait_ge(maxed, g * GH * TT + GH * TT)
                    scores_t(g, 0, 0)
                    if not last:
                        project(g + 1, (hg + 1) % HG, at + 7, len(products))
                    scores_t(g, 0, 1)
                    for kc in range(1, TT):
                        scores_t(g, kc, 0)
                        values(g, hg, kc - 1)
                        scores_t(g, kc, 1)
                        weight_sums(g, kc - 1)
                    values(g, hg, TT - 1)
                    weight_sums(g, TT - 1).then_inc(summed, 1)

                pe.wait_ge(const_ready, 3)
                pe.wait_ge(w_lo, W_LOADS)
                pe.wait_ge(x_lo, 1)
                project(0, 0, 0, len(products))
                groups(group, lambda: project_out(B - 1))(pe)


def layer_norm(nc, sem, ctx, rows, name):
    stats = ctx.enter_context(nc.sbuf_tensor(name + "_stats", [P, NT, 6], F32))
    mean_var = ctx.enter_context(nc.sbuf_tensor(name + "_mean_var", [P, NT, 2], F32))
    eps = ctx.enter_context(nc.sbuf_tensor(name + "_eps", [P, 1], F32))
    rstd = ctx.enter_context(nc.sbuf_tensor(name + "_rstd", [P, NT], F32))
    half_v = ctx.enter_context(nc.sbuf_tensor(name + "_half_v", [P, NT], F32))
    eps_set, gathered, aggregated = sem(name + "_eps_set"), sem(name + "_gathered"), sem(name + "_aggregated")
    rooted, inverted, normed = sem(name + "_rooted"), sem(name + "_inverted"), sem(name + "_normed")

    def statistics(dve, b):
        if b == 0:
            nc.vector.memset(eps[:, :], EPS).then_inc(eps_set, 1)
        for t in range(b * TT, b * TT + TT):
            nc.vector.bn_stats(stats[:, t, :], rows[:, t, :]).then_inc(gathered, 1)
        for t in range(b * TT, b * TT + TT):
            dve.wait_ge(gathered, t + 1)
            nc.vector.bn_aggr(mean_var[:, t, :], stats[:, t, :]).then_inc(aggregated, 1)

    def root(act, b):
        mine = slice(b * TT, b * TT + TT)
        act.wait_ge(eps_set, 1)
        act.wait_ge(aggregated, b * TT + TT)
        nc.scalar.activation(rstd[:, mine], mean_var[:, mine, 1], ACT.Sqrt, bias=eps[:, 0:1]).then_inc(rooted, 1)

    def normalise(dve, b):
        mine = slice(b * TT, b * TT + TT)
        dve.wait_ge(aggregated, b * TT + TT)
        nc.vector.tensor_scalar(half_v[:, mine], mean_var[:, mine, 1], EPS, -0.5, ALU.add, ALU.mult
                                ).then_inc(inverted, 1)
        dve.wait_ge(rooted, b + 1)
        nc.vector.reciprocal(rstd[:, mine], rstd[:, mine]).then_inc(inverted, 1)
        for n in range(2):
            dve.wait_ge(inverted, b * 5 + 2 + n)
            nc.vector.tensor_tensor(half_v[:, mine], half_v[:, mine], rstd[:, mine], ALU.mult).then_inc(inverted, 1)
        dve.wait_ge(inverted, b * 5 + 4)
        nc.vector.scalar_tensor_tensor(rstd[:, mine], half_v[:, mine], 1.5, rstd[:, mine], ALU.add, ALU.mult
                                       ).then_inc(inverted, 1)
        dve.wait_ge(inverted, b * 5 + 5)
        for t in range(b * TT, b * TT + TT):
            nc.vector.tensor_scalar(rows[:, t, :], rows[:, t, :], mean_var[:, t, 0:1], rstd[:, t:t + 1],
                                    ALU.subtract, ALU.mult).then_inc(normed, 1)

    return statistics, root, normalise, normed


def cross_attention(nc, sem, rows, ctxT, ctx_rows, mask):
    with ExitStack() as ctx:
        def sb(name, shape, dt=F32):
            return ctx.enter_context(nc.sbuf_tensor(name, shape, dt))

        statistics, root, normalise, normed = layer_norm(nc, sem, ctx, rows, "norm1")
        raw = sb("raw", [P, 2, 4 * D])
        ct = sb("ct", [P, 2, DC, MP], F32R)
        cr = sb("cr", [P, 2, MC, D], F32R)
        x1 = sb("x1", [P, TT, D])
        x1_t = sb("x1_t", [P, 2, DC, T], F32R)
        mask_u8 = sb("mask_u8", [1, MP], U8)
        mask_bias = sb("mask_bias", [1, MP], BF16)
        any_kept = sb("any_kept", [1, 1])
        weigh = sb("weigh", [P, MP])
        weigh_t = sb("weigh_t", [P, 2, MC, P], F32R)
        stat = sb("stat", [P, 2, 4])
        kept = sb("kept", [P, 1])
        ident = sb("c_ident", [P, P])
        ones_b = sb("c_ones_b", [1, P], BF16)
        ones_f = sb("c_ones_f", [1, P])

        score_ps = ctx.enter_context(nc.psum_tensor("c_score_ps", [P, 4, 512], F32))
        turn_ps = ctx.enter_context(nc.psum_tensor("c_turn_ps", [P, 2, 512], F32))
        out_ps = ctx.enter_context(nc.psum_tensor("c_out_ps", [P, 2, 512], F32))

        raw_in = [sem("c_raw_in0"), sem("c_raw_in1")]
        mask_in = sem("c_mask_in")
        consts, zeroed = sem("c_consts"), sem("c_zeroed")
        raw_hi, raw_lo = sem("c_raw_hi"), sem("c_raw_lo")
        mask_read, kept_done = sem("c_mask_read"), sem("c_kept_done")
        x1_kept, x1_turned, x1_hi, x1_lo = sem("c_x1_kept"), sem("c_x1_turned"), sem("c_x1_hi"), sem("c_x1_lo")
        scored, maxed, exped = sem("c_scored"), sem("c_maxed"), sem("c_exped")
        inverted, w_turned, w_hi, w_lo = sem("c_inverted"), sem("c_w_turned"), sem("c_w_hi"), sem("c_w_lo")
        read_out, written = sem("c_read_out"), sem("c_written")

        SCALE = float(D) ** -0.5
        row_groups = [(c, min(c + 4, MC - 1)) for c in range(0, MC - 1, 4)] + [(MC - 1, MC)]
        LOADS = DC + len(row_groups)
        TG = [(c, min(c + 4, MC)) for c in range(0, MC, 4)]
        NG = len(TG)
        TURNS = {MC - 8: 0, MC - 6: 1, MC - 4: 2, MC - 2: 3}
        assert LOADS % 2 == 0 and TT % 2 == 0 and len(TURNS) == DC

        def places(n):
            if n < DC:
                return raw[:, n % 2, 0:M], ct[:, 0, n, 0:M], ct[:, 1, n, 0:M]
            c0, c1 = row_groups[n - DC]
            k = P if c1 < MC else MR
            return (raw[0:k, n % 2, 0:(c1 - c0) * D],
                    *(cr[0:k, part, c0:c1, :].rearrange("p c d -> p (c d)") for part in range(2)))

        def loaded(b, n):
            return b * (16 * LOADS // 2) + 16 * (n // 2 + 1)

        with nc.Block() as block:

            @block.sync
            def _(sp):
                def load(b, n):
                    dst = places(n)[0]
                    if n < DC:
                        sp.dma_start(dst, ctxT[b, :, n, :]).then_inc(raw_in[n % 2], 16)
                    elif n < LOADS - 1:
                        c0, c1 = row_groups[n - DC]
                        sp.dma_start(dst.rearrange("p (c d) -> p c d", d=D),
                                     ctx_rows[b, c0 * P:c1 * P, :].rearrange("(c p) d -> p c d", p=P)
                                     ).then_inc(raw_in[n % 2], 16)
                    else:
                        sp.dma_start(dst, ctx_rows[b, (MC - 1) * P:M, :]).then_inc(raw_in[n % 2], 16)

                def rest(b):
                    for n in range(2, LOADS):
                        sp.wait_ge(raw_lo, b * LOADS + n - 1)
                        load(b, n)

                load(0, 0)
                load(0, 1)
                sp.wait_ge(consts, 5)
                sp.dma_start(mask_u8[:, 0:M], mask[0]).then_inc(mask_in, 16)
                rest(0)
                with sp.Fori(1, B) as b:
                    sp.wait_ge(mask_read, b * 2)
                    sp.wait_ge(raw_lo, b * LOADS - 1)
                    load(b, 0)
                    sp.dma_start(mask_u8[:, 0:M], mask[b]).then_inc(mask_in, 16)
                    sp.wait_ge(raw_lo, b * LOADS)
                    load(b, 1)
                    rest(b)

            @block.gpsimd
            def _(pool):
                nc.gpsimd.memset(ident[:, :], 1.0).then_inc(consts, 1)
                nc.gpsimd.memset(ones_b[:, :], 1.0).then_inc(consts, 1)
                nc.gpsimd.memset(ones_f[:, :], 1.0).then_inc(consts, 1)
                nc.gpsimd.memset(mask_u8[:, :], 0).then_inc(consts, 1)
                pool.wait_ge(consts, 4)
                nc.gpsimd.affine_select(out=ident[:, :], in_=ident[:, :], compare_op=ALU.is_equal, fill=0.0,
                                        base=0, pattern=[[-1, P]], channel_multiplier=1).then_inc(consts, 1)

            @block.scalar
            def _(act):
                def hi_context(b, n):
                    act.wait_ge(raw_in[n % 2], loaded(b, n))
                    src, hi, _ = places(n)
                    nc.scalar.activation(hi, src, ACT.Copy).then_inc(raw_hi, 1)

                def hi_x1(b, c):
                    act.wait_ge(x1_turned, b * DC + c + 1)
                    nc.scalar.activation(x1_t[:, 0, c, :], turn_ps[:, c % 2, :], ACT.Copy).then_inc(x1_hi, 1)

                def batch(b, last):
                    for qt in range(TT):
                        n = b * TT + qt
                        act.wait_ge(maxed, n * 2 + 2)
                        act.wait_ge(w_turned, n * NG)
                        nc.scalar.activation(weigh[:, :].rearrange("p (f m) -> p f m", f=4), score_ps[:, :, 0:MQ],
                                             ACT.Exp, bias=stat[:, qt % 2, 1:2], scale=SCALE,
                                             accum_out=stat[:, qt % 2, 2:3]).then_inc(exped, 1)
                        if qt == 0:
                            act.wait_ge(read_out, n)
                            for m in range(DC, LOADS):
                                hi_context(b, m)
                        if qt == TT - 1 and not last:
                            for c in range(DC):
                                hi_x1(b + 1, c)
                                if c >= 1:
                                    hi_context(b + 1, c)
                        act.wait_ge(read_out, n)
                        for i, (c0, c1) in enumerate(TG):
                            act.wait_ge(w_turned, n * NG + i + 1)
                            k = P if c1 < MC else ML
                            nc.scalar.activation(weigh_t[0:k, 0, c0:c1, :].rearrange("p c q -> p (c q)"),
                                                 turn_ps[0:k, i % 2, 0:(c1 - c0) * P], ACT.Copy).then_inc(w_hi, 1)
                        if qt == 1 and not last:
                            act.wait_ge(normed, (b + 1) * TT + TT)
                            act.wait_ge(x1_turned, (b + 1) * DC)
                            nc.scalar.activation(x1[:, :, :], rows[:, bass.ds((b + 1) * TT, TT), :], ACT.Copy
                                                 ).then_inc(x1_kept, 1)
                        if qt == TT - 2 and not last:
                            act.wait_ge(scored, b * TT + TT)
                            hi_context(b + 1, 0)

                act.wait_ge(zeroed, 4)
                for c in range(DC):
                    if c == 2:
                        for b in range(B):
                            root(act, b)
                    hi_context(0, c)
                for c in range(DC):
                    hi_x1(0, c)
                with act.Fori(0, B - 1) as b:
                    batch(b, False)
                batch(B - 1, True)

            @block.vector
            def _(dve):
                def lo_context(b, n):
                    src, hi, lo = places(n)
                    dve.wait_ge(raw_hi, b * LOADS + n + 1)
                    nc.vector.tensor_tensor(lo, src, hi.bitcast(F32), ALU.subtract).then_inc(raw_lo, 1)

                def lo_x1(b, c):
                    dve.wait_ge(x1_hi, b * DC + c + 1)
                    nc.vector.tensor_tensor(x1_t[:, 1, c, :], turn_ps[:, c % 2, :], x1_t[:, 0, c, :].bitcast(F32),
                                            ALU.subtract).then_inc(x1_lo, 1)

                def read_mask(b):
                    dve.wait_ge(mask_in, b * 16 + 16)
                    dve.wait_ge(scored, b * TT)
                    nc.vector.tensor_scalar(mask_bias[:, :], mask_u8[:, :], 1.0, -MASKED, ALU.subtract,
                                            ALU.mult).then_inc(mask_read, 1)
                    nc.vector.tensor_reduce(any_kept[:, :], mask_u8[:, :], AX, ALU.max).then_inc(mask_read, 1)

                def maximum(b, qt):
                    n = b * TT + qt
                    dve.wait_ge(scored, n + 1)
                    if qt == 0:
                        nc.vector.tensor_copy(kept[:, :], score_ps[:, 0, MQ:MQ + 1]).then_inc(kept_done, 1)
                    nc.vector.tensor_reduce(stat[:, qt % 2, 0:1], score_ps[:, :, 0:MQ],
                                            mybir.AxisListType.XY, ALU.max).then_inc(maxed, 1)
                    dve.wait_ge(maxed, n * 2 + 1)
                    nc.vector.tensor_scalar(stat[:, qt % 2, 1:2], stat[:, qt % 2, 0:1], 0.1 * MASKED, -SCALE,
                                            ALU.max, ALU.mult).then_inc(maxed, 1)

                def write(b, qt):
                    n = b * TT + qt
                    dve.wait_ge(inverted, n * 3 + 3)
                    dve.wait_ge(read_out, n + 1)
                    row = rows[:, b * TT + qt, :]
                    nc.vector.scalar_tensor_tensor(row, out_ps[:, qt % 2, :], stat[:, qt % 2, 3:4], row,
                                                   ALU.mult, ALU.add).then_inc(written, 1)

                def batch(b, last):
                    for qt in range(TT):
                        n = b * TT + qt
                        dve.wait_ge(exped, n + 1)
                        nc.vector.tensor_scalar(stat[:, qt % 2, 3:4], stat[:, qt % 2, 2:3], 1e-30, None,
                                                ALU.max).then_inc(inverted, 1)
                        dve.wait_ge(inverted, n * 3 + 1)
                        nc.vector.reciprocal(stat[:, qt % 2, 3:4], stat[:, qt % 2, 3:4]).then_inc(inverted, 1)
                        dve.wait_ge(inverted, n * 3 + 2)
                        dve.wait_ge(kept_done, b + 1)
                        nc.vector.tensor_tensor(stat[:, qt % 2, 3:4], stat[:, qt % 2, 3:4], kept[:, :],
                                                ALU.mult).then_inc(inverted, 1)
                        if qt == 0:
                            for m in range(DC, LOADS):
                                lo_context(b, m)
                        if qt == TT - 1 and not last:
                            for c in range(DC):
                                lo_x1(b + 1, c)
                                if c >= 1:
                                    lo_context(b + 1, c)
                        if qt == TT - 1:
                            write(b, TT - 2)
                        for i, (c0, c1) in enumerate(TG):
                            dve.wait_ge(w_hi, n * NG + i + 1)
                            k = P if c1 < MC else ML
                            nc.vector.tensor_tensor(weigh_t[0:k, 1, c0:c1, :].rearrange("p c q -> p (c q)"),
                                                    turn_ps[0:k, i % 2, 0:(c1 - c0) * P],
                                                    weigh_t[0:k, 0, c0:c1, :].rearrange("p c q -> p (c q)").bitcast(F32),
                                                    ALU.subtract).then_inc(w_lo, 1)
                        if qt < TT - 1:
                            maximum(b, qt + 1)
                        elif not last:
                            maximum(b + 1, 0)
                        if qt == TT - 2 and not last:
                            read_mask(b + 1)
                            lo_context(b + 1, 0)
                        if qt != TT - 2:
                            write(b, qt)

                for part in range(2):
                    nc.vector.memset(ct[:, part, :, M:MP].bitcast(F32), 0.0).then_inc(zeroed, 1)
                    nc.vector.memset(cr[:, part, MC - 1, :].bitcast(F32), 0.0).then_inc(zeroed, 1)
                for b in range(B):
                    statistics(dve, b)
                dve.wait_ge(zeroed, 4)
                for c in range(DC):
                    lo_context(0, c)
                read_mask(0)
                normalise(dve, 0)
                for c in range(DC):
                    lo_x1(0, c)
                for b in range(1, B):
                    normalise(dve, b)
                maximum(0, 0)
                with dve.Fori(0, B - 1) as b:
                    batch(b, False)
                batch(B - 1, True)

            @block.tensor
            def _(pe):
                def turn_x1(b, c, src):
                    if c >= 2:
                        pe.wait_ge(x1_lo, b * DC + c - 1)
                    elif isinstance(b, int):
                        pass
                    else:
                        pe.wait_ge(w_lo, b * (TT * NG) - NG - 1 + c)
                    for t in range(TT):
                        mm = nc.tensor.transpose(turn_ps[:, c % 2, t * P:(t + 1) * P],
                                                 src[:, t, c * P:(c + 1) * P], ident[:, :])
                    mm.then_inc(x1_turned, 1)

                def scores(b, qt):
                    n = b * TT + qt
                    pe.wait_ge(exped, n)
                    if qt == 0:
                        pe.wait_ge(mask_read, b * 2 + 2)
                        pe.wait_ge(x1_lo, b * DC + DC)
                        nc.tensor.matmul(score_ps[:, 0, MQ:MQ + 1], ones_f[:, :], any_kept[:, :], start=True,
                                         stop=True)
                    if qt == 1:
                        pe.wait_ge(kept_done, b + 1)
                    for f in range(4):
                        nc.tensor.matmul(score_ps[:, f, 0:MQ], ones_b[:, :], mask_bias[:, f * MQ:(f + 1) * MQ],
                                         start=True, stop=False)
                    for c in range(DC):
                        if qt == 0:
                            pe.wait_ge(raw_lo, b * LOADS + c + 1)
                        for xs, cs in PASSES:
                            for f in range(4):
                                mm = nc.tensor.matmul(score_ps[:, f, 0:MQ], x1_t[:, xs, c, qt * P:(qt + 1) * P],
                                                      ct[:, cs, c, f * MQ:(f + 1) * MQ], start=False,
                                                      stop=(c == DC - 1 and (xs, cs) == PASSES[-1]))
                    mm.then_inc(scored, 1)

                def batch(b, last):
                    for qt in range(TT):
                        n = b * TT + qt
                        if qt < TT - 1:
                            scores(b, qt + 1)
                        elif not last:
                            scores(b + 1, 0)
                        pe.wait_ge(exped, n + 1)
                        if qt == TT - 1 and not last:
                            pe.wait_ge(x1_lo, (b + 1) * DC + DC)
                        for i, (c0, c1) in enumerate(TG):
                            if i >= 2:
                                pe.wait_ge(w_lo, n * NG + i - 1)
                            for c in range(c0, c1):
                                k = P if c < MC - 1 else ML
                                mm = nc.tensor.transpose(turn_ps[0:k, i % 2, (c - c0) * P:(c - c0 + 1) * P],
                                                         weigh[:, c * P:c * P + k], ident[:, :])
                            mm.then_inc(w_turned, 1)
                        if qt >= 1:
                            pe.wait_ge(written, n - 1 if qt > 1 else b * TT)
                        for c in range(MC):
                            k = P if c < MC - 1 else ML
                            if qt == TT - 2 and not last and c in TURNS:
                                if c == MC - 8:
                                    pe.wait_ge(x1_kept, b + 1)
                                    pe.wait_ge(scored, b * TT + TT)
                                turn_x1(b + 1, TURNS[c], x1)
                            pe.wait_ge(w_lo, n * NG + c // 4 + 1)
                            if qt == 0:
                                pe.wait_ge(raw_lo, b * LOADS + min(DC + c // 4, LOADS - 1) + 1)
                            for m, (ws, cs) in enumerate(PASSES):
                                mm = nc.tensor.matmul(out_ps[:, qt % 2, :], weigh_t[0:k, ws, c, :],
                                                      cr[0:k, cs, c, :], start=(c == 0 and m == 0),
                                                      stop=(c == MC - 1 and m == 2))
                        mm.then_inc(read_out, 1)

                pe.wait_ge(consts, 5)
                pe.wait_ge(normed, TT)
                for c in range(DC):
                    turn_x1(0, c, rows)
                scores(0, 0)
                with pe.Fori(0, B - 1) as b:
                    batch(b, False)
                batch(B - 1, True)


def experts(nc, sem, rows, w_experts, gate_wT, expert_bias, out):
    with ExitStack() as ctx:
        def sb(name, shape, dt=F32):
            return ctx.enter_context(nc.sbuf_tensor(name, shape, dt))

        x2_stats, x2_root, x2_normalise, x2_normed = layer_norm(nc, sem, ctx, rows, "norm2")
        out_stats, out_root, out_normalise, out_normed = layer_norm(nc, sem, ctx, rows, "norm3")
        x2_t = sb("x2_t", [P, 2, DC, NT * P], F32R)
        weight = sb("weight", [P, (1 + E) * NT])
        w_raw = sb("w_raw", [P, WE])
        w_sp = sb("w_sp", [P, 2, 2, WE], F32R)
        gated = sb("gated", [P, IC, T])
        h_f = sb("h_f", [P, IC, T])
        h_sp = sb("h_sp", [P, 2, 2, IC, T], F32R)
        gw = sb("gw", [P, DC, P])
        gw_sp = sb("gw_sp", [P, 2, DC, P], F32R)
        bias = sb("bias", [P, E])
        logits_t = sb("logits_t", [P, T])
        score = sb("score", [P, NT, E])
        ranked = sb("ranked", [P, NT, E])
        top = sb("top", [P, NT, 8])
        top_at = sb("top_at", [P, NT, 8], U32)
        top_f = sb("top_f", [P, NT, TOPK])
        expert_id = sb("expert_id", [P, E])
        hit = sb("hit", [P, NT, E, TOPK])
        chosen = sb("chosen", [P, NT, E])
        total = sb("total", [P, NT])
        ident = sb("r_ident", [P, P])

        gate_ps = ctx.enter_context(nc.psum_tensor("gate_ps", [P, IC, T], F32))
        up_ps = ctx.enter_context(nc.psum_tensor("up_ps", [P, IC, T], F32))
        down_ps = ctx.enter_context(nc.psum_tensor("down_ps", [P, TT, D], F32))
        turn_ps, logit_ps, score_ps = down_ps, up_ps[:, 0, :], up_ps[:, 1, :]

        gate_in, consts = sem("r_gate_in"), sem("r_consts")
        gw_hi, gw_lo = sem("r_gw_hi"), sem("r_gw_lo")
        turned, x2_hi, x2_lo = sem("r_turned"), sem("r_x2_hi"), sem("r_x2_lo")
        logits, logits_out, scores_turned = sem("r_logits"), sem("r_logits_out"), sem("r_scores_turned")
        scored, step = sem("r_scored"), sem("r_step")
        w_in, w_hi, w_lo = sem("m_w_in"), sem("m_w_hi"), sem("m_w_lo")
        gate_done, up_done, down_done = sem("m_gate_done"), sem("m_up_done"), sem("m_down_done")
        silu_done, h_done, h_hi, h_lo = sem("m_silu_done"), sem("m_h_done"), sem("m_h_hi"), sem("m_h_lo")
        combined, stored = sem("m_combined"), sem("m_stored")

        ALL = 1 + E
        SPLITS = 3
        PART = WE // SPLITS
        ROUTE_STEPS = 1 + 2 * NT + 1 + TOPK + 5

        def gate_w(par, part, c, i):
            at = c * I + i * P
            return w_sp[:, par, part, at:at + P]

        def up_w(par, part, c, i):
            at = DC * I + c * I + i * P
            return w_sp[:, par, part, at:at + P]

        def down_w(par, part, i):
            at = 2 * DC * I + i * D
            return w_sp[:, par, part, at:at + D]

        def is_last(e):
            return isinstance(e, int) and e == ALL - 1

        def pipeline(eng, front, back):
            def expert(e, par):
                for blk in range(B):
                    if blk < B - 1:
                        front(e, par, blk + 1)
                    elif not is_last(e):
                        front(e + 1, 1 - par, 0)
                    back(e, par, blk)

            front(0, 0, 0)
            expert(0, 0)
            with eng.Fori(0, (ALL - 3) // 2) as pair:
                expert(pair * 2 + 1, 1)
                expert(pair * 2 + 2, 0)
            expert(ALL - 2, 1)
            expert(ALL - 1, 0)

        with nc.Block() as block:

            @block.sync
            def _(sp):
                sp.dma_start(w_raw[:, :], w_experts[0]).then_inc(w_in, 16)
                sp.wait_ge(consts, 4)
                sp.dma_start(gw[:, :, 0:E], gate_wT).then_inc(gate_in, 16)
                sp.dma_start(bias[:, :], expert_bias).then_inc(gate_in, 16)
                with sp.Fori(1, ALL) as e:
                    sp.wait_ge(w_lo, e * SPLITS)
                    sp.dma_start(w_raw[:, :], w_experts[e]).then_inc(w_in, 16)
                for b in range(B):
                    sp.wait_ge(out_normed, (b + 1) * TT)
                    sp.dma_start(out[b].rearrange("(t p) d -> p t d", p=P), rows[:, b * TT:(b + 1) * TT, :]
                                 ).then_inc(stored, 16)
                sp.wait_ge(stored, B * 16)

            @block.gpsimd
            def _(pool):
                nc.gpsimd.memset(ident[:, :], 1.0).then_inc(consts, 1)
                nc.gpsimd.memset(gw[:, :, :], 0.0).then_inc(consts, 1)
                nc.gpsimd.iota(expert_id[:, :], pattern=[[1, E]], base=0, channel_multiplier=0,
                               allow_small_or_imprecise_dtypes=True).then_inc(consts, 1)
                pool.wait_ge(consts, 3)
                nc.gpsimd.affine_select(out=ident[:, :], in_=ident[:, :], compare_op=ALU.is_equal, fill=0.0,
                                        base=0, pattern=[[-1, P]], channel_multiplier=1).then_inc(consts, 1)

            @block.scalar
            def _(act):
                def split(e, par, n):
                    act.wait_ge(w_in, e * 16 + 16)
                    nc.scalar.activation(w_sp[:, par, 0, n * PART:(n + 1) * PART], w_raw[:, n * PART:(n + 1) * PART],
                                         ACT.Copy).then_inc(w_hi, 1)

                def front(e, par, blk):
                    u = e * B + blk
                    act.wait_ge(gate_done, u + 1)
                    act.wait_ge(h_done, u)
                    nc.scalar.activation(gated[:, :, :], gate_ps[:, :, :], ACT.Silu).then_inc(silu_done, 1)
                    act.wait_ge(h_done, u + 1)
                    if not isinstance(u, int) or u >= 2:
                        act.wait_ge(down_done, (u - 1) * TT)
                    nc.scalar.activation(h_sp[:, blk % 2, 0, :, :], h_f[:, :, :], ACT.Copy).then_inc(h_hi, 1)

                def back(e, par, blk):
                    if is_last(e):
                        out_root(act, blk)
                    elif blk < SPLITS:
                        act.wait_ge(down_done, e * (B * TT))
                        split(e + 1, 1 - par, blk)

                act.wait_ge(gate_in, 32)
                nc.scalar.activation(gw_sp[:, 0, :, :], gw[:, :, :], ACT.Copy).then_inc(gw_hi, 1)
                x2_root(act, 0)
                for n in range(SPLITS):
                    split(0, 0, n)
                for b in range(1, B):
                    x2_root(act, b)
                for b in range(B):
                    for c in range(DC):
                        act.wait_ge(turned, b * DC + c + 1)
                        nc.scalar.activation(x2_t[:, 0, c, b * T:(b + 1) * T], turn_ps[:, c, :], ACT.Copy
                                             ).then_inc(x2_hi, 1)
                    act.wait_ge(logits, b + 1)
                    if b >= 1:
                        act.wait_ge(scores_turned, b)
                    nc.scalar.activation(logits_t[:, :], logit_ps, ACT.Copy).then_inc(logits_out, 1)
                    act.wait_ge(scores_turned, b + 1)
                    nc.scalar.activation(score[:, b * TT:(b + 1) * TT, :],
                                         score_ps.rearrange("p (t e) -> p t e", e=P)[:, :, 0:E],
                                         ACT.Sigmoid).then_inc(scored, 1)
                pipeline(act, front, back)

            @block.vector
            def _(dve):
                def split(e, par, n):
                    part = slice(n * PART, (n + 1) * PART)
                    dve.wait_ge(w_hi, e * SPLITS + n + 1)
                    nc.vector.tensor_tensor(w_sp[:, par, 1, part], w_raw[:, part], w_sp[:, par, 0, part].bitcast(F32),
                                            ALU.subtract).then_inc(w_lo, 1)

                def front(e, par, blk):
                    u = e * B + blk
                    dve.wait_ge(silu_done, u + 1)
                    dve.wait_ge(up_done, u + 1)
                    dve.wait_ge(h_lo, u)
                    nc.vector.tensor_tensor(h_f[:, :, :], up_ps[:, :, :], gated[:, :, :], ALU.mult).then_inc(h_done, 1)
                    dve.wait_ge(h_hi, u + 1)
                    nc.vector.tensor_tensor(h_sp[:, blk % 2, 1, :, :], h_f[:, :, :],
                                            h_sp[:, blk % 2, 0, :, :].bitcast(F32), ALU.subtract).then_inc(h_lo, 1)

                def back(e, par, blk):
                    u = e * B + blk
                    if isinstance(e, int) and e == 0 and blk == 0:
                        route()
                    if blk < SPLITS and not is_last(e):
                        split(e + 1, 1 - par, blk)
                    dve.wait_ge(combined, u * TT)
                    if not isinstance(e, int) and blk == 0:
                        dve.wait_ge(step, ROUTE_STEPS)
                    for tt in range(TT):
                        t = blk * TT + tt
                        dve.wait_ge(down_done, u * TT + tt + 1)
                        nc.vector.scalar_tensor_tensor(rows[:, t, :], down_ps[:, tt, :],
                                                       weight[:, bass.ds(e * NT + t, 1)], rows[:, t, :],
                                                       ALU.mult, ALU.add).then_inc(combined, 1)
                    if is_last(e):
                        dve.wait_ge(combined, (u + 1) * TT)
                        out_stats(dve, blk)
                        if blk >= 1:
                            out_normalise(dve, blk - 1)

                def split_x2(b):
                    for c in range(DC):
                        dve.wait_ge(x2_hi, b * DC + c + 1)
                        nc.vector.tensor_tensor(x2_t[:, 1, c, b * T:(b + 1) * T], turn_ps[:, c, :],
                                                x2_t[:, 0, c, b * T:(b + 1) * T].bitcast(F32), ALU.subtract
                                                ).then_inc(x2_lo, 1)

                def route():
                    dve.wait_ge(scored, B)
                    dve.wait_ge(gate_in, 32)
                    nc.vector.tensor_tensor(ranked[:, :, :], score[:, :, :],
                                            bias[:, :].unsqueeze(1).broadcast_to([P, NT, E]), ALU.add).then_inc(step, 1)
                    dve.wait_ge(step, 1)
                    for t in range(NT):
                        nc.vector.max(top[:, t, :], ranked[:, t, :]).then_inc(step, 1)
                    for t in range(NT):
                        dve.wait_ge(step, 2 + t)
                        nc.vector.max_index(top_at[:, t, :], top[:, t, :], ranked[:, t, :]).then_inc(step, 1)
                    n = 1 + 2 * NT
                    dve.wait_ge(step, n)
                    nc.vector.tensor_copy(top_f[:, :, :], top_at[:, :, 0:TOPK]).then_inc(step, 1)
                    dve.wait_ge(step, n + 1)
                    dve.wait_ge(consts, 4)
                    for j in range(TOPK):
                        nc.vector.tensor_tensor(hit[:, :, :, j], expert_id[:, :].unsqueeze(1).broadcast_to([P, NT, E]),
                                                top_f[:, :, j:j + 1].broadcast_to([P, NT, E]), ALU.is_equal
                                                ).then_inc(step, 1)
                    n += 1 + TOPK
                    dve.wait_ge(step, n)
                    nc.vector.tensor_reduce(chosen[:, :, :], hit[:, :, :, :], AX, ALU.add).then_inc(step, 1)
                    dve.wait_ge(step, n + 1)
                    nc.vector.tensor_tensor(chosen[:, :, :], chosen[:, :, :], score[:, :, :], ALU.mult
                                            ).then_inc(step, 1)
                    dve.wait_ge(step, n + 2)
                    nc.vector.tensor_reduce(total[:, :], chosen[:, :, :], AX, ALU.add).then_inc(step, 1)
                    dve.wait_ge(step, n + 3)
                    nc.vector.reciprocal(total[:, :], total[:, :]).then_inc(step, 1)
                    dve.wait_ge(step, n + 4)
                    nc.vector.tensor_tensor(weight[:, NT:ALL * NT].rearrange("p (e t) -> p t e", t=NT),
                                            chosen[:, :, :], total[:, :].unsqueeze(2).broadcast_to([P, NT, E]),
                                            ALU.mult).then_inc(step, 1)

                nc.vector.memset(weight[:, 0:NT], 1.0)
                for b in range(B):
                    x2_stats(dve, b)
                    if b == 1:
                        dve.wait_ge(gw_hi, 1)
                        nc.vector.tensor_tensor(gw_sp[:, 1, :, :], gw[:, :, :], gw_sp[:, 0, :, :].bitcast(F32),
                                                ALU.subtract).then_inc(gw_lo, 1)
                x2_normalise(dve, 0)
                for n in range(SPLITS):
                    split(0, 0, n)
                for b in range(B):
                    if b + 1 < B:
                        x2_normalise(dve, b + 1)
                    split_x2(b)
                pipeline(dve, front, back)
                out_normalise(dve, B - 1)

            @block.tensor
            def _(pe):
                def front(e, par, blk):
                    u = e * B + blk
                    if blk == 0:
                        pe.wait_ge(w_lo, e * SPLITS + SPLITS)
                    for ps, w, free, done in ((gate_ps, gate_w, silu_done, gate_done), (up_ps, up_w, h_done, up_done)):
                        pe.wait_ge(free, u)
                        if ps is up_ps and isinstance(u, int) and u == 0:
                            pe.wait_ge(scored, B)
                        for i in range(IC):
                            for c in range(DC):
                                for n, (ws, xs) in enumerate(PASSES):
                                    mm = nc.tensor.matmul(ps[:, i, :], w(par, ws, c, i),
                                                          x2_t[:, xs, c, blk * T:(blk + 1) * T],
                                                          start=(c == 0 and n == 0), stop=(c == DC - 1 and n == 2))
                        mm.then_inc(done, 1)

                def back(e, par, blk):
                    u = e * B + blk
                    pe.wait_ge(h_lo, u + 1)
                    for tt in range(TT):
                        if not isinstance(u, int) or u >= 1:
                            pe.wait_ge(combined, (u - 1) * TT + tt + 1)
                        for i in range(IC):
                            for n, (hs, ws) in enumerate(PASSES):
                                mm = nc.tensor.matmul(down_ps[:, tt, :], h_sp[:, blk % 2, hs, i, tt * P:(tt + 1) * P],
                                                      down_w(par, ws, i), start=(i == 0 and n == 0),
                                                      stop=(i == IC - 1 and n == 2))
                        mm.then_inc(down_done, 1)

                pe.wait_ge(consts, 4)
                pe.wait_ge(gw_lo, 1)
                for b in range(B):
                    pe.wait_ge(x2_normed, b * TT + TT)
                    for c in range(DC):
                        if b >= 1:
                            pe.wait_ge(x2_lo, (b - 1) * DC + c + 1)
                        for t in range(TT):
                            mm = nc.tensor.transpose(turn_ps[:, c, t * P:(t + 1) * P],
                                                     rows[:, b * TT + t, c * P:(c + 1) * P], ident[:, :])
                        mm.then_inc(turned, 1)
                    if b >= 1:
                        pe.wait_ge(logits_out, b)
                    for c in range(DC):
                        pe.wait_ge(x2_lo, b * DC + c + 1)
                        for n, (ws, xs) in enumerate(PASSES):
                            mm = nc.tensor.matmul(logit_ps, gw_sp[:, ws, c, :], x2_t[:, xs, c, b * T:(b + 1) * T],
                                                  start=(c == 0 and n == 0), stop=(c == DC - 1 and n == 2))
                    mm.then_inc(logits, 1)
                    pe.wait_ge(logits_out, b + 1)
                    if b >= 1:
                        pe.wait_ge(scored, b)
                    for t in range(TT):
                        mm = nc.tensor.transpose(score_ps[:, t * P:(t + 1) * P], logits_t[:, t * P:(t + 1) * P],
                                                 ident[:, :])
                    mm.then_inc(scores_turned, 1)
                pipeline(pe, front, back)


def decoder_block(nc, xT, x, ctxT, ctx_rows, mask, wqkvT, woT, rope, w_experts, gate_wT, expert_bias, out):
    with ExitStack() as ctx:
        def sem(name):
            return ctx.enter_context(nc.semaphore(name))

        rows = ctx.enter_context(nc.sbuf_tensor("rows", [P, NT, D], F32))
        self_attention(nc, sem, rows, xT, x, wqkvT, woT, rope)
        cross_attention(nc, sem, rows, ctxT, ctx_rows, mask)
        experts(nc, sem, rows, w_experts, gate_wT, expert_bias, out)


def by_chunk(w):
    n, k = w.shape
    return w.reshape(n, k // P, P).transpose(2, 1, 0)


def kernel(x, ctx_2048, mask_BxS2_bk0, L0_attn_Wq, L0_attn_Wk, L0_attn_Wv, L0_attn_Wo, L0_ffn_gate_w,
           L0_ffn_expert_bias, L0_ffn_w_gate, L0_ffn_w_up, L0_ffn_w_down, L0_ffn_sw_gate, L0_ffn_sw_up,
           L0_ffn_sw_down):
    import concourse.bacc as bacc
    from concourse.bass_utils import run_bass_kernel_spmd

    x, context = np.asarray(x), np.asarray(ctx_2048)
    tokens = x.reshape(NT * P, D)
    qkv = [by_chunk(np.asarray(w)).reshape(P, DC, HG, GH * HD) for w in (L0_attn_Wq, L0_attn_Wk, L0_attn_Wv)]

    def packed(gate, up, down):
        return np.concatenate([by_chunk(np.asarray(w)).reshape(P, -1) for w in (gate, up, down)], axis=1)

    w_all = [packed(L0_ffn_sw_gate, L0_ffn_sw_up, L0_ffn_sw_down)]
    w_all += [packed(L0_ffn_w_gate[e], L0_ffn_w_up[e], L0_ffn_w_down[e]) for e in range(E)]
    inv_freq = (1.0 / 10000.0 ** (np.arange(HD // 2, dtype=np.float32) / (HD // 2))).astype(np.float32)
    angles = np.arange(T, dtype=np.float32)[:, None] * inv_freq
    cos, sin = (np.tile(np.repeat(f(angles), 2, axis=-1), (1, GH)).astype(np.float32) for f in (np.cos, np.sin))
    sin[:, 0::2] *= -1

    ins = {
        "xT": tokens.T.reshape(DC, P, B, T).transpose(2, 1, 0, 3),
        "x_rows": tokens.reshape(NT, P, D).transpose(1, 0, 2),
        "ctxT": context.reshape(B, M, DC, P).transpose(0, 3, 2, 1),
        "ctx_rows": context,
        "mask": np.asarray(mask_BxS2_bk0).reshape(B, 1, M),
        "wqkvT": np.stack(qkv, axis=3).reshape(P, DC, HG * GW),
        "woT": by_chunk(np.asarray(L0_attn_Wo)).reshape(P, HG * D),
        "rope": np.stack([cos, sin]).reshape(2, TT, P, GH * HD).transpose(0, 2, 1, 3),
        "w_experts": np.stack(w_all),
        "gate_wT": by_chunk(np.asarray(L0_ffn_gate_w)),
        "expert_bias": np.broadcast_to(np.asarray(L0_ffn_expert_bias), (P, E)),
    }
    nc = bacc.Bacc("TRN2", target_bir_lowering=False, num_devices=1)
    ins = {name: np.ascontiguousarray(a) for name, a in ins.items()}
    args = {name: nc.dram_tensor(name, a.shape, mybir.dt.from_np(a.dtype), kind="ExternalInput").ap()
            for name, a in ins.items()}
    out = nc.dram_tensor("out", (B, T, D), F32, kind="ExternalOutput").ap()
    decoder_block(nc, args["xT"], args["x_rows"], args["ctxT"], args["ctx_rows"], args["mask"], args["wqkvT"],
                  args["woT"], args["rope"], args["w_experts"], args["gate_wT"], args["expert_bias"], out)
    return run_bass_kernel_spmd(nc, [ins], core_ids=[0]).results[0]["out"]
```

```python
from contextlib import ExitStack

import numpy as np

import concourse.bass as bass
from concourse import mybir

F32 = mybir.dt.float32
F32R = mybir.dt.float32r
BF16 = mybir.dt.bfloat16
U8 = mybir.dt.uint8
U32 = mybir.dt.uint32
I32 = mybir.dt.int32
ALU = mybir.AluOpType
ACT = mybir.ActivationFunctionType
AX = mybir.AxisListType.X

P = 128
B, T, D = 4, 512, 512
NH, HD = 16, 32
M = 1601
E, I, TOPK = 16, 256, 4
EPS = 1e-5
MASKED = -1e30

TT = T // P
NT = B * TT
DC = D // P
IC = I // P
HG = NH * HD // P
GH = NH // HG
QK = 2 * GH * HD
GW = QK + GH * HD
MQ = 402
MP = 4 * MQ
MC = -(-M // P)
ML = MP - (MC - 1) * P
MR = M - (MC - 1) * P
WE = 2 * DC * I + IC * D
SLOTS = 2 * P
TILES = (NT * P * TOPK + E * (SLOTS - 1)) // SLOTS
PASSES = ((0, 0), (0, 1), (1, 0))


def self_attention(nc, sem, rows, xT, x, wqkvT, woT, rope, gather_x1):
    with ExitStack() as ctx:
        def sb(name, shape, dt=F32):
            return ctx.enter_context(nc.sbuf_tensor(name, shape, dt))

        x_raw = sb("x_raw", [P, DC, T])
        x_sp = sb("x_sp", [P, 2, DC, T], F32R)
        wqkv = sb("wqkv", [P, 2, DC, HG * GW], F32R)
        wo = sb("wo", [P, 2, HG, D], F32R)
        cos_t = sb("cos_t", [P, TT, GW - QK])
        sin_t = sb("sin_t", [P, TT, GW - QK])
        qk_cos = sb("qk_cos", [P, 2, TT, GH * HD])
        qk_sin = sb("qk_sin", [P, 2, TT, GH * HD])
        qk_sp = sb("qk_sp", [P, 2, TT, GH, 3, HD], F32R)
        v = sb("v", [P, 2, TT, GH * HD])
        q_st = sb("q_st", [P, GH, T], F32R)
        k_st = sb("k_st", [P, GH, T], F32R)
        p_t = sb("p_t", [P, GH, TT * (TT + 1) // 2 * P])
        row_max = sb("row_max", [P, TT, GH])
        neg_max = sb("neg_max", [P, TT, GH, 32], F32R)
        o_f = sb("o_f", [P, T])
        o_sp = sb("o_sp", [P, 2, HG, T], F32R)
        ident_f = sb("ident_f", [P, P])
        ident_r = sb("ident_r", [P, P], F32R)
        ident_b = sb("ident_b", [P, P], BF16)
        mask_qk = sb("mask_qk", [P, P], BF16)
        mask_kq = sb("mask_kq", [P, P], BF16)
        ones = sb("ones", [P, HD])

        proj_ps = ctx.enter_context(nc.psum_tensor("proj_ps", [P, 4, 512], F32))
        score_ps = ctx.enter_context(nc.psum_tensor("score_ps", [P, 2, 512], F32))
        o_ps = ctx.enter_context(nc.psum_tensor("o_ps", [P, 512], F32))
        den_ps = ctx.enter_context(nc.psum_tensor("den_ps", [P, 512], F32))

        tables_in, x_in, rows_in = sem("tables_in"), sem("x_in"), sem("rows_in")
        w_in = [sem(f"w_in{slot}") for slot in range(3)]
        const_pool, const_ready = sem("const_pool"), sem("const_ready")
        w_hi, w_lo = sem("w_hi"), sem("w_lo")
        x_hi, x_lo = sem("x_hi"), sem("x_lo")
        projected, roped = sem("projected"), sem("roped")
        v_copied = sem("v_copied")
        q_hi, q_lo, k_hi, k_lo = sem("q_hi"), sem("q_lo"), sem("k_hi"), sem("k_lo")
        turned, q_stacked, k_stacked = sem("turned"), sem("q_stacked"), sem("k_stacked")
        scored, maxed, max_hi, max_lo = sem("scored"), sem("maxed"), sem("max_hi"), sem("max_lo")
        max_turned = sem("max_turned")
        max_stacked_a, max_stacked_v = sem("max_stacked_a"), sem("max_stacked_v")
        scored_t, exped, summed = sem("scored_t"), sem("exped"), sem("summed")
        den_inv, o_scaled, o_hi, o_lo = sem("den_inv"), sem("o_scaled"), sem("o_hi"), sem("o_lo")
        out_proj, res_added = sem("out_proj"), sem("res_added")

        NG = B * HG
        assert HG == TT
        p_at = [sum(TT - j for j in range(kc)) * P for kc in range(TT)]
        W_LOADS = DC + 1
        w_raw = p_t[:, :, :].rearrange("p h n -> p (h n)")

        def weight_load(n):
            slot = n % 3
            if n < DC:
                return slot, w_raw[:, slot * HG * GW:(slot + 1) * HG * GW], wqkv[:, 0, n, :], wqkv[:, 1, n, :]
            assert (slot, n) == (1, DC) and HG * GW + HG * D <= 3 * HG * GW
            return slot, w_raw[:, HG * GW:HG * GW + HG * D], *(wo[:, part, :, :].rearrange("p g n -> p (g n)")
                                                               for part in range(2))

        def split_places(s):
            stack = qk_sp[:, s, :, :, :, :].rearrange("p t h n d -> p (t h) n d")
            src = qk_cos[:, s, :, :].rearrange("p t (h d) -> p (t h) d", d=HD)
            return src, (stack[:, :, 0:2, :], stack[:, :, 0:3:2, :])[s], stack[:, :, 0, :], stack[:, :, 2 - s, :]

        def twice(src):
            return src.unsqueeze(2).broadcast_to([P, TT * GH, 2, HD])

        def groups(body, finish):
            def run(eng):
                for hg in range(HG):
                    body(0, hg, hg == 0, False)
                with eng.Fori(1, B - 1) as b:
                    for hg in range(HG):
                        body(b, hg, False, False)
                for hg in range(HG):
                    body(B - 1, hg, False, hg == HG - 1)
                finish()
            return run

        with nc.Block() as block:

            @block.sync
            def _(sp):
                sp.dma_start(x_raw[:, :, :], xT[0]).then_inc(x_in, 16)
                for n in range(W_LOADS):
                    if n == DC:
                        sp.wait_ge(w_lo, 3)
                    elif n >= 3:
                        sp.wait_ge(w_lo, n - 2)
                    slot, place, _, _ = weight_load(n)
                    sp.dma_start(place, wqkvT[:, n, :] if n < DC else woT).then_inc(w_in[slot], 16)
                    if n == 2:
                        sp.dma_start(cos_t[:, :, :], rope[0]).then_inc(tables_in, 16)
                        sp.dma_start(sin_t[:, :, :], rope[1]).then_inc(tables_in, 16)
                sp.dma_start(rows[:, :, :], x).then_inc(rows_in, 16)
                with sp.Fori(1, B) as b:
                    sp.wait_ge(x_lo, b)
                    sp.dma_start(x_raw[:, :, :], xT[b]).then_inc(x_in, 16)

            @block.gpsimd
            def _(pool):
                nc.gpsimd.memset(ident_f[:, :], 1.0).then_inc(const_pool, 1)
                nc.gpsimd.memset(ident_b[:, :], 1.0).then_inc(const_pool, 1)
                nc.gpsimd.memset(mask_qk[:, :], 0.0).then_inc(const_pool, 1)
                nc.gpsimd.memset(mask_kq[:, :], 0.0).then_inc(const_pool, 1)
                nc.gpsimd.memset(ones[:, :], 1.0).then_inc(const_pool, 1)
                pool.wait_ge(const_pool, 5)
                for m in (ident_f, ident_b):
                    nc.gpsimd.affine_select(out=m[:, :], in_=m[:, :], compare_op=ALU.is_equal, fill=0.0,
                                            base=0, pattern=[[-1, P]], channel_multiplier=1).then_inc(const_pool, 1)
                nc.gpsimd.affine_select(out=mask_qk[:, :], in_=mask_qk[:, :], compare_op=ALU.is_ge, fill=MASKED,
                                        base=0, pattern=[[-1, P]], channel_multiplier=1).then_inc(const_pool, 1)
                nc.gpsimd.affine_select(out=mask_kq[:, :], in_=mask_kq[:, :], compare_op=ALU.is_ge, fill=MASKED,
                                        base=0, pattern=[[1, P]], channel_multiplier=-1).then_inc(const_pool, 1)

                def lo_x(b):
                    pool.wait_ge(x_hi, b + 1)
                    nc.gpsimd.tensor_tensor(x_sp[:, 1, :, :], x_raw[:, :, :], x_sp[:, 0, :, :].bitcast(F32),
                                            ALU.subtract).then_inc(x_lo, 1)

                def lo_q(g):
                    pool.wait_ge(q_hi, g + 1)
                    src, _, hi, lo = split_places(0)
                    nc.gpsimd.tensor_tensor(lo, src, hi.bitcast(F32), ALU.subtract).then_inc(q_lo, 1)

                def lo_out(g, hg):
                    pool.wait_ge(o_hi, g + 1)
                    nc.gpsimd.tensor_tensor(o_sp[:, 1, hg, :], o_f[:, :], o_sp[:, 0, hg, :].bitcast(F32),
                                            ALU.subtract).then_inc(o_lo, 1)

                def group(b, hg, first, last):
                    g = b * HG + hg
                    if not first:
                        lo_out(g - 1, (hg - 1) % HG)
                    if not last:
                        lo_q(g + 1)
                    if hg == HG - 2 and not (isinstance(b, int) and b == B - 1):
                        lo_x(b + 1)

                lo_x(0)
                lo_q(0)
                groups(group, lambda: lo_out(NG - 1, HG - 1))(pool)

            @block.scalar
            def _(act):
                def split_x(b):
                    act.wait_ge(x_in, b * 16 + 16)
                    act.wait_ge(projected, b * (HG * TT))
                    nc.scalar.activation(x_sp[:, 0, :, :], x_raw[:, :, :], ACT.Copy).then_inc(x_hi, 1)

                def keep_v(g, par):
                    act.wait_ge(projected, g * TT + TT)
                    if not isinstance(g, int) or g >= 2:
                        act.wait_ge(summed, g - 1)
                    nc.scalar.activation(v[:, par, :, :], proj_ps[:, :, QK:GW], ACT.Copy).then_inc(v_copied, 1)

                def hi_q(g):
                    act.wait_ge(roped, g * 6 + 3)
                    act.wait_ge(turned, g * 2 * GH)
                    src, two_hi, _, _ = split_places(0)
                    nc.scalar.activation(two_hi, twice(src), ACT.Copy).then_inc(q_hi, 1)

                def hi_out(g, hg):
                    act.wait_ge(o_scaled, g + 1)
                    if hg == 0:
                        act.wait_ge(out_proj, g)
                    nc.scalar.activation(o_sp[:, 0, hg, :], o_f[:, :], ACT.Copy).then_inc(o_hi, 1)

                def group(b, hg, first, last):
                    g = b * HG + hg
                    act.wait_ge(scored_t, g * GH * TT)
                    for h in range(GH):
                        act.wait_ge(turned, g * 2 * GH + 2 * h + 1)
                        nc.scalar.activation(q_st[0:3 * HD, h, :], proj_ps[0:3 * HD, 2 * h % 4, :],
                                             ACT.Copy).then_inc(q_stacked, 1)
                    if not first:
                        hi_out(g - 1, (hg - 1) % HG)
                    act.wait_ge(max_turned, g + 1)
                    for h in range(0, GH, 2):
                        nc.scalar.activation(q_st[3 * HD:P, h, :], den_ps[32 * h:32 * h + 32, :],
                                             ACT.Copy).then_inc(max_stacked_a, 1)
                    act.wait_ge(summed, g)
                    for kc in range(TT):
                        w = T - kc * P
                        for h in range(GH):
                            n = kc * GH + h
                            act.wait_ge(scored_t, g * GH * TT + n + 1)
                            nc.scalar.activation(p_t[:, h, p_at[kc]:p_at[kc] + w],
                                                 score_ps[:, n % 2, kc * P:T], ACT.Exp,
                                                 scale=float(HD) ** -0.5).then_inc(exped, 1)
                            if n == 1 and not last:
                                keep_v(g + 1, (hg + 1) % 2)
                            if n == 2 * GH + 1 and not last:
                                hi_q(g + 1)
                    if hg == HG - 2 and not (isinstance(b, int) and b == B - 1):
                        split_x(b + 1)

                split_x(0)
                for n in range(W_LOADS):
                    slot, place, hi, _ = weight_load(n)
                    act.wait_ge(w_in[slot], 16 * (n // 3 + 1))
                    nc.scalar.activation(hi, place, ACT.Copy).then_inc(w_hi, 1)
                keep_v(0, 0)
                hi_q(0)
                act.wait_ge(w_lo, W_LOADS)
                groups(group, lambda: hi_out(NG - 1, HG - 1))(act)

            @block.vector
            def _(dve):
                dve.wait_ge(const_pool, 9)
                nc.vector.tensor_copy(ident_r[:, :], ident_f[:, :]).then_inc(const_ready, 1)
                nc.vector.memset(neg_max[:, :, :, :].bitcast(F32), 0.0).then_inc(const_ready, 1)
                nc.vector.memset(k_st[3 * HD:P, :, :].bitcast(F32), 1.0).then_inc(const_ready, 1)
                for n in range(W_LOADS):
                    dve.wait_ge(w_hi, n + 1)
                    _, place, hi, lo = weight_load(n)
                    nc.vector.tensor_tensor(lo, place, hi.bitcast(F32), ALU.subtract).then_inc(w_lo, 1)

                def rotate(g):
                    dve.wait_ge(projected, g * TT + TT)
                    dve.wait_ge(v_copied, g + 1)
                    dve.wait_ge(q_lo, g)
                    for s in range(2):
                        part = slice(s * QK // 2, (s + 1) * QK // 2)
                        nc.vector.tensor_tensor(qk_cos[:, s, :, :], proj_ps[:, :, part], cos_t[:, :, :],
                                                ALU.mult).then_inc(roped, 1)
                        swapped = proj_ps[:, :, part].rearrange("p t (n two) -> p t n two", two=2)[:, :, :, ::-1]
                        nc.vector.tensor_tensor(qk_sin[:, s, :, :].rearrange("p t (n two) -> p t n two", two=2),
                                                swapped, sin_t[:, :, :].rearrange("p t (n two) -> p t n two", two=2),
                                                ALU.mult).then_inc(roped, 1)
                        dve.wait_ge(roped, g * 6 + 3 * s + 2)
                        nc.vector.tensor_tensor(qk_cos[:, s, :, :], qk_cos[:, s, :, :], qk_sin[:, s, :, :],
                                                ALU.add).then_inc(roped, 1)
                    dve.wait_ge(roped, g * 6 + 6)
                    dve.wait_ge(turned, g * 2 * GH)
                    src, two_hi, hi, lo = split_places(1)
                    nc.vector.tensor_copy(two_hi, twice(src)).then_inc(k_hi, 1)
                    dve.wait_ge(k_hi, g + 1)
                    nc.vector.tensor_tensor(lo, src, hi.bitcast(F32), ALU.subtract).then_inc(k_lo, 1)

                sums_t = qk_sin[:, 0, :, :].rearrange("p t (n j) -> p (t n) j", j=HD)
                inv_t = qk_sin[:, 1, 0, 0:T // HD]

                def invert_sums(g, part):
                    if part == 0:
                        dve.wait_ge(summed, g + 1)
                        nc.vector.transpose(sums_t, den_ps[:, :].rearrange("p (n j) -> p n j", j=HD)
                                            ).then_inc(den_inv, 1)
                    elif part == 1:
                        dve.wait_ge(den_inv, g * 3 + 1)
                        nc.vector.reciprocal(inv_t, sums_t[:, :, 0]).then_inc(den_inv, 1)
                    elif part == 2:
                        dve.wait_ge(o_lo, g)
                        dve.wait_ge(den_inv, g * 3 + 2)
                        nc.vector.transpose(o_f[:, :].rearrange("p (n j) -> p n j", j=HD),
                                            inv_t.unsqueeze(2).broadcast_to([P, T // HD, HD])).then_inc(den_inv, 1)

                def finish_out(g):
                    dve.wait_ge(den_inv, g * 3 + 3)
                    nc.vector.tensor_tensor(o_f[:, :], o_ps[:, :], o_f[:, :], ALU.mult).then_inc(o_scaled, 1)

                def add_residual(b):
                    for tt in range(TT):
                        dve.wait_ge(out_proj, b * TT + tt + 1)
                        row = rows[:, b * TT + tt, :]
                        nc.vector.tensor_tensor(row, (o_ps, den_ps)[tt % 2][:, :], row, ALU.add
                                                ).then_inc(res_added, 1)
                        dve.wait_ge(res_added, b * TT + tt + 1)
                        gather_x1(b * TT + tt)

                def group(b, hg, first, last):
                    g = b * HG + hg
                    dve.wait_ge(scored_t, g * GH * TT)
                    for h in range(GH):
                        dve.wait_ge(turned, g * 2 * GH + 2 * h + 2)
                        nc.vector.tensor_copy(k_st[0:3 * HD, h, :], proj_ps[0:3 * HD, (2 * h + 1) % 4, :]
                                              ).then_inc(k_stacked, 1)
                    for qt in range(TT):
                        for h in range(GH):
                            n = qt * GH + h
                            dve.wait_ge(scored, g * GH * TT + n + 1)
                            if n == 0:
                                dve.wait_ge(max_lo, g)
                            nc.vector.tensor_reduce(row_max[:, qt, h:h + 1], score_ps[:, n % 2, 0:(qt + 1) * P],
                                                    AX, ALU.max).then_inc(maxed, 1)
                            if n % 2 == 1 and n < 2 * GH and not first:
                                if n // 2 < 3:
                                    invert_sums(g - 1, n // 2)
                                elif n // 2 == 3:
                                    finish_out(g - 1)
                    dve.wait_ge(maxed, g * GH * TT + GH * TT)
                    dve.wait_ge(max_turned, g)
                    nc.vector.tensor_scalar(neg_max[:, :, :, 0], row_max[:, :, :], -1.0, None,
                                            ALU.mult).then_inc(max_hi, 1)
                    dve.wait_ge(max_hi, g + 1)
                    nc.vector.scalar_tensor_tensor(neg_max[:, :, :, 1], row_max[:, :, :], -1.0,
                                                   neg_max[:, :, :, 0].bitcast(F32), ALU.mult, ALU.subtract
                                                   ).then_inc(max_lo, 1)
                    if hg == 0 and not first:
                        add_residual(b - 1)
                    dve.wait_ge(max_turned, g + 1)
                    for h in range(1, GH, 2):
                        nc.vector.tensor_copy(q_st[3 * HD:P, h, :], den_ps[32 * h:32 * h + 32, :]
                                              ).then_inc(max_stacked_v, 1)
                    if not last:
                        rotate(g + 1)

                def finish():
                    for part in range(3):
                        invert_sums(NG - 1, part)
                    finish_out(NG - 1)
                    add_residual(B - 1)

                dve.wait_ge(tables_in, 32)
                rotate(0)
                dve.wait_ge(rows_in, 16)
                groups(group, finish)(dve)

            @block.tensor
            def _(pe):
                products = [(tt, c, n) for tt in range(TT) for c in range(DC) for n in range(3)]

                def project(g, hg, start, stop):
                    for tt, c, n in products[start:stop]:
                        xs, ws = PASSES[n]
                        mm = nc.tensor.matmul(proj_ps[:, tt, 0:GW], x_sp[:, xs, c, tt * P:(tt + 1) * P],
                                              wqkv[:, ws, c, hg * GW:(hg + 1) * GW],
                                              start=(c == 0 and n == 0), stop=(c == DC - 1 and n == 2))
                        if c == DC - 1 and n == 2:
                            mm.then_inc(projected, 1)

                def project_out(b):
                    pe.wait_ge(o_lo, b * HG + HG)
                    for tt in range(TT):
                        if tt >= 2:
                            pe.wait_ge(res_added, b * TT + tt - 1)
                        for c in range(HG):
                            for n, (os, ws) in enumerate(PASSES):
                                mm = nc.tensor.matmul((o_ps, den_ps)[tt % 2][:, :], o_sp[:, os, c, tt * P:(tt + 1) * P],
                                                      wo[:, ws, c, :], start=(c == 0 and n == 0),
                                                      stop=(c == HG - 1 and n == 2))
                        mm.then_inc(out_proj, 1)

                def scores(g, qt, half):
                    w = (qt + 1) * P
                    for h in range(2 * half, 2 * half + 2):
                        n = qt * GH + h
                        if qt == 0:
                            pe.wait_ge(q_stacked, g * GH + h + 1)
                            pe.wait_ge(k_stacked, g * GH + h + 1)
                        if n >= 2:
                            pe.wait_ge(maxed, g * GH * TT + n - 1)
                        else:
                            pe.wait_ge(exped, g * GH * TT)
                        wide = max(w, 2 * P)
                        nc.tensor.matmul(score_ps[:, n % 2, 0:wide], q_st[0:3 * HD, h, qt * P:w],
                                         k_st[0:3 * HD, h, 0:wide], start=True, stop=False)
                        nc.tensor.matmul(score_ps[:, n % 2, w - P:w], ident_b[:, :], mask_qk[:, :],
                                         start=False, stop=True).then_inc(scored, 1)

                def scores_t(g, kc, half):
                    q0 = min(kc * P, T - 2 * P)
                    for h in range(2 * half, 2 * half + 2):
                        n = kc * GH + h
                        if kc == 0 and h % 2 == 0:
                            pe.wait_ge(max_stacked_a, g * (GH // 2) + h // 2 + 1)
                        if kc == 0 and h % 2 == 1:
                            pe.wait_ge(max_stacked_v, g * (GH // 2) + h // 2 + 1)
                        if n >= 2:
                            pe.wait_ge(exped, g * GH * TT + n - 1)
                        nc.tensor.matmul(score_ps[:, n % 2, q0:T], k_st[:, h, kc * P:(kc + 1) * P],
                                         q_st[:, h, q0:T], start=True, stop=False)
                        nc.tensor.matmul(score_ps[:, n % 2, kc * P:(kc + 1) * P], ident_b[:, :],
                                         mask_kq[:, :], start=False, stop=True).then_inc(scored_t, 1)

                def values(g, hg, kc):
                    pe.wait_ge(exped, g * GH * TT + (kc + 1) * GH)
                    for h in range(GH):
                        nc.tensor.matmul(o_ps[h * HD:(h + 1) * HD, kc * P:T], v[:, hg % 2, kc, h * HD:(h + 1) * HD],
                                         p_t[:, h, p_at[kc]:p_at[kc] + T - kc * P],
                                         start=(kc == 0), stop=(kc == TT - 1))

                def weight_sums(g, kc):
                    for h in range(GH):
                        mm = nc.tensor.matmul(den_ps[h * HD:(h + 1) * HD, kc * P:T], ones[:, :],
                                              p_t[:, h, p_at[kc]:p_at[kc] + T - kc * P],
                                              start=(kc == 0), stop=(kc == TT - 1))
                    return mm

                def group(b, hg, first, last):
                    g = b * HG + hg
                    pe.wait_ge(q_lo, g + 1)
                    pe.wait_ge(roped, g * 6 + 5)
                    pe.wait_ge(v_copied, g + 1)
                    for n in range(2 * GH):
                        h, s = n // 2, n % 2
                        if n == 1:
                            pe.wait_ge(k_lo, g + 1)
                        if n >= 4:
                            pe.wait_ge(k_stacked if s else q_stacked, g * GH + h - 1)
                        for tt in range(TT):
                            mm = nc.tensor.transpose(proj_ps[0:3 * HD, n % 4, tt * P:(tt + 1) * P].bitcast(F32R),
                                                     qk_sp[:, s, tt, h, :, :].rearrange("p n d -> p (n d)"),
                                                     ident_r[:, :])
                        mm.then_inc(turned, 1)
                    if hg == HG - 1 and not last:
                        pe.wait_ge(x_lo, b + 2)
                    STEP = 5
                    for n in range(2 * TT):
                        scores(g, n // 2, n % 2)
                        if n == 1 and not last:
                            pe.wait_ge(q_stacked, g * GH + GH)
                            pe.wait_ge(k_stacked, g * GH + GH)
                        if n >= 1 and not last:
                            project(g + 1, (hg + 1) % HG, (n - 1) * STEP, n * STEP)
                    if hg == 0 and not first:
                        project_out(b - 1)
                    at = (2 * TT - 1) * STEP
                    pe.wait_ge(max_lo, g + 1)
                    if hg == 0 and not first:
                        pe.wait_ge(res_added, b * TT)
                    pe.wait_ge(o_scaled, g)
                    for qt in range(TT):
                        mm = nc.tensor.transpose(den_ps[:, qt * P:(qt + 1) * P].bitcast(F32R),
                                                 neg_max[:, qt, :, :].rearrange("p h n -> p (h n)"), ident_r[:, :])
                    mm.then_inc(max_turned, 1)
                    if not last:
                        project(g + 1, (hg + 1) % HG, at, at + 7)
                    pe.wait_ge(maxed, g * GH * TT + GH * TT)
                    scores_t(g, 0, 0)
                    if not last:
                        project(g + 1, (hg + 1) % HG, at + 7, len(products))
                    scores_t(g, 0, 1)
                    for kc in range(1, TT):
                        scores_t(g, kc, 0)
                        values(g, hg, kc - 1)
                        scores_t(g, kc, 1)
                        weight_sums(g, kc - 1)
                    values(g, hg, TT - 1)
                    weight_sums(g, TT - 1).then_inc(summed, 1)

                pe.wait_ge(const_ready, 3)
                pe.wait_ge(w_lo, W_LOADS)
                pe.wait_ge(x_lo, 1)
                project(0, 0, 0, len(products))
                groups(group, lambda: project_out(B - 1))(pe)


def layer_norm(nc, sem, ctx, rows, name, by_scalar=False):
    stats = ctx.enter_context(nc.sbuf_tensor(name + "_stats", [P, NT, 6], F32))
    mean_var = ctx.enter_context(nc.sbuf_tensor(name + "_mean_var", [P, NT, 2], F32))
    eps = ctx.enter_context(nc.sbuf_tensor(name + "_eps", [P, 1], F32))
    rstd = ctx.enter_context(nc.sbuf_tensor(name + "_rstd", [P, NT], F32))
    half_v = ctx.enter_context(nc.sbuf_tensor(name + "_half_v", [P, NT], F32))
    eps_set, gathered, aggregated = sem(name + "_eps_set"), sem(name + "_gathered"), sem(name + "_aggregated")
    rooted, inverted, normed = sem(name + "_rooted"), sem(name + "_inverted"), sem(name + "_normed")
    shifted = sem(name + "_shifted") if by_scalar else None

    def gather(t):
        nc.vector.bn_stats(stats[:, t, :], rows[:, t, :]).then_inc(gathered, 1)

    def aggregate(dve, b):
        if b == 0:
            nc.vector.memset(eps[:, :], EPS).then_inc(eps_set, 1)
        for t in range(b * TT, b * TT + TT):
            dve.wait_ge(gathered, t + 1)
            nc.vector.bn_aggr(mean_var[:, t, :], stats[:, t, :]).then_inc(aggregated, 1)

    def root(act, b):
        mine = slice(b * TT, b * TT + TT)
        act.wait_ge(eps_set, 1)
        act.wait_ge(aggregated, b * TT + TT)
        nc.scalar.activation(rstd[:, mine], mean_var[:, mine, 1], ACT.Sqrt, bias=eps[:, 0:1]).then_inc(rooted, 1)

    def normalise(dve, b):
        mine = slice(b * TT, b * TT + TT)
        dve.wait_ge(aggregated, b * TT + TT)
        nc.vector.tensor_scalar(half_v[:, mine], mean_var[:, mine, 1], EPS, -0.5, ALU.add, ALU.mult
                                ).then_inc(inverted, 1)
        dve.wait_ge(rooted, b + 1)
        nc.vector.reciprocal(rstd[:, mine], rstd[:, mine]).then_inc(inverted, 1)
        for n in range(2):
            dve.wait_ge(inverted, b * 5 + 2 + n)
            nc.vector.tensor_tensor(half_v[:, mine], half_v[:, mine], rstd[:, mine], ALU.mult).then_inc(inverted, 1)
        dve.wait_ge(inverted, b * 5 + 4)
        nc.vector.scalar_tensor_tensor(rstd[:, mine], half_v[:, mine], 1.5, rstd[:, mine], ALU.add, ALU.mult
                                       ).then_inc(inverted, 1)
        dve.wait_ge(inverted, b * 5 + 5)
        if by_scalar:
            nc.vector.scalar_tensor_tensor(half_v[:, mine], mean_var[:, mine, 0], -1.0, rstd[:, mine],
                                           ALU.mult, ALU.mult).then_inc(shifted, 1)
            return
        for t in range(b * TT, b * TT + TT):
            nc.vector.tensor_scalar(rows[:, t, :], rows[:, t, :], mean_var[:, t, 0:1], rstd[:, t:t + 1],
                                    ALU.subtract, ALU.mult).then_inc(normed, 1)

    def root_and_scale(act, b):
        root(act, b)
        act.wait_ge(shifted, b + 1)
        for t in range(b * TT, b * TT + TT):
            nc.scalar.activation(rows[:, t, :], rows[:, t, :], ACT.Identity, bias=half_v[:, t:t + 1],
                                 scale=rstd[:, t:t + 1]).then_inc(normed, 1)

    return gather, aggregate, root_and_scale if by_scalar else root, normalise, normed


def cross_attention(nc, sem, rows, x1_norm, ctxT, ctx_rows, mask, gather_x2):
    with ExitStack() as ctx:
        def sb(name, shape, dt=F32):
            return ctx.enter_context(nc.sbuf_tensor(name, shape, dt))

        _, aggregate, root, normalise, normed = x1_norm
        RING = 3
        raw = sb("raw", [P, RING, M])
        ct = sb("ct", [P, 2, DC, MP], F32R)
        cr = sb("cr", [P, 2, MC, D], F32R)
        x1 = sb("x1", [P, TT, D])
        x1_t = sb("x1_t", [P, 2, DC, T], F32R)
        mask_u8 = sb("mask_u8", [1, MP], U8)
        mask_bias = sb("mask_bias", [1, MP], BF16)
        any_kept = sb("any_kept", [1, 1])
        weigh = sb("weigh", [P, MP])
        weigh_t = sb("weigh_t", [P, 2, MC, P], F32R)
        stat = sb("stat", [P, 2, 4])
        kept = sb("kept", [P, 1])
        ident = sb("c_ident", [P, P])
        ones_b = sb("c_ones_b", [1, P], BF16)
        ones_f = sb("c_ones_f", [1, P])

        score_ps = ctx.enter_context(nc.psum_tensor("c_score_ps", [P, 4, 512], F32))
        turn_ps = ctx.enter_context(nc.psum_tensor("c_turn_ps", [P, 2, 512], F32))
        out_ps = ctx.enter_context(nc.psum_tensor("c_out_ps", [P, 2, 512], F32))

        raw_in = [sem(f"c_raw_in{slot}") for slot in range(RING)]
        mask_in = sem("c_mask_in")
        consts, zeroed = sem("c_consts"), sem("c_zeroed")
        raw_hi = sem("c_raw_hi")
        raw_lo_v, raw_lo_p = sem("c_raw_lo_v"), sem("c_raw_lo_p")
        bias_set, any_found, kept_done = sem("c_bias_set"), sem("c_any_found"), sem("c_kept_done")
        x1_kept, x1_turned, x1_hi, x1_lo = sem("c_x1_kept"), sem("c_x1_turned"), sem("c_x1_hi"), sem("c_x1_lo")
        scored, maxed, exped = sem("c_scored"), sem("c_maxed"), sem("c_exped")
        inverted, w_turned, w_hi, w_lo = sem("c_inverted"), sem("c_w_turned"), sem("c_w_hi"), sem("c_w_lo")
        read_out, written = sem("c_read_out"), sem("c_written")

        SCALE = float(D) ** -0.5
        GR = M // D
        row_groups = [(c, min(c + GR, MC - 1)) for c in range(0, MC - 1, GR)] + [(MC - 1, MC)]
        LOADS = DC + len(row_groups)
        POOL_LOADS = (1, 3)
        TG = [(c, min(c + 4, MC)) for c in range(0, MC, 4)]
        NG = len(TG)
        TURNS = {MC - 8: 0, MC - 6: 1, MC - 4: 2, MC - 2: 3}
        assert LOADS % RING == 0 and TT % 2 == 0 and len(TURNS) == DC

        def places(n):
            if n < DC:
                return raw[:, n % RING, 0:M], ct[:, 0, n, 0:M], ct[:, 1, n, 0:M]
            c0, c1 = row_groups[n - DC]
            k = P if c1 < MC else MR
            return (raw[0:k, n % RING, 0:(c1 - c0) * D],
                    *(cr[0:k, part, c0:c1, :].rearrange("p c d -> p (c d)") for part in range(2)))

        def loaded(b, n):
            return b * (16 * LOADS // RING) + 16 * (n // RING + 1)

        def split(b, n):
            n, behind = n % LOADS, n // LOADS
            if n in POOL_LOADS:
                return raw_lo_p, b * len(POOL_LOADS) + behind * len(POOL_LOADS) + POOL_LOADS.index(n) + 1
            mine = [m for m in range(LOADS) if m not in POOL_LOADS]
            return raw_lo_v, b * len(mine) + behind * len(mine) + mine.index(n) + 1

        with nc.Block() as block:

            @block.sync
            def _(sp):
                def load(b, n):
                    dst = places(n)[0]
                    if n < DC:
                        sp.dma_start(dst, ctxT[b, :, n, :]).then_inc(raw_in[n % RING], 16)
                    elif n < LOADS - 1:
                        c0, c1 = row_groups[n - DC]
                        sp.dma_start(dst.rearrange("p (c d) -> p c d", d=D),
                                     ctx_rows[b, c0 * P:c1 * P, :].rearrange("(c p) d -> p c d", p=P)
                                     ).then_inc(raw_in[n % RING], 16)
                    else:
                        sp.dma_start(dst, ctx_rows[b, (MC - 1) * P:M, :]).then_inc(raw_in[n % RING], 16)

                def rest(b):
                    for n in range(RING, LOADS):
                        sp.wait_ge(*split(b, n - RING))
                        load(b, n)

                for n in range(RING):
                    load(0, n)
                sp.wait_ge(consts, 5)
                sp.dma_start(mask_u8[:, 0:M], mask[0]).then_inc(mask_in, 16)
                rest(0)
                with sp.Fori(1, B) as b:
                    sp.wait_ge(bias_set, b)
                    sp.wait_ge(any_found, b)
                    sp.wait_ge(*split(b, -RING))
                    load(b, 0)
                    sp.dma_start(mask_u8[:, 0:M], mask[b]).then_inc(mask_in, 16)
                    for n in range(1, RING):
                        sp.wait_ge(*split(b, n - RING))
                        load(b, n)
                    rest(b)

            @block.gpsimd
            def _(pool):
                nc.gpsimd.memset(ident[:, :], 1.0).then_inc(consts, 1)
                nc.gpsimd.memset(ones_b[:, :], 1.0).then_inc(consts, 1)
                nc.gpsimd.memset(ones_f[:, :], 1.0).then_inc(consts, 1)
                nc.gpsimd.memset(mask_u8[:, :], 0).then_inc(consts, 1)
                pool.wait_ge(consts, 4)
                nc.gpsimd.affine_select(out=ident[:, :], in_=ident[:, :], compare_op=ALU.is_equal, fill=0.0,
                                        base=0, pattern=[[-1, P]], channel_multiplier=1).then_inc(consts, 1)

                def lo_context(b, n):
                    src, hi, lo = places(n)
                    pool.wait_ge(raw_hi, b * LOADS + n + 1)
                    nc.gpsimd.tensor_tensor(lo, src, hi.bitcast(F32), ALU.subtract).then_inc(raw_lo_p, 1)

                for n in POOL_LOADS:
                    lo_context(0, n)
                with pool.Fori(1, B) as b:
                    for n in POOL_LOADS:
                        lo_context(b, n)

            @block.scalar
            def _(act):
                def hi_context(b, n):
                    act.wait_ge(raw_in[n % RING], loaded(b, n))
                    src, hi, _ = places(n)
                    nc.scalar.activation(hi, src, ACT.Copy).then_inc(raw_hi, 1)

                def hi_x1(b, c):
                    act.wait_ge(x1_turned, b * DC + c + 1)
                    nc.scalar.activation(x1_t[:, 0, c, :], turn_ps[:, c % 2, :], ACT.Copy).then_inc(x1_hi, 1)

                def batch(b, last):
                    for qt in range(TT):
                        n = b * TT + qt
                        act.wait_ge(maxed, n * 2 + 2)
                        act.wait_ge(w_turned, n * NG)
                        nc.scalar.activation(weigh[:, :].rearrange("p (f m) -> p f m", f=4), score_ps[:, :, 0:MQ],
                                             ACT.Exp, bias=stat[:, qt % 2, 1:2], scale=SCALE,
                                             accum_out=stat[:, qt % 2, 2:3]).then_inc(exped, 1)
                        if qt == 0:
                            act.wait_ge(read_out, n)
                            for m in range(DC, LOADS):
                                hi_context(b, m)
                        if qt == TT - 1 and not last:
                            for c in range(DC):
                                hi_x1(b + 1, c)
                                if c >= 1:
                                    hi_context(b + 1, c)
                        act.wait_ge(read_out, n)
                        for i, (c0, c1) in enumerate(TG):
                            act.wait_ge(w_turned, n * NG + i + 1)
                            k = P if c1 < MC else ML
                            nc.scalar.activation(weigh_t[0:k, 0, c0:c1, :].rearrange("p c q -> p (c q)"),
                                                 turn_ps[0:k, i % 2, 0:(c1 - c0) * P], ACT.Copy).then_inc(w_hi, 1)
                        if qt == 1 and not last:
                            act.wait_ge(normed, (b + 1) * TT + TT)
                            act.wait_ge(x1_turned, (b + 1) * DC)
                            nc.scalar.activation(x1[:, :, :], rows[:, bass.ds((b + 1) * TT, TT), :], ACT.Copy
                                                 ).then_inc(x1_kept, 1)
                        if qt == TT - 2 and not last:
                            act.wait_ge(scored, b * TT + TT)
                            hi_context(b + 1, 0)

                act.wait_ge(zeroed, 4)
                for b in range(B):
                    root(act, b)
                hi_context(0, 0)
                for c in range(DC):
                    hi_x1(0, c)
                for c in range(1, DC):
                    hi_context(0, c)
                with act.Fori(0, B - 1) as b:
                    batch(b, False)
                batch(B - 1, True)

            @block.vector
            def _(dve):
                def lo_context(b, n):
                    src, hi, lo = places(n)
                    dve.wait_ge(raw_hi, b * LOADS + n + 1)
                    nc.vector.tensor_tensor(lo, src, hi.bitcast(F32), ALU.subtract).then_inc(raw_lo_v, 1)

                def lo_x1(b, c):
                    dve.wait_ge(x1_hi, b * DC + c + 1)
                    nc.vector.tensor_tensor(x1_t[:, 1, c, :], turn_ps[:, c % 2, :], x1_t[:, 0, c, :].bitcast(F32),
                                            ALU.subtract).then_inc(x1_lo, 1)

                def find_any(b):
                    dve.wait_ge(mask_in, b * 16 + 16)
                    nc.vector.tensor_reduce(any_kept[:, :], mask_u8[:, :], AX, ALU.max).then_inc(any_found, 1)

                def set_bias(b):
                    dve.wait_ge(mask_in, b * 16 + 16)
                    dve.wait_ge(scored, b * TT)
                    nc.vector.tensor_scalar(mask_bias[:, :], mask_u8[:, :], 1.0, -MASKED, ALU.subtract,
                                            ALU.mult).then_inc(bias_set, 1)

                def maximum(b, qt):
                    n = b * TT + qt
                    dve.wait_ge(scored, n + 1)
                    if qt == 0:
                        nc.vector.tensor_copy(kept[:, :], score_ps[:, 0, MQ:MQ + 1]).then_inc(kept_done, 1)
                    nc.vector.tensor_reduce(stat[:, qt % 2, 0:1], score_ps[:, :, 0:MQ],
                                            mybir.AxisListType.XY, ALU.max).then_inc(maxed, 1)
                    dve.wait_ge(maxed, n * 2 + 1)
                    nc.vector.tensor_scalar(stat[:, qt % 2, 1:2], stat[:, qt % 2, 0:1], 0.1 * MASKED, -SCALE,
                                            ALU.max, ALU.mult).then_inc(maxed, 1)

                def write(b, qt):
                    n = b * TT + qt
                    dve.wait_ge(inverted, n * 3 + 3)
                    dve.wait_ge(read_out, n + 1)
                    row = rows[:, b * TT + qt, :]
                    nc.vector.scalar_tensor_tensor(row, out_ps[:, qt % 2, :], stat[:, qt % 2, 3:4], row,
                                                   ALU.mult, ALU.add).then_inc(written, 1)
                    dve.wait_ge(written, n + 1)
                    gather_x2(n)

                def batch(b, last):
                    for qt in range(TT):
                        n = b * TT + qt
                        dve.wait_ge(exped, n + 1)
                        nc.vector.tensor_scalar(stat[:, qt % 2, 3:4], stat[:, qt % 2, 2:3], 1e-30, None,
                                                ALU.max).then_inc(inverted, 1)
                        dve.wait_ge(inverted, n * 3 + 1)
                        nc.vector.reciprocal(stat[:, qt % 2, 3:4], stat[:, qt % 2, 3:4]).then_inc(inverted, 1)
                        dve.wait_ge(inverted, n * 3 + 2)
                        dve.wait_ge(kept_done, b + 1)
                        nc.vector.tensor_tensor(stat[:, qt % 2, 3:4], stat[:, qt % 2, 3:4], kept[:, :],
                                                ALU.mult).then_inc(inverted, 1)
                        if qt == 0:
                            for m in range(DC, LOADS):
                                lo_context(b, m)
                        if qt == TT - 1 and not last:
                            for c in range(DC):
                                lo_x1(b + 1, c)
                                if c >= 1 and c not in POOL_LOADS:
                                    lo_context(b + 1, c)
                        if qt == TT - 1:
                            write(b, TT - 2)
                        for i, (c0, c1) in enumerate(TG):
                            dve.wait_ge(w_hi, n * NG + i + 1)
                            k = P if c1 < MC else ML
                            nc.vector.tensor_tensor(weigh_t[0:k, 1, c0:c1, :].rearrange("p c q -> p (c q)"),
                                                    turn_ps[0:k, i % 2, 0:(c1 - c0) * P],
                                                    weigh_t[0:k, 0, c0:c1, :].rearrange("p c q -> p (c q)").bitcast(F32),
                                                    ALU.subtract).then_inc(w_lo, 1)
                        if qt < TT - 1:
                            maximum(b, qt + 1)
                        elif not last:
                            maximum(b + 1, 0)
                        if qt == TT - 2 and not last:
                            set_bias(b + 1)
                            lo_context(b + 1, 0)
                        if qt == TT - 3 and not last:
                            find_any(b + 1)
                        if qt != TT - 2:
                            write(b, qt)

                for b in range(B):
                    aggregate(dve, b)
                for part in range(2):
                    nc.vector.memset(ct[:, part, :, M:MP].bitcast(F32), 0.0).then_inc(zeroed, 1)
                    nc.vector.memset(cr[:, part, MC - 1, :].bitcast(F32), 0.0).then_inc(zeroed, 1)
                normalise(dve, 0)
                dve.wait_ge(zeroed, 4)
                lo_context(0, 0)
                for c in range(DC):
                    lo_x1(0, c)
                find_any(0)
                set_bias(0)
                for c in range(1, DC):
                    if c not in POOL_LOADS:
                        lo_context(0, c)
                for b in range(1, B):
                    normalise(dve, b)
                maximum(0, 0)
                with dve.Fori(0, B - 1) as b:
                    batch(b, False)
                batch(B - 1, True)

            @block.tensor
            def _(pe):
                def turn_x1(b, c, src):
                    if c >= 2:
                        pe.wait_ge(x1_lo, b * DC + c - 1)
                    elif isinstance(b, int):
                        pass
                    else:
                        pe.wait_ge(w_lo, b * (TT * NG) - NG - 1 + c)
                    for t in range(TT):
                        mm = nc.tensor.transpose(turn_ps[:, c % 2, t * P:(t + 1) * P],
                                                 src[:, t, c * P:(c + 1) * P], ident[:, :])
                    mm.then_inc(x1_turned, 1)

                def scores(b, qt):
                    n = b * TT + qt
                    pe.wait_ge(exped, n)
                    if qt == 0:
                        pe.wait_ge(any_found, b + 1)
                        pe.wait_ge(bias_set, b + 1)
                        pe.wait_ge(x1_lo, b * DC + DC)
                        nc.tensor.matmul(score_ps[:, 0, MQ:MQ + 1], ones_f[:, :], any_kept[:, :], start=True,
                                         stop=True)
                    if qt == 1:
                        pe.wait_ge(kept_done, b + 1)
                    for f in range(4):
                        nc.tensor.matmul(score_ps[:, f, 0:MQ], ones_b[:, :], mask_bias[:, f * MQ:(f + 1) * MQ],
                                         start=True, stop=False)
                    for c in range(DC):
                        if qt == 0:
                            pe.wait_ge(*split(b, c))
                        for xs, cs in PASSES:
                            for f in range(4):
                                mm = nc.tensor.matmul(score_ps[:, f, 0:MQ], x1_t[:, xs, c, qt * P:(qt + 1) * P],
                                                      ct[:, cs, c, f * MQ:(f + 1) * MQ], start=False,
                                                      stop=(c == DC - 1 and (xs, cs) == PASSES[-1]))
                    mm.then_inc(scored, 1)

                def batch(b, last):
                    for qt in range(TT):
                        n = b * TT + qt
                        if qt < TT - 1:
                            scores(b, qt + 1)
                        elif not last:
                            scores(b + 1, 0)
                        pe.wait_ge(exped, n + 1)
                        if qt == TT - 1 and not last:
                            pe.wait_ge(x1_lo, (b + 1) * DC + DC)
                        for i, (c0, c1) in enumerate(TG):
                            if i >= 2:
                                pe.wait_ge(w_lo, n * NG + i - 1)
                            for c in range(c0, c1):
                                k = P if c < MC - 1 else ML
                                mm = nc.tensor.transpose(turn_ps[0:k, i % 2, (c - c0) * P:(c - c0 + 1) * P],
                                                         weigh[:, c * P:c * P + k], ident[:, :])
                            mm.then_inc(w_turned, 1)
                        if qt >= 1:
                            pe.wait_ge(written, n - 1 if qt > 1 else b * TT)
                        for c in range(MC):
                            k = P if c < MC - 1 else ML
                            if qt == TT - 2 and not last and c in TURNS:
                                if c == MC - 8:
                                    pe.wait_ge(x1_kept, b + 1)
                                    pe.wait_ge(scored, b * TT + TT)
                                turn_x1(b + 1, TURNS[c], x1)
                            pe.wait_ge(w_lo, n * NG + c // 4 + 1)
                            if qt == 0:
                                pe.wait_ge(*split(b, min(DC + c // GR, LOADS - 1)))
                            for m, (ws, cs) in enumerate(PASSES):
                                mm = nc.tensor.matmul(out_ps[:, qt % 2, :], weigh_t[0:k, ws, c, :],
                                                      cr[0:k, cs, c, :], start=(c == 0 and m == 0),
                                                      stop=(c == MC - 1 and m == 2))
                        mm.then_inc(read_out, 1)

                pe.wait_ge(consts, 5)
                pe.wait_ge(normed, TT)
                for c in range(DC):
                    turn_x1(0, c, rows)
                scores(0, 0)
                with pe.Fori(0, B - 1) as b:
                    batch(b, False)
                batch(B - 1, True)


def route(nc, sem, rows, x2_norm, gate_wT, expert_bias, x2_rows, plan):
    slot_of, weight_of, token_at, expert_at = plan
    _, x2_aggregate, x2_root, x2_normalise, x2_normed = x2_norm
    with ExitStack() as ctx:
        def sb(name, shape, dt=F32):
            return ctx.enter_context(nc.sbuf_tensor(name, shape, dt))

        MARKS = 4
        N_TILES = T * B // SLOTS
        x2_t = sb("r_x2_t", [P, 2, 2, DC, T], F32R)
        gw = sb("gw", [P, DC, P])
        gw_sp = sb("gw_sp", [P, 2, DC, P], F32R)
        bias = sb("bias", [P, E])
        logits_t = sb("logits_t", [P, T])
        score = sb("score", [P, NT, E])
        ranked = sb("ranked", [P, NT, E])
        top = sb("top", [P, NT, 8])
        top_at = sb("top_at", [P, NT, 8], U32)
        top_f = sb("top_f", [P, NT, TOPK])
        hit = sb("hit", [P, TOPK, NT, E])
        chosen = sb("chosen", [P, NT, E])
        chosen_b = sb("chosen_b", [P, NT, E], BF16)
        picked = sb("picked", [P, TOPK, NT, E])
        total = sb("total", [P, NT])
        before = sb("before", [P, NT + 1, E])
        filled = sb("filled", [P, E, N_TILES])
        tiles_of = sb("tiles_of", [P, E])
        first = sb("first", [P, E + 1])
        place = sb("place", [P, NT, E])
        slot_f = sb("slot_f", [P, TOPK, NT])
        low_u = sb("low_u", [P, TOPK, NT], U32)
        high_u = sb("high_u", [P, TOPK, NT], U32)
        low_f = sb("low_f", [P, TOPK, NT])
        high_f = sb("high_f", [P, TOPK, NT])
        ended = sb("ended", [P, TILES, E])
        expert_f = sb("expert_f", [P, TILES])
        row_hot = sb("row_hot", [P, MARKS, TOPK, P], F32R)
        col_one = sb("col_one", [P, MARKS, TOPK, 2 * TILES])
        col_hot = sb("col_hot", [P, MARKS, TOPK, 2 * TILES], F32R)
        ident = sb("r_ident", [P, P])
        earlier = sb("earlier", [P, P], BF16)
        ones_b = sb("r_ones_b", [P, P], BF16)
        count = sb("count", [P, P])
        steps_of = sb("steps_of", [P, N_TILES])
        token_id = sb("token_id", [P, NT])

        turn_ps = ctx.enter_context(nc.psum_tensor("r_turn_ps", [P, DC, 512], F32))
        logit_ps = ctx.enter_context(nc.psum_tensor("r_logit_ps", [P, 512], F32))
        score_ps = ctx.enter_context(nc.psum_tensor("r_score_ps", [P, 512], F32))
        rank_ps = ctx.enter_context(nc.psum_tensor("r_rank_ps", [P, 512], F32))
        token_ps = ctx.enter_context(nc.psum_tensor("r_token_ps", [P, 512], F32))

        gate_in, consts = sem("r_gate_in"), sem("r_consts")
        gw_hi, gw_lo = sem("r_gw_hi"), sem("r_gw_lo")
        turned, x2_hi, x2_lo = sem("r_turned"), sem("r_x2_hi"), sem("r_x2_lo")
        logits, logits_out, scores_turned = sem("r_logits"), sem("r_logits_out"), sem("r_scores_turned")
        scored, step, ranks = sem("r_scored"), sem("r_step"), sem("r_ranks")
        marked, col_set = sem("r_marked"), sem("r_col_set")
        placed, x2_out = sem("r_placed"), sem("r_x2_out")

        N_COUNTED = 1 + 2 * NT + 1 + TOPK + 2
        CONSTS = 9

        with nc.Block() as block:

            @block.sync
            def _(sp):
                sp.wait_ge(consts, CONSTS)
                sp.dma_start(gw[:, :, 0:E], gate_wT).then_inc(gate_in, 16)
                sp.dma_start(bias[:, :], expert_bias).then_inc(gate_in, 16)
                for b in range(B):
                    sp.wait_ge(x2_normed, b * TT + TT)
                    sp.dma_start(x2_rows[b * T:(b + 1) * T, :].rearrange("(t p) d -> p t d", p=P),
                                 rows[:, b * TT:(b + 1) * TT, :]).then_inc(x2_out, 16)
                sp.wait_ge(x2_out, B * 16)

            @block.gpsimd
            def _(pool):
                nc.gpsimd.memset(ident[:, :], 1.0).then_inc(consts, 1)
                nc.gpsimd.memset(earlier[:, :], 1.0).then_inc(consts, 1)
                nc.gpsimd.memset(ones_b[:, :], 1.0).then_inc(consts, 1)
                nc.gpsimd.memset(gw[:, :, :], 0.0).then_inc(consts, 1)
                for table, pattern, up in ((count, [[1, P]], 0), (steps_of, [[SLOTS, N_TILES]], 0),
                                           (token_id, [[P, NT]], 1)):
                    nc.gpsimd.iota(table[:, :], pattern=pattern, base=0, channel_multiplier=up,
                                   allow_small_or_imprecise_dtypes=True).then_inc(consts, 1)
                pool.wait_ge(consts, 7)
                nc.gpsimd.affine_select(out=ident[:, :], in_=ident[:, :], compare_op=ALU.is_equal, fill=0.0,
                                        base=0, pattern=[[-1, P]], channel_multiplier=1).then_inc(consts, 1)
                nc.gpsimd.affine_select(out=earlier[:, :], in_=earlier[:, :], compare_op=ALU.is_ge, fill=0.0,
                                        base=-1, pattern=[[1, P]], channel_multiplier=-1).then_inc(consts, 1)

            @block.scalar
            def _(act):
                for b in range(B):
                    x2_root(act, b)
                act.wait_ge(gate_in, 32)
                nc.scalar.activation(gw_sp[:, 0, :, :], gw[:, :, :], ACT.Copy).then_inc(gw_hi, 1)
                def hi_x2(b):
                    if b >= 2:
                        act.wait_ge(logits, b - 1)
                    for c in range(DC):
                        act.wait_ge(turned, b * DC + c + 1)
                        nc.scalar.activation(x2_t[:, b % 2, 0, c, :], turn_ps[:, c, :], ACT.Copy).then_inc(x2_hi, 1)

                hi_x2(0)
                for b in range(B):
                    if b + 1 < B:
                        hi_x2(b + 1)
                    act.wait_ge(logits, b + 1)
                    if b >= 1:
                        act.wait_ge(scores_turned, b)
                    nc.scalar.activation(logits_t[:, :], logit_ps[:, :], ACT.Copy).then_inc(logits_out, 1)
                    act.wait_ge(scores_turned, b + 1)
                    nc.scalar.activation(score[:, b * TT:(b + 1) * TT, :],
                                         score_ps[:, :].rearrange("p (t e) -> p t e", e=P)[:, :, 0:E],
                                         ACT.Sigmoid).then_inc(scored, 1)
                for t in range(NT):
                    act.wait_ge(marked, t * 2 + 2)
                    if t >= MARKS:
                        act.wait_ge(placed, t - MARKS + 1)
                    nc.scalar.activation(col_hot[:, t % MARKS, :, :], col_one[:, t % MARKS, :, :], ACT.Copy,
                                         scale=token_id[:, t:t + 1]).then_inc(col_set, 1)
                act.wait_ge(placed, NT)
                nc.scalar.activation(token_at[:, :], token_ps[:, 0:2 * TILES], ACT.Copy)

            @block.vector
            def _(dve):
                n_step = [0]

                def stepped(instruction):
                    n_step[0] += 1
                    return instruction.then_inc(step, 1)

                def choose():
                    dve.wait_ge(scored, B)
                    dve.wait_ge(gate_in, 32)
                    stepped(nc.vector.tensor_tensor(ranked[:, :, :], score[:, :, :],
                                                    bias[:, :].unsqueeze(1).broadcast_to([P, NT, E]), ALU.add))
                    dve.wait_ge(step, 1)
                    for t in range(NT):
                        stepped(nc.vector.max(top[:, t, :], ranked[:, t, :]))
                    for t in range(NT):
                        dve.wait_ge(step, 2 + t)
                        stepped(nc.vector.max_index(top_at[:, t, :], top[:, t, :], ranked[:, t, :]))
                    dve.wait_ge(step, n_step[0])
                    stepped(nc.vector.tensor_copy(top_f[:, :, :], top_at[:, :, 0:TOPK]))
                    dve.wait_ge(step, n_step[0])
                    dve.wait_ge(consts, CONSTS)
                    for j in range(TOPK):
                        stepped(nc.vector.tensor_tensor(hit[:, j, :, :],
                                                        count[:, 0:E].unsqueeze(1).broadcast_to([P, NT, E]),
                                                        top_f[:, :, j:j + 1].broadcast_to([P, NT, E]), ALU.is_equal))
                    dve.wait_ge(step, n_step[0])
                    stepped(nc.vector.tensor_reduce(chosen[:, :, :], hit[:, :, :, :].rearrange("p j t e -> p t e j"),
                                                    AX, ALU.add))
                    dve.wait_ge(step, n_step[0])
                    stepped(nc.vector.tensor_copy(chosen_b[:, :, :], chosen[:, :, :]))
                    assert n_step[0] == N_COUNTED

                def weigh():
                    for j in range(TOPK):
                        stepped(nc.vector.tensor_tensor(picked[:, j, :, :], hit[:, j, :, :], score[:, :, :], ALU.mult))
                    dve.wait_ge(step, n_step[0])
                    stepped(nc.vector.tensor_reduce(weight_of[:, :, :], picked[:, :, :, :], AX, ALU.add))
                    dve.wait_ge(step, n_step[0])
                    stepped(nc.vector.tensor_reduce(total[:, :], weight_of[:, :, :].rearrange("p j t -> p t j"),
                                                    AX, ALU.add))
                    dve.wait_ge(step, n_step[0])
                    stepped(nc.vector.reciprocal(total[:, :], total[:, :]))
                    dve.wait_ge(step, n_step[0])
                    stepped(nc.vector.tensor_tensor(weight_of[:, :, :], weight_of[:, :, :],
                                                    total[:, :].unsqueeze(1).broadcast_to([P, TOPK, NT]), ALU.mult))

                def lay_out():
                    ranks_of = rank_ps[:, 0:NT * E].rearrange("p (t e) -> p t e", e=E)
                    counts_of = rank_ps[:, NT * E:2 * NT * E].rearrange("p (t e) -> p t e", e=E)
                    dve.wait_ge(ranks, 1)
                    stepped(nc.vector.memset(before[:, 0, :], 0.0))
                    stepped(nc.vector.memset(first[:, 0:1], 0.0))
                    for t in range(NT):
                        dve.wait_ge(step, n_step[0])
                        stepped(nc.vector.tensor_tensor(before[:, t + 1, :], counts_of[:, t, :], before[:, t, :],
                                                        ALU.add))
                    dve.wait_ge(step, n_step[0])
                    stepped(nc.vector.tensor_tensor(filled[:, :, :],
                                                    before[:, NT, :].unsqueeze(2).broadcast_to([P, E, N_TILES]),
                                                    steps_of[:, :].unsqueeze(1).broadcast_to([P, E, N_TILES]), ALU.is_gt))
                    dve.wait_ge(step, n_step[0])
                    stepped(nc.vector.tensor_reduce(tiles_of[:, :], filled[:, :, :], AX, ALU.add))
                    for e in range(E):
                        dve.wait_ge(step, n_step[0])
                        stepped(nc.vector.tensor_tensor(first[:, e + 1:e + 2], first[:, e:e + 1], tiles_of[:, e:e + 1],
                                                        ALU.add))
                    dve.wait_ge(step, n_step[0])
                    stepped(nc.vector.tensor_tensor(ended[:, :, :],
                                                    count[:, 0:TILES].unsqueeze(2).broadcast_to([P, TILES, E]),
                                                    first[:, 1:E + 1].unsqueeze(1).broadcast_to([P, TILES, E]),
                                                    ALU.is_ge))
                    stepped(nc.vector.tensor_tensor(place[:, :, :], ranks_of, before[:, 0:NT, :], ALU.add))
                    dve.wait_ge(step, n_step[0])
                    stepped(nc.vector.tensor_reduce(expert_f[:, :], ended[:, :, :], AX, ALU.add))
                    stepped(nc.vector.scalar_tensor_tensor(place[:, :, :],
                                                           first[:, 0:E].unsqueeze(1).broadcast_to([P, NT, E]),
                                                           float(SLOTS), place[:, :, :], ALU.mult, ALU.add))
                    dve.wait_ge(step, n_step[0])
                    stepped(nc.vector.tensor_scalar(expert_at[:, :], expert_f[0:1, :], float(E - 1), 1.0,
                                                    ALU.min, ALU.add))
                    for j in range(TOPK):
                        stepped(nc.vector.tensor_tensor(picked[:, j, :, :], hit[:, j, :, :], place[:, :, :], ALU.mult))
                    dve.wait_ge(step, n_step[0])
                    stepped(nc.vector.tensor_reduce(slot_f[:, :, :], picked[:, :, :, :], AX, ALU.add))
                    dve.wait_ge(step, n_step[0])
                    stepped(nc.vector.tensor_copy(slot_of[:, :, :], slot_f[:, :, :]))
                    dve.wait_ge(step, n_step[0])
                    stepped(nc.vector.tensor_scalar(low_u[:, :, :], slot_of[:, :, :], P - 1, None, ALU.bitwise_and))
                    stepped(nc.vector.tensor_scalar(high_u[:, :, :], slot_of[:, :, :], P.bit_length() - 1, None,
                                                    ALU.logical_shift_right))
                    dve.wait_ge(step, n_step[0])
                    stepped(nc.vector.tensor_copy(low_f[:, :, :], low_u[:, :, :]))
                    stepped(nc.vector.tensor_copy(high_f[:, :, :], high_u[:, :, :]))
                    dve.wait_ge(step, n_step[0])

                def mark(t):
                    if t >= MARKS:
                        dve.wait_ge(placed, t - MARKS + 1)
                    for hot, n, value in ((row_hot, P, low_f), (col_one, 2 * TILES, high_f)):
                        nc.vector.tensor_tensor(hot[:, t % MARKS, :, :],
                                                count[:, 0:n].unsqueeze(1).broadcast_to([P, TOPK, n]),
                                                value[:, :, t:t + 1].broadcast_to([P, TOPK, n]), ALU.is_equal
                                                ).then_inc(marked, 1)

                for b in range(B):
                    x2_aggregate(dve, b)
                x2_normalise(dve, 0)
                dve.wait_ge(gw_hi, 1)
                nc.vector.tensor_tensor(gw_sp[:, 1, :, :], gw[:, :, :], gw_sp[:, 0, :, :].bitcast(F32),
                                        ALU.subtract).then_inc(gw_lo, 1)
                for b in range(B):
                    if b + 1 < B:
                        x2_normalise(dve, b + 1)
                    for c in range(DC):
                        dve.wait_ge(x2_hi, b * DC + c + 1)
                        nc.vector.tensor_tensor(x2_t[:, b % 2, 1, c, :], turn_ps[:, c, :],
                                                x2_t[:, b % 2, 0, c, :].bitcast(F32), ALU.subtract).then_inc(x2_lo, 1)
                choose()
                lay_out()
                for t in range(NT):
                    mark(t)
                weigh()

            @block.tensor
            def _(pe):
                def turn(b, c):
                    if c == 0:
                        pe.wait_ge(x2_normed, b * TT + TT)
                    if b >= 1:
                        pe.wait_ge(x2_lo, (b - 1) * DC + c + 1)
                    for t in range(TT):
                        mm = nc.tensor.transpose(turn_ps[:, c, t * P:(t + 1) * P],
                                                 rows[:, b * TT + t, c * P:(c + 1) * P], ident[:, :])
                    mm.then_inc(turned, 1)

                def logit(b, c):
                    if b >= 1 and c == 0:
                        pe.wait_ge(logits_out, b)
                    pe.wait_ge(x2_lo, b * DC + c + 1)
                    for n, (ws, xs) in enumerate(PASSES):
                        mm = nc.tensor.matmul(logit_ps[:, :], gw_sp[:, ws, c, :], x2_t[:, b % 2, xs, c, :],
                                              start=(c == 0 and n == 0), stop=(c == DC - 1 and n == 2))
                    if c == DC - 1:
                        mm.then_inc(logits, 1)

                def turn_scores(b):
                    pe.wait_ge(logits_out, b + 1)
                    if b >= 1:
                        pe.wait_ge(scored, b)
                    for t in range(TT):
                        mm = nc.tensor.transpose(score_ps[:, t * P:(t + 1) * P], logits_t[:, t * P:(t + 1) * P],
                                                 ident[:, :])
                    mm.then_inc(scores_turned, 1)

                def rank():
                    pe.wait_ge(step, N_COUNTED)
                    nc.tensor.matmul(rank_ps[:, 0:NT * E], earlier[:, :], chosen_b[:, :, :].rearrange("p t e -> p (t e)"),
                                     start=True, stop=True)
                    nc.tensor.matmul(rank_ps[:, NT * E:2 * NT * E], ones_b[:, :],
                                     chosen_b[:, :, :].rearrange("p t e -> p (t e)"), start=True, stop=True
                                     ).then_inc(ranks, 1)

                def mark(t):
                    pe.wait_ge(marked, t * 2 + 1)
                    pe.wait_ge(col_set, t + 1)
                    for j in range(TOPK):
                        mm = nc.tensor.matmul(token_ps[:, 0:2 * TILES], row_hot[:, t % MARKS, j, :], col_hot[:, t % MARKS, j, :],
                                              start=(t == 0 and j == 0), stop=(t == NT - 1 and j == TOPK - 1))
                    mm.then_inc(placed, 1)

                pe.wait_ge(consts, CONSTS)
                for c in range(DC):
                    turn(0, c)
                pe.wait_ge(gw_lo, 1)
                for b in range(B):
                    for c in range(DC):
                        logit(b, c)
                        if b + 1 < B:
                            turn(b + 1, c)
                    turn_scores(b)
                rank()
                for t in range(NT):
                    mark(t)


def routed_experts(nc, sem, w_experts, x2_rows, y_rows, plan):
    _, _, token_at, expert_at = plan
    with ExitStack() as ctx:
        def sb(name, shape, dt=F32):
            return ctx.enter_context(nc.sbuf_tensor(name, shape, dt))

        HALVES = SLOTS // P
        GATE, UP, DOWN = range(3)
        PART = WE // 3
        assert PART == DC * I == IC * D
        w_raw = sb("e_w_raw", [P, 2, 3, PART])
        w_sp = sb("e_w_sp", [P, 2, 3, 2, PART], F32R)
        index = sb("e_index", [P, 2, HALVES], U32)
        x_g = sb("e_x_g", [P, 2, HALVES, D])
        x_t = sb("e_x_t", [P, 2, 2, DC, SLOTS], F32R)
        gated = sb("e_gated", [P, 2, IC, SLOTS])
        h_f = sb("e_h_f", [P, 2, IC, SLOTS])
        h_sp = sb("e_h_sp", [P, 2, 2, IC, SLOTS], F32R)
        y = sb("e_y", [P, 2, HALVES, D])
        ident = sb("e_ident", [P, P])
        turn_ps = ctx.enter_context(nc.psum_tensor("e_turn_ps", [P, 2, DC // 2, SLOTS], F32))
        gate_ps = ctx.enter_context(nc.psum_tensor("e_gate_ps", [P, 2, IC, SLOTS], F32))
        up_ps = ctx.enter_context(nc.psum_tensor("e_up_ps", [P, 2, IC, SLOTS], F32))
        down_ps = ctx.enter_context(nc.psum_tensor("e_down_ps", [P, HALVES, D], F32))

        consts = sem("e_consts")
        w_in = [[sem(f"e_w_in{part}{par}") for par in range(2)] for part in range(3)]
        x_in = [[sem(f"e_x_in{half}{par}") for par in range(2)] for half in range(HALVES)]
        w_hi = [sem(f"e_w_hi{part}") for part in range(3)]
        w_lo = [sem(f"e_w_lo{part}") for part in range(3)]
        indexed, x_turned, x_hi, x_lo = sem("e_indexed"), sem("e_x_turned"), sem("e_x_hi"), sem("e_x_lo")
        gate_done, up_done, down_done = sem("e_gate_done"), sem("e_up_done"), sem("e_down_done")
        silu_done, h_done, h_hi, h_lo = sem("e_silu_done"), sem("e_h_done"), sem("e_h_hi"), sem("e_h_lo")
        y_first, y_second = sem("e_y_first"), sem("e_y_second")
        y_stored = [sem(f"e_y_stored{par}") for par in range(2)]

        AHEAD = 3

        def steps(step, eng):
            for n in range(-AHEAD, 0):
                step(n, n % 2)
            pairs = (TILES - AHEAD) // 2
            with eng.Fori(0, pairs) as pair:
                step(pair * 2, 0)
                step(pair * 2 + 1, 1)
            for n in range(2 * pairs, TILES):
                step(n, n % 2)

        def exists(m):
            return not isinstance(m, int) or 0 <= m < TILES

        def past(m, k):
            return not isinstance(m, int) or m >= k

        def times(m, par):
            return m - par + 2

        with nc.Block() as block:

            @block.sync
            def _(sp):
                def load(m, par, part, expert):
                    if past(m, 2):
                        sp.wait_ge(w_lo[part], m - 1)
                        sp.wait_ge(consts, 2)
                    sp.dma_start(w_raw[:, par, part, :],
                                 w_experts[bass.ds(expert, 1), :, part * PART:(part + 1) * PART]
                                 .rearrange("o p n -> p (o n)")).then_inc(w_in[part][par], 16)

                def which(m):
                    return sp.value_load(expert_at[0:1, bass.ds(m, 1)] if not isinstance(m, int)
                                         else expert_at[0:1, m:m + 1], min_val=1, max_val=E)

                def step(n, par):
                    if exists(n + 3):
                        expert = which(n + 3)
                        load(n + 3, 1 - par, GATE, expert)
                        load(n + 3, 1 - par, UP, expert)
                    if exists(n + 2):
                        load(n + 2, par, DOWN, which(n + 2))
                    if exists(n):
                        sp.wait_ge(y_first, n + 1)
                        sp.wait_ge(y_second, n + 1)
                        sp.wait_ge(consts, 2)
                        dst = y_rows[bass.ds(n * SLOTS, SLOTS), :]
                        sp.dma_start(dst.rearrange("(h p) d -> p h d", p=P), y[:, par, :, :]
                                     ).then_inc(y_stored[par], 16)

                sp.wait_ge(consts, 2)
                steps(step, sp)
                for par in range(2):
                    sp.wait_ge(y_stored[par], 16 * ((TILES + 1 - par) // 2))

            @block.gpsimd
            def _(pool):
                nc.gpsimd.memset(ident[:, :], 1.0).then_inc(consts, 1)
                pool.wait_ge(consts, 1)
                nc.gpsimd.affine_select(out=ident[:, :], in_=ident[:, :], compare_op=ALU.is_equal, fill=0.0,
                                        base=0, pattern=[[-1, P]], channel_multiplier=1).then_inc(consts, 1)

                def step(n, par):
                    m, par = n + 3, 1 - par
                    if exists(m):
                        ready = m + 1 if isinstance(m, int) else pool.to_reg(m + 1)
                        pool.wait_ge(consts, 2)
                        pool.wait_ge(indexed, ready)
                        for half in range(HALVES):
                            nc.gpsimd.indirect_dma_start(
                                x_g[:, par, half, :], None, x2_rows,
                                bass.IndirectOffsetOnAxis(ap=index[:, par, half:half + 1], axis=0)
                            ).then_inc(x_in[half][par], 16)

                steps(step, pool)

            @block.scalar
            def _(act):
                def hi_w(m, par, part):
                    act.wait_ge(w_in[part][par], times(m, par) * 8)
                    if past(m, 2):
                        act.wait_ge(down_done if part == DOWN else up_done, m - 1 if part != DOWN else (m - 1) * HALVES)
                    nc.scalar.activation(w_sp[:, par, part, 0, :], w_raw[:, par, part, :], ACT.Copy
                                         ).then_inc(w_hi[part], 1)

                def step(n, par):
                    if exists(n + 2):
                        hi_w(n + 2, par, GATE)
                        hi_w(n + 2, par, UP)
                    if exists(n + 1):
                        m = n + 1
                        act.wait_ge(gate_done, m + 1)
                        if past(m, 2):
                            act.wait_ge(h_done, m - 1)
                        nc.scalar.activation(gated[:, 1 - par, :, :], gate_ps[:, 1 - par, :, :], ACT.Silu
                                             ).then_inc(silu_done, 1)
                    if exists(n + 2):
                        m = n + 2
                        for i in range(2):
                            act.wait_ge(x_turned, m * 2 + i + 1)
                            if past(m, 2):
                                act.wait_ge(up_done, m - 1)
                            nc.scalar.activation(x_t[:, par, 0, i * DC // 2:(i + 1) * DC // 2, :], turn_ps[:, i, :, :],
                                                 ACT.Copy).then_inc(x_hi, 1)
                    if exists(n + 1):
                        m = n + 1
                        hi_w(m, 1 - par, DOWN)
                        act.wait_ge(h_done, m + 1)
                        if past(m, 2):
                            act.wait_ge(down_done, (m - 1) * HALVES)
                        nc.scalar.activation(h_sp[:, 1 - par, 0, :, :], h_f[:, 1 - par, :, :], ACT.Copy
                                             ).then_inc(h_hi, 1)
                    if exists(n):
                        act.wait_ge(down_done, n * HALVES + 1)
                        if past(n, 2):
                            act.wait_ge(y_stored[par], times(n, par) * 8 - 16)
                        nc.scalar.activation(y[:, par, 0, :], down_ps[:, 0, :], ACT.Copy).then_inc(y_first, 1)

                steps(step, act)

            @block.vector
            def _(dve):
                def lo_w(m, par, part):
                    dve.wait_ge(w_hi[part], m + 1)
                    nc.vector.tensor_tensor(w_sp[:, par, part, 1, :], w_raw[:, par, part, :],
                                            w_sp[:, par, part, 0, :].bitcast(F32), ALU.subtract
                                            ).then_inc(w_lo[part], 1)

                def step(n, par):
                    if exists(n + 3):
                        m = n + 3
                        if past(m, 2):
                            for half in range(HALVES):
                                dve.wait_ge(x_in[half][1 - par], times(m, 1 - par) * 8 - 16)
                            dve.wait_ge(x_turned, (m - 1) * 2)
                        nc.vector.tensor_scalar(index[:, 1 - par, :], token_at[:, bass.ds(m * HALVES, HALVES)],
                                                1.0, None, ALU.mult).then_inc(indexed, 1)
                    if exists(n + 2):
                        lo_w(n + 2, par, GATE)
                        lo_w(n + 2, par, UP)
                        for i in range(2):
                            dve.wait_ge(x_hi, (n + 2) * 2 + i + 1)
                            some = slice(i * DC // 2, (i + 1) * DC // 2)
                            nc.vector.tensor_tensor(x_t[:, par, 1, some, :], turn_ps[:, i, :, :],
                                                    x_t[:, par, 0, some, :].bitcast(F32), ALU.subtract
                                                    ).then_inc(x_lo, 1)
                    if exists(n + 1):
                        m = n + 1
                        lo_w(m, 1 - par, DOWN)
                        dve.wait_ge(silu_done, m + 1)
                        dve.wait_ge(up_done, m + 1)
                        if past(m, 2):
                            dve.wait_ge(h_lo, m - 1)
                        nc.vector.tensor_tensor(h_f[:, 1 - par, :, :], up_ps[:, 1 - par, :, :], gated[:, 1 - par, :, :],
                                                ALU.mult).then_inc(h_done, 1)
                        dve.wait_ge(h_hi, m + 1)
                        nc.vector.tensor_tensor(h_sp[:, 1 - par, 1, :, :], h_f[:, 1 - par, :, :],
                                                h_sp[:, 1 - par, 0, :, :].bitcast(F32), ALU.subtract
                                                ).then_inc(h_lo, 1)
                    if exists(n):
                        dve.wait_ge(down_done, n * HALVES + 2)
                        if past(n, 2):
                            dve.wait_ge(y_stored[par], times(n, par) * 8 - 16)
                        nc.vector.tensor_scalar(y[:, par, 1, :], down_ps[:, 1, :], 1.0, None, ALU.mult
                                                ).then_inc(y_second, 1)

                steps(step, dve)

            @block.tensor
            def _(pe):
                def front(m, par, part):
                    ps, free, done = ((gate_ps, silu_done, gate_done), (up_ps, h_done, up_done))[part]
                    pe.wait_ge(x_lo, m * 2 + 2)
                    pe.wait_ge(w_lo[part], m + 1)
                    if past(m, 2):
                        pe.wait_ge(free, m - 1)
                    for i in range(IC):
                        for c in range(DC):
                            at = c * I + i * P
                            for n, (ws, xs) in enumerate(PASSES):
                                mm = nc.tensor.matmul(ps[:, par, i, :], w_sp[:, par, part, ws, at:at + P],
                                                      x_t[:, par, xs, c, :], start=(c == 0 and n == 0),
                                                      stop=(c == DC - 1 and n == 2))
                    mm.then_inc(done, 1)

                def turn(m, par):
                    for half in range(HALVES):
                        pe.wait_ge(x_in[half][par], times(m, par) * 8)
                    for c in range(DC):
                        i = c // (DC // 2)
                        if c % (DC // 2) == 0 and past(m, 1):
                            pe.wait_ge(x_lo, (m - 1) * 2 + i + 1)
                        for half in range(HALVES):
                            mm = nc.tensor.transpose(turn_ps[:, i, c % (DC // 2), half * P:(half + 1) * P],
                                                     x_g[:, par, half, c * P:(c + 1) * P], ident[:, :])
                        if c % (DC // 2) == DC // 2 - 1:
                            mm.then_inc(x_turned, 1)

                def back(m, par):
                    pe.wait_ge(h_lo, m + 1)
                    pe.wait_ge(w_lo[DOWN], m + 1)
                    for half, read in ((0, y_first), (1, y_second)):
                        if past(m, 1):
                            pe.wait_ge(read, m)
                        for i in range(IC):
                            for n, (hs, ws) in enumerate(PASSES):
                                mm = nc.tensor.matmul(down_ps[:, half, :],
                                                      h_sp[:, par, hs, i, half * P:(half + 1) * P],
                                                      w_sp[:, par, DOWN, ws, i * D:(i + 1) * D],
                                                      start=(i == 0 and n == 0), stop=(i == IC - 1 and n == 2))
                        mm.then_inc(down_done, 1)

                def step(n, par):
                    if exists(n + 1):
                        front(n + 1, 1 - par, GATE)
                    if exists(n + 2):
                        turn(n + 2, par)
                    if exists(n + 1):
                        front(n + 1, 1 - par, UP)
                    if exists(n):
                        back(n, par)

                pe.wait_ge(consts, 2)
                steps(step, pe)


def combine(nc, sem, rows, w_shared, y_rows, plan, out):
    slot_of, weight_of, _, _ = plan
    with ExitStack() as ctx:
        def sb(name, shape, dt=F32):
            return ctx.enter_context(nc.sbuf_tensor(name, shape, dt))

        gather, aggregate, root, normalise, normed = layer_norm(nc, sem, ctx, rows, "norm3", by_scalar=True)
        RING = 4
        PART = WE // 3
        assert PART == DC * I == IC * D
        y_g = sb("y_g", [P, RING, TOPK, D])
        x2_t = sb("s_x2_t", [P, 2, DC, NT * P], F32R)
        w_raw = sb("s_w_raw", [P, WE])
        w_sp = sb("s_w_sp", [P, 2, WE], F32R)
        gated = sb("s_gated", [P, IC, T])
        h_f = sb("s_h_f", [P, IC, T])
        h_sp = sb("s_h_sp", [P, 2, 2, IC, T], F32R)
        ident = sb("s_ident", [P, P])
        gate_ps = ctx.enter_context(nc.psum_tensor("s_gate_ps", [P, IC, T], F32))
        up_ps = ctx.enter_context(nc.psum_tensor("s_up_ps", [P, IC, T], F32))
        down_ps = ctx.enter_context(nc.psum_tensor("s_down_ps", [P, 2, D], F32))
        turn_ps = ctx.enter_context(nc.psum_tensor("s_turn_ps", [P, 2, 512], F32))

        consts = sem("s_consts")
        turned, x2_hi, x2_lo = sem("s_turned"), sem("s_x2_hi"), sem("s_x2_lo")
        w_in, w_hi, w_lo = sem("s_w_in"), sem("s_w_hi"), sem("s_w_lo")
        gate_done, up_done, down_done = sem("s_gate_done"), sem("s_up_done"), sem("s_down_done")
        silu_done, h_done, h_hi, h_lo = sem("s_silu_done"), sem("s_h_done"), sem("s_h_hi"), sem("s_h_lo")
        shared_added = sem("s_shared_added")
        y_in = [sem(f"y_in{slot}") for slot in range(RING)]
        added, stored = sem("y_added"), sem("f_stored")

        with nc.Block() as block:

            @block.sync
            def _(sp):
                sp.dma_start(w_raw[:, :], w_shared).then_inc(w_in, 16)
                for b in range(B):
                    sp.wait_ge(normed, (b + 1) * TT)
                    sp.dma_start(out[b].rearrange("(t p) d -> p t d", p=P), rows[:, b * TT:(b + 1) * TT, :]
                                 ).then_inc(stored, 16)
                sp.wait_ge(stored, B * 16)

            @block.gpsimd
            def _(pool):
                nc.gpsimd.memset(ident[:, :], 1.0).then_inc(consts, 1)
                pool.wait_ge(consts, 1)
                nc.gpsimd.affine_select(out=ident[:, :], in_=ident[:, :], compare_op=ALU.is_equal, fill=0.0,
                                        base=0, pattern=[[-1, P]], channel_multiplier=1).then_inc(consts, 1)
                for t in range(NT):
                    for j in range(TOPK):
                        if t >= RING:
                            u = t - RING
                            pool.wait_ge(added, (u - u % 2) * TOPK + 2 * j + u % 2 + 1)
                        nc.gpsimd.indirect_dma_start(
                            y_g[:, t % RING, j, :], None, y_rows,
                            bass.IndirectOffsetOnAxis(ap=slot_of[:, j, t:t + 1], axis=0)
                        ).then_inc(y_in[t % RING], 16)

            @block.scalar
            def _(act):
                def hi_x2(b):
                    for c in range(DC):
                        act.wait_ge(turned, b * DC + c + 1)
                        nc.scalar.activation(x2_t[:, 0, c, b * T:(b + 1) * T], turn_ps[:, c % 2, :], ACT.Copy
                                             ).then_inc(x2_hi, 1)

                def front(b):
                    act.wait_ge(gate_done, b + 1)
                    if b >= 1:
                        act.wait_ge(h_done, b)
                    nc.scalar.activation(gated[:, :, :], gate_ps[:, :, :], ACT.Silu).then_inc(silu_done, 1)
                    act.wait_ge(h_done, b + 1)
                    if b >= 2:
                        act.wait_ge(down_done, (b - 1) * TT)
                    nc.scalar.activation(h_sp[:, b % 2, 0, :, :], h_f[:, :, :], ACT.Copy).then_inc(h_hi, 1)

                hi_x2(0)
                act.wait_ge(w_in, 16)
                for part in range(3):
                    mine = slice(part * PART, (part + 1) * PART)
                    nc.scalar.activation(w_sp[:, 0, mine], w_raw[:, mine], ACT.Copy).then_inc(w_hi, 1)
                hi_x2(1)
                front(0)
                front(1)
                hi_x2(2)
                root(act, 0)
                front(2)
                hi_x2(3)
                front(3)
                root(act, 1)
                root(act, 2)
                root(act, 3)

            @block.vector
            def _(dve):
                def lo_x2(b, c):
                    dve.wait_ge(x2_hi, b * DC + c + 1)
                    nc.vector.tensor_tensor(x2_t[:, 1, c, b * T:(b + 1) * T], turn_ps[:, c % 2, :],
                                            x2_t[:, 0, c, b * T:(b + 1) * T].bitcast(F32), ALU.subtract
                                            ).then_inc(x2_lo, 1)

                def front(b):
                    dve.wait_ge(silu_done, b + 1)
                    dve.wait_ge(up_done, b + 1)
                    if b >= 1:
                        dve.wait_ge(h_lo, b)
                    nc.vector.tensor_tensor(h_f[:, :, :], up_ps[:, :, :], gated[:, :, :], ALU.mult).then_inc(h_done, 1)
                    dve.wait_ge(h_hi, b + 1)
                    nc.vector.tensor_tensor(h_sp[:, b % 2, 1, :, :], h_f[:, :, :],
                                            h_sp[:, b % 2, 0, :, :].bitcast(F32), ALU.subtract).then_inc(h_lo, 1)

                def add_routed(first, last, behind_shared=False):
                    for pair in range(first, last, 2):
                        for j in range(TOPK):
                            for t in (pair, pair + 1):
                                if j == 0:
                                    dve.wait_ge(y_in[t % RING], 16 * TOPK * (t // RING + 1))
                                if j >= 1:
                                    dve.wait_ge(added, pair * TOPK + 2 * j - 1 + t - pair)
                                elif behind_shared:
                                    dve.wait_ge(shared_added, t + 1)
                                nc.vector.scalar_tensor_tensor(rows[:, t, :], y_g[:, t % RING, j, :],
                                                               weight_of[:, j, t:t + 1], rows[:, t, :],
                                                               ALU.mult, ALU.add).then_inc(added, 1)

                def add_shared(b, so_far, next_x2=None):
                    dve.wait_ge(added, so_far * TOPK)
                    for tt in range(TT):
                        t = b * TT + tt
                        dve.wait_ge(down_done, t + 1)
                        nc.vector.tensor_tensor(rows[:, t, :], down_ps[:, t % 2, :], rows[:, t, :],
                                                ALU.add).then_inc(shared_added, 1)
                        if next_x2 is not None:
                            lo_x2(next_x2, tt)

                def norm(b):
                    dve.wait_ge(added, (b + 1) * TT * TOPK)
                    for t in range(b * TT, (b + 1) * TT):
                        dve.wait_ge(shared_added, t + 1)
                        gather(t)
                    aggregate(dve, b)
                    normalise(dve, b)

                for c in range(DC):
                    lo_x2(0, c)
                for part in range(3):
                    mine = slice(part * PART, (part + 1) * PART)
                    dve.wait_ge(w_hi, part + 1)
                    nc.vector.tensor_tensor(w_sp[:, 1, mine], w_raw[:, mine], w_sp[:, 0, mine].bitcast(F32),
                                            ALU.subtract).then_inc(w_lo, 1)
                for c in range(DC):
                    lo_x2(1, c)
                add_routed(0, 2)
                front(0)
                add_routed(2, 4)
                front(1)
                add_shared(0, 4, next_x2=2)
                norm(0)
                add_routed(4, 6)
                front(2)
                add_shared(1, 6, next_x2=3)
                add_routed(6, 8, behind_shared=True)
                add_routed(8, 10)
                front(3)
                add_shared(2, 10)
                add_shared(3, 10)
                norm(1)
                add_routed(10, 12, behind_shared=True)
                norm(2)
                add_routed(12, 16, behind_shared=True)
                norm(3)

            @block.tensor
            def _(pe):
                def turn(b, c):
                    n = b * DC + c
                    if n >= 2:
                        pe.wait_ge(x2_lo, n - 1)
                    for t in range(TT):
                        mm = nc.tensor.transpose(turn_ps[:, c % 2, t * P:(t + 1) * P],
                                                 rows[:, b * TT + t, c * P:(c + 1) * P], ident[:, :])
                    mm.then_inc(turned, 1)

                def front(b):
                    pe.wait_ge(x2_lo, b * DC + DC)
                    for part, ps, start_at, free, done in ((0, gate_ps, 0, silu_done, gate_done),
                                                           (1, up_ps, PART, h_done, up_done)):
                        if b == 0:
                            pe.wait_ge(w_lo, part + 1)
                        if b == 0 and part == 1:
                            for c in range(DC):
                                turn(1, c)
                        if b >= 1:
                            pe.wait_ge(free, b)
                        for i in range(IC):
                            for c in range(DC):
                                at = start_at + c * I + i * P
                                for n, (ws, xs) in enumerate(PASSES):
                                    mm = nc.tensor.matmul(ps[:, i, :], w_sp[:, ws, at:at + P],
                                                          x2_t[:, xs, c, b * T:(b + 1) * T],
                                                          start=(c == 0 and n == 0), stop=(c == DC - 1 and n == 2))
                        mm.then_inc(done, 1)

                def back(b, next_x2=None):
                    pe.wait_ge(h_lo, b + 1)
                    pe.wait_ge(w_lo, 3)
                    for tt in range(TT):
                        t = b * TT + tt
                        if t >= 2:
                            pe.wait_ge(shared_added, t - 1)
                        for i in range(IC):
                            at = 2 * PART + i * D
                            for n, (hs, ws) in enumerate(PASSES):
                                mm = nc.tensor.matmul(down_ps[:, t % 2, :], h_sp[:, b % 2, hs, i, tt * P:(tt + 1) * P],
                                                      w_sp[:, ws, at:at + D], start=(i == 0 and n == 0),
                                                      stop=(i == IC - 1 and n == 2))
                        mm.then_inc(down_done, 1)
                        if next_x2 is not None:
                            turn(next_x2, tt)

                assert TT == DC
                pe.wait_ge(consts, 2)
                for c in range(DC):
                    turn(0, c)
                front(0)
                front(1)
                back(0, next_x2=2)
                front(2)
                back(1, next_x2=3)
                front(3)
                back(2)
                back(3)


def experts(nc, sem, rows, x2_norm, w_experts, gate_wT, expert_bias, out):
    with ExitStack() as ctx:
        slot_of = ctx.enter_context(nc.sbuf_tensor("slot_of", [P, TOPK, NT], U32))
        weight_of = ctx.enter_context(nc.sbuf_tensor("weight_of", [P, TOPK, NT], F32))
        token_at = ctx.enter_context(nc.sbuf_tensor("token_at", [P, 2 * TILES], F32))
        expert_at = ctx.enter_context(nc.sbuf_tensor("expert_at", [1, TILES], I32))
        plan = slot_of, weight_of, token_at, expert_at
        x2_rows = nc.dram_tensor("x2_rows", (NT * P, D), F32, kind="Internal").ap()
        y_rows = nc.dram_tensor("y_rows", (TILES * SLOTS, D), F32, kind="Internal").ap()
        route(nc, sem, rows, x2_norm, gate_wT, expert_bias, x2_rows, plan)
        routed_experts(nc, sem, w_experts, x2_rows, y_rows, plan)
        combine(nc, sem, rows, w_experts[0], y_rows, plan, out)


def decoder_block(nc, xT, x, ctxT, ctx_rows, mask, wqkvT, woT, rope, w_experts, gate_wT, expert_bias, out):
    with ExitStack() as ctx:
        def sem(name):
            return ctx.enter_context(nc.semaphore(name))

        rows = ctx.enter_context(nc.sbuf_tensor("rows", [P, NT, D], F32))
        x1_norm = layer_norm(nc, sem, ctx, rows, "norm1")
        self_attention(nc, sem, rows, xT, x, wqkvT, woT, rope, x1_norm[0])
        x2_norm = layer_norm(nc, sem, ctx, rows, "norm2")
        cross_attention(nc, sem, rows, x1_norm, ctxT, ctx_rows, mask, x2_norm[0])
        experts(nc, sem, rows, x2_norm, w_experts, gate_wT, expert_bias, out)


def by_chunk(w):
    n, k = w.shape
    return w.reshape(n, k // P, P).transpose(2, 1, 0)


def kernel(x, ctx_2048, mask_BxS2_bk0, L0_attn_Wq, L0_attn_Wk, L0_attn_Wv, L0_attn_Wo, L0_ffn_gate_w,
           L0_ffn_expert_bias, L0_ffn_w_gate, L0_ffn_w_up, L0_ffn_w_down, L0_ffn_sw_gate, L0_ffn_sw_up,
           L0_ffn_sw_down):
    import concourse.bacc as bacc
    from concourse.bass_utils import run_bass_kernel_spmd

    x, context = np.asarray(x), np.asarray(ctx_2048)
    tokens = x.reshape(NT * P, D)
    qkv = [by_chunk(np.asarray(w)).reshape(P, DC, HG, GH * HD) for w in (L0_attn_Wq, L0_attn_Wk, L0_attn_Wv)]

    def packed(gate, up, down):
        return np.concatenate([by_chunk(np.asarray(w)).reshape(P, -1) for w in (gate, up, down)], axis=1)

    w_all = [packed(L0_ffn_sw_gate, L0_ffn_sw_up, L0_ffn_sw_down)]
    w_all += [packed(L0_ffn_w_gate[e], L0_ffn_w_up[e], L0_ffn_w_down[e]) for e in range(E)]
    inv_freq = (1.0 / 10000.0 ** (np.arange(HD // 2, dtype=np.float32) / (HD // 2))).astype(np.float32)
    angles = np.arange(T, dtype=np.float32)[:, None] * inv_freq
    cos, sin = (np.tile(np.repeat(f(angles), 2, axis=-1), (1, GH)).astype(np.float32) for f in (np.cos, np.sin))
    sin[:, 0::2] *= -1

    ins = {
        "xT": tokens.T.reshape(DC, P, B, T).transpose(2, 1, 0, 3),
        "x_rows": tokens.reshape(NT, P, D).transpose(1, 0, 2),
        "ctxT": context.reshape(B, M, DC, P).transpose(0, 3, 2, 1),
        "ctx_rows": context,
        "mask": np.asarray(mask_BxS2_bk0).reshape(B, 1, M),
        "wqkvT": np.stack(qkv, axis=3).reshape(P, DC, HG * GW),
        "woT": by_chunk(np.asarray(L0_attn_Wo)).reshape(P, HG * D),
        "rope": np.stack([cos, sin]).reshape(2, TT, P, GH * HD).transpose(0, 2, 1, 3),
        "w_experts": np.stack(w_all),
        "gate_wT": by_chunk(np.asarray(L0_ffn_gate_w)),
        "expert_bias": np.broadcast_to(np.asarray(L0_ffn_expert_bias), (P, E)),
    }
    nc = bacc.Bacc("TRN2", target_bir_lowering=False, num_devices=1)
    ins = {name: np.ascontiguousarray(a) for name, a in ins.items()}
    args = {name: nc.dram_tensor(name, a.shape, mybir.dt.from_np(a.dtype), kind="ExternalInput").ap()
            for name, a in ins.items()}
    out = nc.dram_tensor("out", (B, T, D), F32, kind="ExternalOutput").ap()
    decoder_block(nc, args["xT"], args["x_rows"], args["ctxT"], args["ctx_rows"], args["mask"], args["wqkvT"],
                  args["woT"], args["rope"], args["w_experts"], args["gate_wT"], args["expert_bias"], out)
    return run_bass_kernel_spmd(nc, [ins], core_ids=[0]).results[0]["out"]
```
